# Optimizing a Trainium2 kernel written in Bass

```python
import numpy as np
import jax
import jax.numpy as jnp

def _softmax(x, axis=-1):
    return jax.nn.softmax(x, axis=axis)

def _gelu(x):
    return jax.nn.gelu(x, approximate=True)

def _silu(x):
    return jax.nn.silu(x)

def _sigmoid(x):
    return jax.nn.sigmoid(x)

def _layernorm(x, axis=-1, eps=1e-05):
    m = jnp.mean(x, axis=axis, keepdims=True)
    v = jnp.var(x, axis=axis, keepdims=True)
    return (x - m) / jnp.sqrt(v + eps)

def _scatter_add(tgt, idx, src, axis=0):
    return tgt.at[idx].add(src)

def _segment_sum(src, seg, n):
    return jax.ops.segment_sum(src, seg, n)
kernel_name = 'mk_recurrent_d2_jaxref_r8_de8493'

def setup_inputs(seed: int=0):
    np.random.seed(seed)
    _w = jnp.asarray

    def _L0_attn_setup():
        import jax, jax.numpy as jnp
        import numpy as np
        DIM_IN, DIM_K, DIM_V, NH = (128, 128, 128, 16)
        DK, DV = (DIM_K // NH, DIM_V // NH)
        key = jax.random.key(seed)
        kx, kq, kk, kv = jax.random.split(key, 4)
        x = jax.random.normal(kx, (4, 256, DIM_IN), dtype=jnp.float32)
        Wq = jax.random.normal(kq, (DIM_K, DIM_IN), dtype=jnp.float32) / np.sqrt(DIM_IN)
        Wk = jax.random.normal(kk, (DK, DIM_IN), dtype=jnp.float32) / np.sqrt(DIM_IN)
        Wv = jax.random.normal(kv, (DV, DIM_IN), dtype=jnp.float32) / np.sqrt(DIM_IN)
        return {'x': x, 'Wq': Wq, 'Wk': Wk, 'Wv': Wv}
    _L0_attn_in = _L0_attn_setup()

    def _L0_ffn_setup():
        import jax, jax.numpy as jnp
        import numpy as np
        D_MODEL = 128
        D_FF = 512
        NUM_M = 2
        E_ROUTER = 8 * NUM_M - 1
        D_FF_R = D_FF // NUM_M
        TOP_K = NUM_M * 2 - 1
        B, T = (2, 256)

        def _expert_stack(x, W1, b1, W2, b2):
            h = jax.nn.gelu(jnp.einsum('btd,edf->ebtf', x, W1) + b1[:, None, None, :], approximate=False)
            return jnp.einsum('ebtf,efd->ebtd', h, W2) + b2[:, None, None, :]
        key = jax.random.key(seed)
        ks = jax.random.split(key, 12)
        s = lambda fan_in: 1.0 / np.sqrt(fan_in)
        x = jax.random.normal(ks[0], (B, T, D_MODEL), dtype=jnp.float32)
        sW1 = jax.random.uniform(ks[1], (1, D_MODEL, D_FF), jnp.float32, -s(D_MODEL), s(D_MODEL))
        sb1 = jax.random.uniform(ks[2], (1, D_FF), jnp.float32, -s(D_MODEL), s(D_MODEL))
        sW2 = jax.random.uniform(ks[3], (1, D_FF, D_MODEL), jnp.float32, -s(D_FF), s(D_FF))
        sb2 = jax.random.uniform(ks[4], (1, D_MODEL), jnp.float32, -s(D_FF), s(D_FF))
        rW1 = jax.random.uniform(ks[5], (E_ROUTER, D_MODEL, D_FF_R), jnp.float32, -s(D_MODEL), s(D_MODEL))
        rb1 = jax.random.uniform(ks[6], (E_ROUTER, D_FF_R), jnp.float32, -s(D_MODEL), s(D_MODEL))
        rW2 = jax.random.uniform(ks[7], (E_ROUTER, D_FF_R, D_MODEL), jnp.float32, -s(D_FF_R), s(D_FF_R))
        rb2 = jax.random.uniform(ks[8], (E_ROUTER, D_MODEL), jnp.float32, -s(D_FF_R), s(D_FF_R))
        gW = jax.random.uniform(ks[9], (D_MODEL, E_ROUTER), jnp.float32, -s(D_MODEL), s(D_MODEL))
        gb = jax.random.uniform(ks[10], (E_ROUTER,), jnp.float32, -s(D_MODEL), s(D_MODEL))
        return {'x': x, 'sW1': sW1, 'sb1': sb1, 'sW2': sW2, 'sb2': sb2, 'rW1': rW1, 'rb1': rb1, 'rW2': rW2, 'rb2': rb2, 'gW': gW, 'gb': gb}
    _L0_ffn_in = _L0_ffn_setup()

    def _L1_attn_setup():
        import math
        import jax, jax.numpy as jnp
        import numpy as np
        D_MODEL = 128
        NUM_HEADS = 16
        D_HEAD = D_MODEL // NUM_HEADS
        K_S = 32
        B, N = (2, 256)

        def _attn(x, Wq, bq, Wk, bk, Wv, bv, Wo, bo):
            b, n, _ = x.shape
            q = (x @ Wq.T + bq).reshape(b, n, NUM_HEADS, D_HEAD).transpose(0, 2, 1, 3)
            k = (x @ Wk.T + bk).reshape(b, n, NUM_HEADS, D_HEAD).transpose(0, 2, 1, 3)
            v = (x @ Wv.T + bv).reshape(b, n, NUM_HEADS, D_HEAD).transpose(0, 2, 1, 3)
            scores = jnp.einsum('bhqd,bhkd->bhqk', q, k) / math.sqrt(D_HEAD)
            causal = jnp.triu(jnp.ones((n, n), dtype=bool), k=1)
            neg_inf = jnp.array(-jnp.inf, dtype=scores.dtype)
            scores = jnp.where(causal, neg_inf, scores)
            vals, idx = jax.lax.top_k(scores, K_S)
            masked = jnp.full_like(scores, -jnp.inf)
            masked = jnp.put_along_axis(masked, idx, vals, axis=-1, inplace=False)
            attn = jax.nn.softmax(masked, axis=-1)
            out = jnp.einsum('bhqk,bhkd->bhqd', attn, v)
            out = out.transpose(0, 2, 1, 3).reshape(b, n, D_MODEL)
            y = out @ Wo.T + bo
            return (y, attn.mean(axis=1))

        def _reference_tuple_inner(x, Wq, bq, Wk, bk, Wv, bv, Wo, bo):
            return _attn(x, Wq, bq, Wk, bk, Wv, bv, Wo, bo)
        key = jax.random.key(seed)
        ks = jax.random.split(key, 9)
        s = 1.0 / math.sqrt(D_MODEL)
        return {'x': jax.random.normal(ks[0], (B, N, D_MODEL), dtype=jnp.float32), 'Wq': jax.random.normal(ks[1], (D_MODEL, D_MODEL), dtype=jnp.float32) * s, 'bq': jnp.zeros((D_MODEL,), dtype=jnp.float32), 'Wk': jax.random.normal(ks[2], (D_MODEL, D_MODEL), dtype=jnp.float32) * s, 'bk': jnp.zeros((D_MODEL,), dtype=jnp.float32), 'Wv': jax.random.normal(ks[3], (D_MODEL, D_MODEL), dtype=jnp.float32) * s, 'bv': jnp.zeros((D_MODEL,), dtype=jnp.float32), 'Wo': jax.random.normal(ks[4], (D_MODEL, D_MODEL), dtype=jnp.float32) * s, 'bo': jnp.zeros((D_MODEL,), dtype=jnp.float32)}
    _L1_attn_in = _L1_attn_setup()

    def _L1_ffn_setup():
        import jax, jax.numpy as jnp
        import numpy as np
        TOP_K = 2
        key = jax.random.key(seed)
        ks = jax.random.split(key, 5)
        B, S, H, I, E = (4, 256, 128, 512, 8)
        scale_hi = (2.0 / (H + I)) ** 0.5
        scale_he = (2.0 / (H + E)) ** 0.5
        return {'x': jax.random.normal(ks[0], (B, S, H), dtype=jnp.float32), 'router_w': jax.random.normal(ks[1], (E, H), dtype=jnp.float32) * scale_he, 'gate_w': jax.random.normal(ks[2], (E, I, H), dtype=jnp.float32) * scale_hi, 'up_w': jax.random.normal(ks[3], (E, I, H), dtype=jnp.float32) * scale_hi, 'down_w': jax.random.normal(ks[4], (E, H, I), dtype=jnp.float32) * scale_hi}
    _L1_ffn_in = _L1_ffn_setup()
    _d = {'L0_attn_x': _L0_attn_in['x'], 'L0_attn_Wq': _L0_attn_in['Wq'], 'L0_attn_Wk': _L0_attn_in['Wk'], 'L0_attn_Wv': _L0_attn_in['Wv'], 'L0_ffn_sW1': _L0_ffn_in['sW1'], 'L0_ffn_sb1': _L0_ffn_in['sb1'], 'L0_ffn_sW2': _L0_ffn_in['sW2'], 'L0_ffn_sb2': _L0_ffn_in['sb2'], 'L0_ffn_rW1': _L0_ffn_in['rW1'], 'L0_ffn_rb1': _L0_ffn_in['rb1'], 'L0_ffn_rW2': _L0_ffn_in['rW2'], 'L0_ffn_rb2': _L0_ffn_in['rb2'], 'L0_ffn_gW': _L0_ffn_in['gW'], 'L0_ffn_gb': _L0_ffn_in['gb'], 'L1_attn_Wq': _L1_attn_in['Wq'], 'L1_attn_bq': _L1_attn_in['bq'], 'L1_attn_Wk': _L1_attn_in['Wk'], 'L1_attn_bk': _L1_attn_in['bk'], 'L1_attn_Wv': _L1_attn_in['Wv'], 'L1_attn_bv': _L1_attn_in['bv'], 'L1_attn_Wo': _L1_attn_in['Wo'], 'L1_attn_bo': _L1_attn_in['bo'], 'L1_ffn_router_w': _L1_ffn_in['router_w'], 'L1_ffn_gate_w': _L1_ffn_in['gate_w'], 'L1_ffn_up_w': _L1_ffn_in['up_w'], 'L1_ffn_down_w': _L1_ffn_in['down_w']}
    _x0 = _d['L0_attn_x']
    _d['L0_attn_x'] = jax.random.normal(jax.random.fold_in(jax.random.key(seed), 1), (16, 256, 128), dtype=_x0.dtype)
    del _x0
    return _d

def reference(L0_attn_x, L0_attn_Wq, L0_attn_Wk, L0_attn_Wv, L0_ffn_sW1, L0_ffn_sb1, L0_ffn_sW2, L0_ffn_sb2, L0_ffn_rW1, L0_ffn_rb1, L0_ffn_rW2, L0_ffn_rb2, L0_ffn_gW, L0_ffn_gb, L1_attn_Wq, L1_attn_bq, L1_attn_Wk, L1_attn_bk, L1_attn_Wv, L1_attn_bv, L1_attn_Wo, L1_attn_bo, L1_ffn_router_w, L1_ffn_gate_w, L1_ffn_up_w, L1_ffn_down_w):

    def _L0_attn_ref(x, Wq, Wk, Wv):
        import jax, jax.numpy as jnp
        import numpy as np
        DIM_IN, DIM_K, DIM_V, NH = (128, 128, 128, 16)
        DK, DV = (DIM_K // NH, DIM_V // NH)
        B, S, _ = x.shape
        scale = 1.0 / np.sqrt(DK)
        q = (x @ Wq.T).reshape(B, S, NH, DK).transpose(0, 2, 1, 3)
        k = x @ Wk.T
        v = x @ Wv.T
        dist = jnp.einsum('bhqd,bkd->bhqk', q, k) * scale
        dist = jax.nn.softmax(dist, axis=-1)
        att = jnp.einsum('bhqk,bkd->bhqd', dist, v)
        return att.transpose(0, 2, 1, 3).reshape(B, S, DIM_V)

    def _L0_ffn_ref(x, sW1, sb1, sW2, sb2, rW1, rb1, rW2, rb2, gW, gb):
        import jax, jax.numpy as jnp
        import numpy as np
        D_MODEL = 128
        D_FF = 512
        NUM_M = 2
        E_ROUTER = 8 * NUM_M - 1
        D_FF_R = D_FF // NUM_M
        TOP_K = NUM_M * 2 - 1
        B, T = (2, 256)

        def _expert_stack(x, W1, b1, W2, b2):
            h = jax.nn.gelu(jnp.einsum('btd,edf->ebtf', x, W1) + b1[:, None, None, :], approximate=False)
            return jnp.einsum('ebtf,efd->ebtd', h, W2) + b2[:, None, None, :]
        shared_enc = _expert_stack(x, sW1, sb1, sW2, sb2).sum(0)
        weights = jax.nn.softmax(x @ gW + gb, axis=-1)
        topv, topi = jax.lax.top_k(weights, TOP_K)
        gated = (jax.nn.one_hot(topi, E_ROUTER, dtype=weights.dtype) * topv[..., None]).sum(axis=-2)
        router_out = _expert_stack(x, rW1, rb1, rW2, rb2)
        router_enc = jnp.einsum('ebtd,bte->btd', router_out, gated)
        return shared_enc + router_enc + x

    def _L1_attn_ref(x, Wq, bq, Wk, bk, Wv, bv, Wo, bo):
        import math
        import jax, jax.numpy as jnp
        import numpy as np
        D_MODEL = 128
        NUM_HEADS = 16
        D_HEAD = D_MODEL // NUM_HEADS
        K_S = 32
        B, N = (2, 256)

        def _attn(x, Wq, bq, Wk, bk, Wv, bv, Wo, bo):
            b, n, _ = x.shape
            q = (x @ Wq.T + bq).reshape(b, n, NUM_HEADS, D_HEAD).transpose(0, 2, 1, 3)
            k = (x @ Wk.T + bk).reshape(b, n, NUM_HEADS, D_HEAD).transpose(0, 2, 1, 3)
            v = (x @ Wv.T + bv).reshape(b, n, NUM_HEADS, D_HEAD).transpose(0, 2, 1, 3)
            scores = jnp.einsum('bhqd,bhkd->bhqk', q, k) / math.sqrt(D_HEAD)
            causal = jnp.triu(jnp.ones((n, n), dtype=bool), k=1)
            neg_inf = jnp.array(-jnp.inf, dtype=scores.dtype)
            scores = jnp.where(causal, neg_inf, scores)
            vals, idx = jax.lax.top_k(scores, K_S)
            masked = jnp.full_like(scores, -jnp.inf)
            masked = jnp.put_along_axis(masked, idx, vals, axis=-1, inplace=False)
            attn = jax.nn.softmax(masked, axis=-1)
            out = jnp.einsum('bhqk,bhkd->bhqd', attn, v)
            out = out.transpose(0, 2, 1, 3).reshape(b, n, D_MODEL)
            y = out @ Wo.T + bo
            return (y, attn.mean(axis=1))

        def _reference_tuple_inner(x, Wq, bq, Wk, bk, Wv, bv, Wo, bo):
            return _attn(x, Wq, bq, Wk, bk, Wv, bv, Wo, bo)
        return _reference_tuple_inner(x, Wq, bq, Wk, bk, Wv, bv, Wo, bo)[0]

    def _L1_ffn_ref(x, router_w, gate_w, up_w, down_w):
        import jax, jax.numpy as jnp
        import numpy as np
        TOP_K = 2
        B, S, H = x.shape
        E = router_w.shape[0]
        xf = x.reshape(-1, H)
        logits = xf @ router_w.T
        probs = jax.nn.softmax(logits, axis=-1)
        topk_p, topk_i = jax.lax.top_k(probs, TOP_K)
        topk_p = topk_p / topk_p.sum(axis=-1, keepdims=True)

        def body(out, inputs):
            e, gw, uw, dw = inputs
            sel = topk_i == e
            mask = sel.any(axis=-1)
            w_tok = (topk_p * sel).sum(axis=-1)
            cnt = mask.sum().astype(xf.dtype)
            mean_w = jnp.where(cnt > 0, w_tok.sum() / jnp.maximum(cnt, 1.0), 0.0)
            h = jax.nn.silu(xf @ gw.T) * (xf @ uw.T)
            eo = h @ dw.T
            out = out + mask[:, None].astype(xf.dtype) * eo * mean_w
            return (out, None)
        out0 = jnp.zeros_like(xf)
        out, _ = jax.lax.scan(body, out0, (jnp.arange(E), gate_w, up_w, down_w))
        return out.reshape(B, S, H)
    x = L0_attn_x
    xn = _layernorm(x, axis=-1)
    s = _L0_attn_ref(xn, L0_attn_Wq, L0_attn_Wk, L0_attn_Wv)
    g = _silu(_L0_ffn_ref(xn, L0_ffn_sW1, L0_ffn_sb1, L0_ffn_sW2, L0_ffn_sb2, L0_ffn_rW1, L0_ffn_rb1, L0_ffn_rW2, L0_ffn_rb2, L0_ffn_gW, L0_ffn_gb))
    x = x + s * g
    xn = _layernorm(x, axis=-1)
    s = _L1_attn_ref(xn, L1_attn_Wq, L1_attn_bq, L1_attn_Wk, L1_attn_bk, L1_attn_Wv, L1_attn_bv, L1_attn_Wo, L1_attn_bo)
    g = _silu(_L1_ffn_ref(xn, L1_ffn_router_w, L1_ffn_gate_w, L1_ffn_up_w, L1_ffn_down_w))
    x = x + s * g
    return x

_drawn_inputs = setup_inputs


def setup_inputs(seed=0):
    import zlib

    import numpy as np

    out = dict(_drawn_inputs(seed))
    spreads = {'L1_attn_bq': (0.0, 2.0),
     'L1_attn_bk': (0.0, 2.0),
     'L1_attn_bv': (0.0, 0.759),
     'L1_attn_bo': (0.0, 0.8)}
    factors = {'L0_ffn_sW1': 3.657,
     'L0_ffn_sb1': 8.0,
     'L0_ffn_sW2': 3.388,
     'L0_ffn_sb2': 30.589,
     'L0_ffn_rW1': 8.0,
     'L0_ffn_rb1': 8.0,
     'L0_ffn_rW2': 8.0,
     'L0_ffn_rb2': 27.383,
     'L0_ffn_gW': 8.0,
     'L0_ffn_gb': 8.0,
     'L1_attn_Wq': 3.545,
     'L1_attn_Wk': 2.966}
    for name, (base, spread) in spreads.items():
        noise = np.random.default_rng([zlib.crc32(name.encode()), seed]).standard_normal(out[name].shape)
        drawn = base * np.exp(spread * noise) if base else spread * noise
        out[name] = jnp.asarray(drawn.astype(out[name].dtype))
    for name, factor in factors.items():
        out[name] = (out[name] * factor).astype(out[name].dtype)
    return out
```

```python
from contextlib import ExitStack

import numpy as np

import concourse.bass as bass
from concourse import mybir

F32 = mybir.dt.float32
F32R = mybir.dt.float32r
BF16 = mybir.dt.bfloat16
ALU = mybir.AluOpType
ACT = mybir.ActivationFunctionType
AX_X = mybir.AxisListType.X

P = 128
D = 128
NSEQ, SEQ = 16, 256
NTOK = NSEQ * SEQ
NT = NTOK // P
CH = 512
CT = CH // P
NCH = NTOK // CH
NH, DH = 16, 8
NG, HG = 4, 4
SCALE = float(DH) ** -0.5
TOPK = 32
F_SH, F_R, NE0 = 512, 256, 15
T_SH = F_SH // P
TILES0 = (F_SH + NE0 * F_R) // P
NE1, F1 = 8, 512
TILES1 = NE1 * F1 // P
PER_E1 = F1 // P
EPS = 1e-5
MASKED = -1.0e30
TAKEN = -2.0e30
IS_TAKEN = -1.5e30
NEVER = -3.0e38
ROUNDS = 8
W1C = 3 * P
W0 = 2 * SEQ


def plan(topk, mqa_per_round):
    rounds, n, waiting, searched = [], 0, [], []
    for r in range(ROUNDS):
        scored = [(1, r)] if topk else []
        scored += [(0, n + k) for k in range(mqa_per_round[r])]
        n += mqa_per_round[r]
        scored = scored or [None]
        slots = []
        for k, pair in enumerate(scored):
            turned = []
            if k == (1 if topk and len(scored) > 1 else 0):
                turned += searched
                searched = [(1, r)] if topk else []
            if pair is None or pair[0] == 0 or len(scored) == 1:
                turned += waiting
                waiting = [pair] if pair is not None and pair[0] == 0 else []
            slots.append((pair, turned))
        rounds.append(slots)
    rounds.append([(None, waiting + searched)])
    return rounds


def build(nc, A, out):
    GD = nc.dram_tensor("gates_t", (16, NTOK), F32, kind="Internal").ap()
    MD = nc.dram_tensor("masks_t", (NE1, NTOK), F32, kind="Internal").ap()
    with ExitStack() as ctx:
        def sb(name, shape, dt=F32, c=ctx):
            return c.enter_context(nc.sbuf_tensor(name, shape, dt))

        ps = ctx.enter_context(nc.psum_tensor("ps", [P, 8, 512], F32))
        B_H0, B_H1, B_ACC, B_S, B_PT, B_O, B_MI = 0, 1, 2, 3, 5, 6, 7
        S = ps[:, B_S:B_S + 2, :]
        PT = ps[:, B_PT, :]
        OB = [ps[:, B_O, 0:SEQ], ps[:, B_O, SEQ:2 * SEQ]]
        MI = ps[:, B_MI, :]
        ACC = ps[:, B_ACC, :]

        xall = sb("xall", [P, NT, D])
        sall = sb("sall", [P, NT, D])
        xT = sb("xT", [P, NTOK])
        ident = sb("ident", [P, P])
        ident16 = sb("ident16", [P, P], BF16)
        causal16 = sb("causal16", [P, P], BF16)
        lane = sb("lane", [P, HG])
        ones = sb("ones", [P, P])
        wq0 = sb("wq0", [P, D])
        wk0 = sb("wk0", [P, NH, DH])
        wv0 = sb("wv0", [P, DH])
        wq1 = sb("wq1", [P, D])
        wk1 = sb("wk1", [P, D])
        wv1 = sb("wv1", [P, D])
        wo1 = sb("wo1", [P, D])
        rows = sb("rows", [1, 2 * D])
        cols = sb("cols", [P, 2])
        bkm = sb("bkm", [P, HG])
        rw1 = sb("rw1", [P, NE1])
        epsb = sb("epsb", [P, 1])
        racc = sb("racc", [P, CT, 16])
        xw1 = sb("xw1", [P, SEQ])
        qT1 = sb("qT1", [P, SEQ])
        km1 = sb("km1", [P, HG, SEQ])
        vx1 = sb("vx1", [P, 2, NH, 32])
        e1 = sb("e1", [P, 2, 2, W1C])
        xr = sb("xr", [P, 2, 2, W1C])
        top8 = sb("top8", [P, 2, 4, 4, 8])
        nm1 = sb("nm1", [P, 2, 4])
        pts = sb("pts", [P, 2, 2, W0])
        ot1 = sb("ot1", [P, HG, SEQ])
        att1 = sb("att1", [P, 2, D])
        attT = sb("attT", [P, SEQ])
        rc1 = sb("rc1", [P, NH])
        xhi = sb("xhi", [P, CH], F32R)
        xlo = sb("xlo", [P, CH], F32R)

        sems = {}

        def sem(name):
            sems[name] = ctx.enter_context(nc.semaphore(name))
            return sems[name]

        x_in = [sem(f"x_in{n}") for n in range(4)]
        w_in = sem("w_in")
        stage_in = [sem(f"stage_in{n}") for n in range(2)]
        gate_in = [sem(f"gate_in{n}") for n in range(4)]
        stored = sem("stored")
        xw1_ready = sem("xw1_ready")
        xw0_ready = sem("xw0_ready")
        qkv_ready = sem("qkv_ready")
        scored = sem("scored")
        neg_max = sem("neg_max")
        row_max = sem("row_max")
        exp_done = sem("exp_done")
        top_found = sem("top_found")
        top_taken = sem("top_taken")
        is_taken = sem("is_taken")
        p_ready = sem("p_ready")
        turned = sem("turned")
        pts_ready = sem("pts_ready")
        pv_done = sem("pv_done")
        o_taken = sem("o_taken")
        mi_full = sem("mi_full")
        mi_free = sem("mi_free")
        rc_ready = sem("rc_ready")
        att_ready = sem("att_ready")
        split = sem("split")
        up_done = sem("up_done")
        act_done = sem("act_done")
        gated = sem("gated")
        down_done = sem("down_done")
        masked = sem("masked")
        acc_taken = sem("acc_taken")
        silu_done = sem("silu_done")
        resid = sem("resid")
        stats = sem("stats")
        aggr = sem("aggr")
        std_done = sem("std_done")
        rstd_done = sem("rstd_done")
        xn_ready = sem("xn_ready")
        xt_ready = sem("xt_ready")
        kept = sem("kept")
        lg_ready = sem("lg_ready")
        lg_max = sem("lg_max")
        lg_dif = sem("lg_dif")
        lg_exp = sem("lg_exp")
        lg_taken = sem("lg_taken")
        route = sem("route")
        mask_t = sem("mask_t")
        prep = sem("prep")
        consts = sem("consts")

        numbers = sorted(s.num for s in sems.values())
        assert numbers == list(range(numbers[0], numbers[0] + len(numbers)))

        def clear_semaphores():
            nc.multi_engine_barrier(list(nc.engines.keys()),
                                    sems_to_clear=range(numbers[0], numbers[-1] + 1))

        clear_semaphores()

        def pair_heads(n):
            j, gp = n // 2, n % 2
            return j, (2 * gp, 2 * gp + 1)

        def tiles(n, layer):
            if layer == 1:
                return [(g, c, w) for g in range(2) for c, w in ((0, P), (P, 2 * P))]
            return [(g, c, SEQ) for g in range(2) for c in (0, SEQ)]

        class Schedule:

            def __init__(self, topk, mqa_per_round):
                self.rounds = plan(topk, mqa_per_round)
                self.scored = [p for r in self.rounds for p, _ in r if p is not None]
                self.turned = [p for r in self.rounds for _, t in r for p in t]

            def s(self, pair):
                return self.scored.index(pair)

            def t(self, pair):
                return self.turned.index(pair)

            def o_before(self, pair):
                return sum(1 for q in self.turned[:self.t(pair)] if q[1] % 2 == 1)

        def attention_steps(sch, mqa):

            def pe_scores(pe, pair):
                layer, n = pair
                k = sch.s(pair)
                if k:
                    pe.wait_ge(exp_done, k)
                j, groups = pair_heads(n % ROUNDS)
                if layer == 1:
                    qT, km = qT1[:, :], km1
                    for b in range(2):
                        o = S[:, b, 0:W1C].rearrange("p (a k) -> p a k", k=P)[:, 0:3:2, :]
                        nc.tensor.matmul(o, ident16[:, :],
                                         causal16[:, :].unsqueeze(1).broadcast_to([P, 2, P]),
                                         start=True, stop=True)
                    for c0, w, q0 in ((0, P, 0), (P, 2 * P, P)):
                        for b, g in enumerate(groups):
                            last = nc.tensor.matmul(S[:, b, c0:c0 + w],
                                                    qT[32 * g:32 * g + 32, q0:q0 + P],
                                                    km[32 * g:32 * g + 32, j, 0:w],
                                                    start=False, stop=True, skip_group_check=True)
                else:
                    qT, km = mqa.qT[:, n // ROUNDS, :], mqa.km[:, n // ROUNDS, :, :]
                    for q in range(2):
                        for b, g in enumerate(groups):
                            last = nc.tensor.matmul(S[:, b, q * SEQ:(q + 1) * SEQ],
                                                    qT[32 * g:32 * g + 32, q * P:(q + 1) * P],
                                                    km[32 * g:32 * g + 32, j, :],
                                                    start=True, stop=True)
                last.then_inc(scored, 1)

            def pe_turn(pe, pair, fill):
                layer, n = pair
                k = sch.t(pair)
                j, groups = pair_heads(n % ROUNDS)
                for b in range(2):
                    if 2 * k + b:
                        pe.wait_ge(pts_ready, 2 * k + b)
                    if layer == 1:
                        pe.wait_ge(p_ready, n + 1)
                        src = e1[:, n % 2, b, :]
                        blocks = (0, P, 2 * P)
                    else:
                        pe.wait_ge(exp_done, sch.s(pair) + 1)
                        src = mqa.e[:, n % 2, b, :]
                        blocks = (0, SEQ, P, SEQ + P)
                    for m, c in enumerate(blocks):
                        last = nc.tensor.transpose(PT[:, m * P:(m + 1) * P], src[:, c:c + P], ident[:, :])
                    last.then_inc(turned, 1)
                    fill(pe)
                pe.wait_ge(pts_ready, 2 * k + 2)
                if sch.o_before(pair):
                    pe.wait_ge(o_taken, sch.o_before(pair))
                for kt in range(2):
                    for b, g in enumerate(groups):
                        o = OB[layer][32 * g:32 * g + 32, :]
                        p = pts[:, k % 2, b, :]
                        if layer == 1:
                            h = HG * g + j
                            if kt == 0:
                                last = nc.tensor.matmul(o, vx1[:, 0, h, :], p[:, 0:SEQ],
                                                        start=True, stop=True)
                            else:
                                last = nc.tensor.matmul(o[:, P:SEQ], vx1[:, 1, h, :], p[:, SEQ:W1C],
                                                        start=False, stop=True, skip_group_check=True)
                        else:
                            last = nc.tensor.matmul(o, mqa.vx[:, n // ROUNDS, kt, :],
                                                    p[:, kt * SEQ:(kt + 1) * SEQ],
                                                    start=(kt == 0), stop=(kt == 1))
                last.then_inc(pv_done, 1)

            def act_exp(act, pair):
                layer, n = pair
                act.wait_ge(neg_max, sch.s(pair) + 1)
                if layer == 1:
                    act.wait_ge(top_taken, 16 * n + 4)
                    if n >= 2:
                        act.wait_ge(turned, 2 * sch.t((1, n - 2)) + 2)
                    dst, nm = e1[:, n % 2], nm1[:, n % 2]
                else:
                    if n >= 2:
                        act.wait_ge(turned, 2 * sch.t((0, n - 2)) + 2)
                    dst, nm = mqa.e[:, n % 2], mqa.nm[:, n % 2]
                for m, (b, c, w) in enumerate(tiles(n, layer)):
                    last = nc.scalar.activation(dst[:, b, c:c + w], S[:, b, c:c + w], ACT.Exp,
                                                bias=nm[:, m:m + 1], scale=SCALE)
                last.then_inc(exp_done, 1)

            def act_empty(act, pair, b):
                k = sch.t(pair)
                w = W1C if pair[0] == 1 else W0
                act.wait_ge(turned, 2 * k + b + 1)
                if k >= 2:
                    act.wait_ge(pv_done, k - 1)
                nc.scalar.activation(pts[:, k % 2, b, 0:w], PT[:, 0:w], ACT.Copy).then_inc(pts_ready, 1)

            def act_output(act, pair):
                layer, n = pair
                act.wait_ge(pv_done, sch.t(pair) + 1)
                j = (n % ROUNDS) // 2
                dst = ot1[:, j, :] if layer == 1 else mqa.ot[:, n // ROUNDS, j, :]
                nc.scalar.activation(dst, OB[layer], ACT.Copy).then_inc(o_taken, 1)

            def dve_max(dve, pair):
                n = pair[1]
                dve.wait_ge(scored, sch.s(pair) + 1)
                nc.vector.reduce_max(mqa.mx[:, n % 2, :], S.rearrange("p b (q k) -> p (b q) k", k=SEQ),
                                     AX_X).then_inc(row_max, 1)
                dve.wait_ge(row_max, n + 1)
                nc.vector.tensor_scalar(mqa.nm[:, n % 2, :], mqa.mx[:, n % 2, :], -SCALE, None,
                                        ALU.mult).then_inc(neg_max, 1)

            def dve_top(dve, n, k):
                if k == 0:
                    dve.wait_ge(scored, sch.s((1, n)) + 1)
                    if n >= 2:
                        dve.wait_ge(p_ready, n - 1)
                done = 16 * n + 4 * k
                for m, (b, c, w) in enumerate(tiles(n, 1)):
                    src = S[:, b, c:c + w] if k == 0 else xr[:, n % 2, b, c:c + w]
                    if k:
                        dve.wait_ge(top_taken, done - 4 + m + 1)
                    nc.vector.max(top8[:, n % 2, k, m, :], src).then_inc(top_found, 1)
                if k == 0:
                    dve.wait_ge(top_found, done + 4)
                    nc.vector.tensor_scalar(nm1[:, n % 2, :], top8[:, n % 2, 0, :, 0], -SCALE, None,
                                            ALU.mult).then_inc(neg_max, 1)
                for m, (b, c, w) in enumerate(tiles(n, 1)):
                    src = S[:, b, c:c + w] if k == 0 else xr[:, n % 2, b, c:c + w]
                    dve.wait_ge(top_found, done + m + 1)
                    nc.vector.match_replace(xr[:, n % 2, b, c:c + w], top8[:, n % 2, k, m, :], src,
                                            TAKEN).then_inc(top_taken, 1)

            def pool_select(pool, n):
                pool.wait_ge(top_taken, 16 * n + 16)
                pool.wait_ge(exp_done, sch.s((1, n)) + 1)
                nc.gpsimd.tensor_scalar(xr[:, n % 2], xr[:, n % 2], IS_TAKEN, None, ALU.is_lt
                                        ).then_inc(is_taken, 1)
                pool.wait_ge(is_taken, n + 1)
                nc.gpsimd.tensor_tensor(e1[:, n % 2], e1[:, n % 2], xr[:, n % 2], ALU.mult
                                        ).then_inc(p_ready, 1)

            return pe_scores, pe_turn, act_exp, act_empty, act_output, dve_max, dve_top, pool_select

        def block(i, phase, topk, seq0):
            is_a, is_b, is_m = phase == "A", phase == "B", phase == "M"
            sch = Schedule(topk, [3, 3, 3, 3, 2, 2, 0, 0] if is_a else [0] * ROUNDS)
            per_round = {"A": [6, 6, 6, 6, 5, 5, 0, 0], "B": [4] * ROUNDS, "M": [0] * ROUNDS}[phase]
            first = [sum(per_round[:r]) for r in range(ROUNDS + 1)]
            (pe_scores, pe_turn, act_exp, act_empty, act_output, dve_max, dve_top,
             pool_select) = attention_steps(sch, mqa if is_a else None)
            tok0 = i * CH
            chunk = xT[:, bass.ds(tok0, CH)]
            x_tiles = xall[:, bass.ds(i * CT, CT), :]

            uses = ["qk1", "v1"] if topk else []
            if is_a:
                uses += ["qk0_0", "v0_0", "qk0_1", "v0_1", "o0_0", "o0_1", "o0_2", "o0_3",
                         "ffn", "ln", "logits", "masks"]
            if is_m:
                uses += ["total"]
            if is_b:
                uses += ["ffn"]
            if topk:
                uses += ["o1_0", "o1_1", "att1", "y1"]

            def bank_mine(pe, name):
                if uses.index(name):
                    pe.wait_ge(mi_free, uses.index(name))

            def bank_full(eng, name):
                eng.wait_ge(mi_full, uses.index(name) + 1)

            with nc.Block(no_gpsimd_drain=True) as blk:

                @blk.sync
                def _(sp):
                    if is_a:
                        for e in range(NE0):
                            if e >= 4:
                                sp.wait_ge(gated, 2 * (e - 4) + 2)
                            sp.dma_start(mqa.gate[:, e % 4, :],
                                         GD[e:e + 1, bass.ds(tok0, CH)].broadcast_to([P, CH])
                                         ).then_inc(gate_in[e % 4], 16)
                            if e == 3:
                                sp.dma_start(mqa.gt[:, :], GD[:, bass.ds(tok0, CH)]).then_inc(w_in, 16)
                        sp.wait_ge(mask_t, 1)
                        sp.dma_start(MD[:, bass.ds(tok0, CH)], mqa.mkT).then_inc(stored, 16)
                        sp.wait_ge(stored, 16)
                    if is_b:
                        for e in range(NE1):
                            if e >= 2:
                                sp.wait_ge(masked, 2 * (e - 2) + 2)
                            sp.dma_start(moe.mask[:, e % 2, :],
                                         MD[e:e + 1, bass.ds(tok0, CH)].broadcast_to([P, CH])
                                         ).then_inc(gate_in[e % 2], 16)
                    if is_m:
                        sp.dma_start(moe.down[:, :, :], A["w_down"]).then_inc(w_in, 16)
                        for n in range(8):
                            if n >= 2:
                                sp.wait_ge(split, n - 1)
                            src = A["w_gate" if n < 4 else "w_up"][:, (n % 4) * 1024:(n % 4 + 1) * 1024]
                            sp.dma_start(moe.stage[:, n % 2, :], src).then_inc(stage_in[n % 2], 16)

                @blk.tensor
                def _(pe):
                    n_down = [0]

                    def up(t):
                        if t >= 2:
                            pe.wait_ge(act_done, t - 1)
                        f = slice(t * P, (t + 1) * P)
                        o = ps[:, B_H0 + t % 2, :]
                        nc.tensor.matmul(o, mqa.w1hi[:, f], xhi[:, :], start=True, stop=False)
                        nc.tensor.matmul(o, mqa.w1lo[:, f], xhi[:, :], start=False, stop=False)
                        nc.tensor.matmul(o, mqa.w1hi[:, f], xlo[:, :], start=False, stop=True
                                         ).then_inc(up_done, 1)

                    def down(t):
                        if t < T_SH:
                            pe.wait_ge(act_done, t + 1)
                        else:
                            pe.wait_ge(gated, t - T_SH + 1)
                        nc.tensor.matmul(ACC, mqa.w2[:, t, :], mqa.hb[:, t % 6, :], start=(t == 0), stop=False
                                         ).then_inc(down_done, 1)

                    def gate_up(t):
                        f = slice(t * P, (t + 1) * P)
                        e = t // PER_E1
                        if t:
                            pe.wait_ge(act_done, t)
                        o = ps[:, B_H0, :]
                        nc.tensor.matmul(o, moe.ghi[:, f], xhi[:, :], start=True, stop=False)
                        nc.tensor.matmul(o, moe.glo[:, f], xhi[:, :], start=False, stop=False)
                        nc.tensor.matmul(o, moe.ghi[:, f], xlo[:, :], start=False, stop=True
                                         ).then_inc(up_done, 1)
                        if t:
                            pe.wait_ge(gated, t)
                        if t % PER_E1 == 0:
                            pe.wait_ge(masked, 2 * e + 2)
                        o = ps[:, B_H1, :]
                        mhi, mlo = moe.xmhi[:, e % 2, :], moe.xmlo[:, e % 2, :]
                        nc.tensor.matmul(o, moe.uhi[:, f], mhi, start=True, stop=False)
                        nc.tensor.matmul(o, moe.ulo[:, f], mhi, start=False, stop=False)
                        nc.tensor.matmul(o, moe.uhi[:, f], mlo, start=False, stop=True
                                         ).then_inc(up_done, 1)

                    def down1(t):
                        pe.wait_ge(gated, t + 1)
                        nc.tensor.matmul(ACC, moe.down[:, t, :], moe.h[:, t % 2, :], start=(t == 0),
                                         stop=(t == TILES1 - 1)).then_inc(down_done, 1)

                    if topk:
                        pe.wait_ge(xw1_ready, 1)
                        bank_mine(pe, "qk1")
                        nc.tensor.matmul(MI[:, 0:SEQ], wq1[:, :], xw1[:, :], start=True, stop=True)
                        nc.tensor.matmul(MI[:, SEQ:2 * SEQ], wk1[:, :], xw1[:, :], start=True,
                                         stop=True).then_inc(mi_full, 1)
                        bank_mine(pe, "v1")
                        for q in range(2):
                            o = MI[:, q * P:(q + 1) * P]
                            nc.tensor.matmul(o, xw1[:, q * P:(q + 1) * P], wv1[:, :], start=True, stop=False)
                            last = nc.tensor.matmul(o, ones[0:1, :], rows[0:1, 0:D], start=False, stop=True)
                        last.then_inc(mi_full, 1)
                    if is_a:
                        pe.wait_ge(xw0_ready, 1)
                        for s in range(2):
                            xs = mqa.xw[:, s * SEQ:(s + 1) * SEQ]
                            bank_mine(pe, f"qk0_{s}")
                            nc.tensor.matmul(MI[:, 0:SEQ], wq0[:, :], xs, start=True, stop=True)
                            nc.tensor.matmul(MI[:, SEQ:2 * SEQ], wk0[:, :, :].rearrange("p h d -> p (h d)"),
                                             xs, start=True, stop=True).then_inc(mi_full, 1)
                            bank_mine(pe, f"v0_{s}")
                            for q in range(2):
                                last = nc.tensor.matmul(MI[:, q * DH:(q + 1) * DH], xs[:, q * P:(q + 1) * P],
                                                        wv0[:, :], start=True, stop=True)
                            last.then_inc(mi_full, 1)
                    if topk or is_a:
                        pe.wait_ge(qkv_ready, n_qkv(topk, is_a))
                    if is_a or is_b:
                        pe.wait_ge(split, 2)
                    if is_a:
                        pe.wait_ge(w_in, 16)

                    for r in range(ROUNDS + 1):
                        if is_a and r == ROUNDS:
                            break
                        tile = [first[r] if r < ROUNDS else TILES1]

                        def fill(pe):
                            if is_a and n_down[0] < first[r]:
                                down(n_down[0])
                                n_down[0] += 1
                            if is_b and r < ROUNDS and tile[0] < first[r + 1]:
                                gate_up(tile[0])
                                if tile[0]:
                                    down1(tile[0] - 1)
                                tile[0] += 1

                        for pair, turn in sch.rounds[r]:
                            if pair is not None:
                                pe_scores(pe, pair)
                            if is_b and r < ROUNDS:
                                fill(pe)
                            for t in turn:
                                pe_turn(pe, t, fill)
                        if is_a:
                            while n_down[0] < first[r]:
                                fill(pe)
                            for t in range(first[r], first[r + 1]):
                                up(t)
                        if is_b and r < ROUNDS:
                            while tile[0] < first[r + 1]:
                                fill(pe)
                    if is_a:
                        nc.tensor.matmul(ACC, mqa.b2[:, :], mqa.gt[:, :], start=False, stop=True
                                         ).then_inc(down_done, 1)
                        pe.wait_ge(o_taken, n_l0_out(sch))
                        for q in range(4):
                            bank_mine(pe, f"o0_{q}")
                            for j in range(HG):
                                last = nc.tensor.transpose(MI[:, j * P:(j + 1) * P],
                                                           mqa.ot[:, q // 2, j, (q % 2) * P:(q % 2 + 1) * P],
                                                           ident[:, :])
                            last.then_inc(mi_full, 1)
                        bank_mine(pe, "ffn")
                        pe.wait_ge(acc_taken, 1)
                        for t in range(CT):
                            last = nc.tensor.transpose(MI[:, t * P:(t + 1) * P],
                                                       mqa.fs[:, t * P:(t + 1) * P], ident[:, :])
                        last.then_inc(mi_full, 1)
                        bank_mine(pe, "ln")
                        pe.wait_ge(xn_ready, CT)
                        for t in range(CT):
                            last = nc.tensor.transpose(MI[:, t * P:(t + 1) * P], mqa.xn[:, t, :], ident[:, :])
                        last.then_inc(mi_full, 1)
                        bank_mine(pe, "logits")
                        pe.wait_ge(xt_ready, 1)
                        for t in range(CT):
                            last = nc.tensor.matmul(MI[:, t * NE1:(t + 1) * NE1],
                                                    mqa.xtn[:, t * P:(t + 1) * P], rw1[:, :],
                                                    start=True, stop=True)
                        last.then_inc(mi_full, 1)
                        bank_mine(pe, "masks")
                        pe.wait_ge(route, 1)
                        for t in range(CT):
                            last = nc.tensor.transpose(MI[0:NE1, t * P:(t + 1) * P], mqa.mw[:, t, 0:NE1],
                                                       ident[:, :])
                        last.then_inc(mi_full, 1)
                        for _, turn in sch.rounds[ROUNDS]:
                            for t in turn:
                                pe_turn(pe, t, lambda pe: None)
                    if is_m:
                        bank_mine(pe, "total")
                        pe.wait_ge(route, 1)
                        nc.tensor.matmul(MI[:, 0:16], ones[:, :], moe.rsum[:, :], start=True, stop=True
                                         ).then_inc(mi_full, 1)
                    if is_b:
                        down1(TILES1 - 1)
                        bank_mine(pe, "ffn")
                        pe.wait_ge(acc_taken, 1)
                        for t in range(CT):
                            last = nc.tensor.transpose(MI[:, t * P:(t + 1) * P],
                                                       moe.fs[:, t * P:(t + 1) * P], ident[:, :])
                        last.then_inc(mi_full, 1)
                    if topk:
                        pe.wait_ge(o_taken, len([p for p in sch.turned if p[1] % 2 == 1]))
                        for q in range(2):
                            bank_mine(pe, f"o1_{q}")
                            for j in range(HG):
                                last = nc.tensor.transpose(MI[:, j * P:(j + 1) * P],
                                                           ot1[:, j, q * P:(q + 1) * P], ident[:, :])
                            last.then_inc(mi_full, 1)
                        n_att = (4 if is_a else 0)
                        bank_mine(pe, "att1")
                        pe.wait_ge(att_ready, n_att + 2)
                        for q in range(2):
                            last = nc.tensor.transpose(MI[:, q * P:(q + 1) * P], att1[:, q, :], ident[:, :])
                        last.then_inc(mi_full, 1)
                        bank_mine(pe, "y1")
                        pe.wait_ge(prep, 1)
                        for q in range(2):
                            o = MI[:, q * P:(q + 1) * P]
                            nc.tensor.matmul(o, attT[:, q * P:(q + 1) * P], wo1[:, :], start=True, stop=False)
                            last = nc.tensor.matmul(o, ones[0:1, :], rows[0:1, D:2 * D], start=False, stop=True)
                        last.then_inc(mi_full, 1)

                @blk.scalar
                def _(act):
                    def gelu(t):
                        act.wait_ge(up_done, t + 1)
                        if t >= 6:
                            act.wait_ge(down_done, t - 5)
                        nc.scalar.activation(mqa.hb[:, t % 6, :], ps[:, B_H0 + t % 2, :], ACT.Gelu,
                                             bias=mqa.b1[:, t:t + 1]).then_inc(act_done, 1)

                    def silu(t):
                        act.wait_ge(up_done, 2 * t + 1)
                        if t >= 2:
                            act.wait_ge(gated, t - 1)
                        nc.scalar.activation(moe.sg[:, t % 2, :], ps[:, B_H0, :], ACT.Silu
                                             ).then_inc(act_done, 1)

                    def heads_kept(bank, bias_q, bias_k, qT, km):
                        bank_full(act, bank)
                        nc.scalar.activation(qT, MI[:, 0:SEQ], ACT.Identity, bias=bias_q)
                        for j in range(HG):
                            last = nc.scalar.activation(km[:, j, :], MI[:, SEQ:2 * SEQ], ACT.Identity,
                                                        bias=bias_k[j], scale=lane[:, j:j + 1])
                        last.then_inc(mi_free, 1)

                    if topk:
                        nc.scalar.activation(xw1[:, :], xT[:, bass.ds(seq0, SEQ)], ACT.Copy
                                             ).then_inc(xw1_ready, 1)
                        heads_kept("qk1", cols[:, 0:1], [bkm[:, j:j + 1] for j in range(HG)], qT1[:, :], km1)
                        bank_full(act, "v1")
                        nc.scalar.activation(vx1[:, :, :, 0:DH],
                                             MI[:, 0:SEQ].rearrange("p (q h d) -> p q h d", q=2, d=DH),
                                             ACT.Copy).then_inc(mi_free, 1)
                    if is_a:
                        for s in range(2):
                            heads_kept(f"qk0_{s}", 0.0, [0.0] * HG, mqa.qT[:, s, :], mqa.km[:, s])
                            bank_full(act, f"v0_{s}")
                            nc.scalar.activation(mqa.vx[:, s, :, 0:DH],
                                                 MI[:, 0:2 * DH].rearrange("p (q d) -> p q d", d=DH),
                                                 ACT.Copy).then_inc(mi_free, 1)
                    finish_qkv(act, topk, is_a)

                    n_silu = [0]
                    for r in range(ROUNDS + 1):
                        if is_a and r == ROUNDS:
                            break
                        full_lane = []
                        tile = [first[r] if r < ROUNDS else TILES1]

                        def fill():
                            if is_b and r < ROUNDS and tile[0] < first[r + 1]:
                                silu(tile[0])
                                tile[0] += 1

                        for pair, turn in sch.rounds[r]:
                            if pair is not None:
                                act_exp(act, pair)
                            for t in full_lane:
                                act_output(act, t)
                            full_lane = []
                            if is_b and r < ROUNDS:
                                fill()
                            for t in turn:
                                for b in range(2):
                                    act_empty(act, t, b)
                                    fill()
                                if t[1] % 2 == 1:
                                    full_lane.append(t)
                                    if t is not turn[-1]:
                                        act_output(act, full_lane.pop())
                        for t in full_lane:
                            act_output(act, t)
                        if is_a:
                            for t in range(first[r], first[r + 1]):
                                gelu(t)
                        if is_b and r < ROUNDS:
                            while tile[0] < first[r + 1]:
                                fill()
                        if is_m and r < ROUNDS:
                            act.wait_ge(stage_in[r % 2], 16 * (r // 2 + 1))
                            dst = moe.ghi if r < 4 else moe.uhi
                            nc.scalar.activation(dst[:, (r % 4) * 1024:(r % 4 + 1) * 1024],
                                                 moe.stage[:, r % 2, :], ACT.Copy).then_inc(kept, 1)
                    if is_a:
                        bank_full(act, "ffn")
                        nc.scalar.activation(mqa.g0[:, :, :].rearrange("p t d -> p (t d)"), MI, ACT.Silu
                                             ).then_inc(mi_free, 1)
                        act.wait_ge(aggr, CT)
                        nc.scalar.activation(mqa.std[:, :], mqa.mv[:, :, 1], ACT.Sqrt, bias=epsb[:, :]
                                             ).then_inc(std_done, 1)
                        bank_full(act, "ln")
                        nc.scalar.activation(mqa.xtn, MI, ACT.Copy).then_inc(mi_free, 1)
                        act.wait_ge(mi_free, uses.index("ln") + 1)
                        nc.scalar.activation(chunk, mqa.xtn, ACT.Copy).then_inc(xt_ready, 1)
                        act.wait_ge(lg_dif, 1)
                        nc.scalar.activation(mqa.ex[:, :, :], mqa.dif[:, :, :], ACT.Exp).then_inc(lg_exp, 1)
                        bank_full(act, "masks")
                        nc.scalar.activation(mqa.mkT, MI[0:NE1, :], ACT.Copy).then_inc(mi_free, 1)
                        act.wait_ge(mi_free, uses.index("masks") + 1)
                        nc.scalar.sem_inc(mask_t, 1)
                        for _, turn in sch.rounds[ROUNDS]:
                            for t in turn:
                                for b in range(2):
                                    act_empty(act, t, b)
                                if t[1] % 2 == 1:
                                    act_output(act, t)
                    if is_m:
                        act.wait_ge(w_in, 16)
                        act.wait_ge(acc_taken, 1)
                        for e in range(NE1):
                            w = moe.down[:, e * PER_E1:(e + 1) * PER_E1, :]
                            nc.scalar.activation(w, w, ACT.Copy, scale=moe.mean[:, e:e + 1])
                    if is_b:
                        bank_full(act, "ffn")
                        nc.scalar.activation(chunk, MI, ACT.Silu).then_inc(mi_free, 1)
                    if topk:
                        bank_full(act, "att1")
                        nc.scalar.activation(attT[:, :], MI[:, 0:SEQ], ACT.Copy).then_inc(mi_free, 1)
                        act.wait_ge(mi_free, uses.index("att1") + 1)
                        nc.scalar.sem_inc(prep, 1)
                        bank_full(act, "y1")
                        nc.scalar.activation(s_tiles(seq0),
                                             MI[:, 0:SEQ].rearrange("p (q d) -> p q d", d=D),
                                             ACT.Copy).then_inc(mi_free, 1)

                @blk.vector
                def _(dve):
                    def gated_tile(t):
                        dve.wait_ge(act_done, t + 1)
                        dve.wait_ge(up_done, 2 * t + 2)
                        if t >= 2:
                            dve.wait_ge(down_done, t - 1)
                        nc.vector.tensor_tensor(moe.h[:, t % 2, :], moe.sg[:, t % 2, :], ps[:, B_H1, :],
                                                ALU.mult).then_inc(gated, 1)

                    def heads_out(bank, dst, n):
                        o = MI.rearrange("p (j g e) -> p j g e", j=HG, g=NG)
                        bank_full(dve, bank)
                        if n:
                            dve.wait_ge(att_ready, n)
                        rc = rc1[:, :].rearrange("p (j g) -> p j g", j=HG)
                        nc.vector.reciprocal(rc, o[:, :, :, DH]).then_inc(rc_ready, 1)
                        dve.wait_ge(rc_ready, n + 1)
                        nc.vector.tensor_tensor(dst.rearrange("p (g j d) -> p j g d", g=NG, j=HG),
                                                o[:, :, :, 0:DH],
                                                rc.unsqueeze(3).broadcast_to([P, HG, NG, DH]),
                                                ALU.mult).then_inc(att_ready, 1)
                        dve.wait_ge(att_ready, n + 1)
                        nc.vector.sem_inc(mi_free, 1)

                    if is_a:
                        nc.vector.tensor_copy(mqa.xw[:, :], chunk).then_inc(xw0_ready, 1)
                    if is_a or is_b:
                        nc.vector.tensor_copy(xhi[:, :], chunk).then_inc(split, 1)
                        dve.wait_ge(split, 1)
                        nc.vector.tensor_tensor(xlo[:, :], chunk, xhi[:, :].bitcast(F32), ALU.subtract
                                                ).then_inc(split, 1)

                    def tail_of_layer0(step):
                        if step == 0:
                            for q in range(4):
                                heads_out(f"o0_{q}", mqa.att[:, q, :], q)
                            dve.wait_ge(down_done, TILES0 + 1)
                            nc.vector.tensor_tensor(mqa.fs[:, :], ACC, mqa.xw[:, :], ALU.add
                                                    ).then_inc(acc_taken, 1)
                        if step == 1:
                            dve.wait_ge(mi_free, uses.index("ffn") + 1)
                            dve.wait_ge(att_ready, 4)
                            nc.vector.tensor_tensor(mqa.g0[:, :, :], mqa.g0[:, :, :], mqa.att[:, :, :],
                                                    ALU.mult).then_inc(silu_done, 1)
                            dve.wait_ge(silu_done, 1)
                            nc.vector.tensor_tensor(mqa.x1[:, :, :], x_tiles, mqa.g0[:, :, :],
                                                    ALU.add).then_inc(resid, 1)
                            dve.wait_ge(resid, 1)
                            for t in range(CT):
                                nc.vector.bn_stats(mqa.bs[:, t, :], mqa.x1[:, t, :]).then_inc(stats, 1)
                            for t in range(CT):
                                dve.wait_ge(stats, t + 1)
                                nc.vector.bn_aggr(mqa.mv[:, t, :], mqa.bs[:, t, :]).then_inc(aggr, 1)
                        if step == 2:
                            dve.wait_ge(std_done, 1)
                            nc.vector.reciprocal(mqa.rstd[:, :], mqa.std[:, :]).then_inc(rstd_done, 1)
                            dve.wait_ge(rstd_done, 1)
                            for t in range(CT):
                                nc.vector.tensor_scalar(mqa.xn[:, t, :], mqa.x1[:, t, :],
                                                        mqa.mv[:, t, 0:1], mqa.rstd[:, t:t + 1],
                                                        ALU.subtract, ALU.mult).then_inc(xn_ready, 1)
                        if step == 3:
                            bank_full(dve, "logits")
                            nc.vector.tensor_copy(mqa.lg[:, :, 0:NE1],
                                                  MI[:, 0:CT * NE1].rearrange("p (t e) -> p t e", e=NE1)
                                                  ).then_inc(lg_ready, 1)
                            dve.wait_ge(lg_ready, 1)
                            nc.vector.sem_inc(mi_free, 1)
                            for t in range(CT):
                                nc.vector.max(mqa.l8[:, t, :], mqa.lg[:, t, :]).then_inc(lg_max, 1)
                            dve.wait_ge(lg_max, CT)
                            nc.vector.tensor_tensor(mqa.dif[:, :, :], mqa.lg[:, :, 0:NE1],
                                                    mqa.l8[:, :, 0:1].broadcast_to([P, CT, NE1]),
                                                    ALU.subtract).then_inc(lg_dif, 1)
                            nc.vector.tensor_copy(mqa.rep[:, :, 0:2], mqa.l8[:, :, 0:2]).then_inc(lg_ready, 1)
                            dve.wait_ge(lg_ready, 2)
                            for t in range(CT):
                                nc.vector.match_replace(mqa.lt[:, t, :], mqa.rep[:, t, :], mqa.lg[:, t, :],
                                                        TAKEN).then_inc(lg_taken, 1)
                            dve.wait_ge(lg_taken, CT)
                            nc.vector.tensor_scalar(mqa.mw[:, :, 0:NE1], mqa.lt[:, :, 0:NE1], IS_TAKEN, None,
                                                    ALU.is_lt).then_inc(route, 1)
                            dve.wait_ge(route, 1)
                            dve.wait_ge(lg_exp, 1)
                            nc.vector.tensor_tensor(mqa.dif[:, :, :], mqa.mw[:, :, 0:NE1], mqa.ex[:, :, :],
                                                    ALU.mult).then_inc(route, 1)
                            dve.wait_ge(route, 2)
                            nc.vector.reduce_sum(mqa.ws[:, :], mqa.dif[:, :, :], AX_X).then_inc(route, 1)
                            dve.wait_ge(route, 3)
                            nc.vector.reciprocal(mqa.rw[:, :], mqa.ws[:, :]).then_inc(route, 1)
                            dve.wait_ge(route, 4)
                            nc.vector.tensor_tensor(mqa.mw[:, :, NE1:2 * NE1], mqa.dif[:, :, :],
                                                    mqa.rw[:, :].unsqueeze(2).broadcast_to([P, CT, NE1]),
                                                    ALU.mult).then_inc(route, 1)
                            dve.wait_ge(route, 5)
                            nc.vector.tensor_tensor(racc[:, :, :], racc[:, :, :], mqa.mw[:, :, :],
                                                    ALU.add).then_inc(route, 1)

                    for r in range(ROUNDS):
                        new = [p for p, _ in sch.rounds[r] if p is not None and p[0] == 0]
                        step = 0
                        for k in range(4):
                            if topk:
                                dve_top(dve, r, k)
                            if k < len(new):
                                dve_max(dve, new[k])
                            if is_b:
                                gated_tile(first[r] + k)
                            if is_a and r == ROUNDS - 1:
                                tail_of_layer0(k)
                        if is_m and r == 0:
                            nc.vector.reduce_sum(moe.rsum[:, :], racc[:, :, :].rearrange("p t e -> p e t"),
                                                 AX_X).then_inc(route, 1)
                        if is_m and r == ROUNDS - 1:
                            bank_full(dve, "total")
                            nc.vector.tensor_copy(moe.tot[:, :], MI[:, 0:16]).then_inc(aggr, 1)
                            dve.wait_ge(aggr, 1)
                            nc.vector.sem_inc(mi_free, 1)
                            nc.vector.tensor_scalar(moe.cnt[:, :], moe.tot[:, 0:NE1], 1.0, None, ALU.max
                                                    ).then_inc(aggr, 1)
                            dve.wait_ge(aggr, 2)
                            nc.vector.reciprocal(moe.rcnt[:, :], moe.cnt[:, :]).then_inc(aggr, 1)
                            dve.wait_ge(aggr, 3)
                            nc.vector.tensor_tensor(moe.mean[:, :], moe.tot[:, NE1:2 * NE1], moe.rcnt[:, :],
                                                    ALU.mult).then_inc(acc_taken, 1)
                    if is_b:
                        dve.wait_ge(down_done, TILES1)
                        nc.vector.tensor_copy(moe.fs[:, :], ACC).then_inc(acc_taken, 1)
                    if topk:
                        n = 4 if is_a else 0
                        for q in range(2):
                            heads_out(f"o1_{q}", att1[:, q, :], n + q)

                @blk.gpsimd
                def _(pool):
                    def gate(t):
                        e = (t - T_SH) // 2
                        pool.wait_ge(act_done, t + 1)
                        pool.wait_ge(gate_in[e % 4], 16 * (e // 4 + 1))
                        h = mqa.hb[:, t % 6, :]
                        nc.gpsimd.tensor_tensor(h, h, mqa.gate[:, e % 4, :], ALU.mult).then_inc(gated, 1)

                    def mask(e):
                        if e == 0:
                            pool.wait_ge(split, 2)
                        pool.wait_ge(gate_in[e % 2], 16 * (e // 2 + 1))
                        if e >= 2:
                            pool.wait_ge(up_done, 2 * PER_E1 * (e - 1))
                        for src, dst in ((xhi, moe.xmhi), (xlo, moe.xmlo)):
                            nc.gpsimd.tensor_tensor(dst[:, e % 2, :], src[:, :].bitcast(F32),
                                                    moe.mask[:, e % 2, :], ALU.mult).then_inc(masked, 1)

                    if is_b:
                        mask(0)
                    for r in range(ROUNDS):
                        if is_b and r + 1 < NE1:
                            mask(r + 1)
                        if is_a and r == ROUNDS - 1:
                            pool.wait_ge(resid, 1)
                            nc.gpsimd.tensor_copy(x_tiles, mqa.x1[:, :, :]).then_inc(kept, 1)
                        if is_a:
                            for t in range(max(first[r], T_SH), first[r + 1]):
                                gate(t)
                        if is_m:
                            pool.wait_ge(kept, r + 1)
                            hi, lo = (moe.ghi, moe.glo) if r < 4 else (moe.uhi, moe.ulo)
                            c = slice((r % 4) * 1024, (r % 4 + 1) * 1024)
                            nc.gpsimd.tensor_tensor(lo[:, c], moe.stage[:, r % 2, :],
                                                    hi[:, c].bitcast(F32), ALU.subtract).then_inc(split, 1)
                        if topk:
                            pool_select(pool, r)

        def n_qkv(topk, is_a):
            return (1 if topk else 0) + (2 if is_a else 0)

        def finish_qkv(act, topk, is_a):
            n = (2 if topk else 0) + (4 if is_a else 0)
            if n:
                act.wait_ge(mi_free, n)
                nc.scalar.sem_inc(qkv_ready, n_qkv(topk, is_a))

        def n_l0_out(sch):
            last0 = max(n for n, p in enumerate(sch.turned) if p[0] == 0)
            return sum(1 for p in sch.turned[:last0 + 1] if p[1] % 2 == 1)

        def s_tiles(seq0):
            return sall[:, :, :].rearrange("p t d -> p (t d)")[:, bass.ds(seq0, SEQ)
                                                               ].rearrange("p (q d) -> p q d", d=D)

        class Bufs:
            pass

        phase_a = ExitStack()
        mqa = Bufs()

        def sa(name, shape, dt=F32):
            return sb(name, shape, dt, phase_a)

        mqa.w1hi = sa("w1hi", [P, TILES0 * P], F32R)
        mqa.w1lo = sa("w1lo", [P, TILES0 * P], F32R)
        mqa.w2 = sa("w2", [P, TILES0, D])
        mqa.b1 = sa("b1", [P, TILES0])
        mqa.b2 = sa("b2", [16, D])
        mqa.vx = sa("vx0", [P, 2, 2, 32])
        mqa.lg = sa("lg1", [P, CT, NE1 + 6])
        mqa.rep = sa("rep1", [P, CT, 8])

        prologue = ExitStack()

        def sp_(name, shape, dt=F32):
            return sb(name, shape, dt, prologue)

        raw = sp_("raw", [P, TILES0 * P])
        cst = sp_("cst", [P, P])
        wk8 = sp_("wk8", [P, DH])
        gw0 = sp_("gw0", [P, NE0])
        gb0 = sp_("gb0", [1, NE0])
        bs = sp_("bs", [P, NT, 6])
        mv = sp_("mv", [P, NT, 2])
        std = sp_("std", [P, NT])
        rstd = sp_("rstd", [P, NT])
        xn = sp_("xn", [P, 2, CT, D])
        lg = sp_("lg", [P, NT, NE0 + 5])
        lt = sp_("lt", [P, NT, NE0 + 5])
        l8 = sp_("l8", [P, NT, 8])
        rep = sp_("rep", [P, NT, 8])
        dif = sp_("dif", [P, NT, NE0])
        ex = sp_("ex", [P, NT, NE0])
        ws = sp_("ws", [P, NT])
        rw = sp_("rw", [P, NT])
        gates = sp_("gates", [P, NT, 16])
        gT = sp_("gT", [16, NTOK])
        XP = NT // 4
        weights = [(ident[:, :], A["ident"]), (cst[:, :], A["causal"]), (lane[:, :], A["lane"]),
                   (gw0[:, :], A["gw0"]), (gb0[:, :], A["gb0"]),
                   (wq0[:, :], A["wq0"]), (wk8[:, :], A["wk0"]), (wv0[:, :], A["wv0"]),
                   (wq1[:, :], A["wq1"]), (wk1[:, :], A["wk1"]), (wv1[:, :], A["wv1"]),
                   (wo1[:, :], A["wo1"]), (rows[:, :], A["rows1"]), (cols[:, :], A["cols1"]),
                   (rw1[:, :], A["rw1"]), (mqa.b1[:, :], A["b1"]), (mqa.b2[:, :], A["b2"])]
        x_dram = A["x"].rearrange("(t p) d -> p t d", p=P)

        with nc.Block(no_gpsimd_drain=True) as blk:
            @blk.sync
            def _(sp):
                for n in range(4):
                    sp.dma_start(xall[:, n * XP:(n + 1) * XP, :], x_dram[:, n * XP:(n + 1) * XP, :]
                                 ).then_inc(x_in[n], 16)
                sp.dma_start(raw[:, :], A["w1"]).then_inc(stage_in[0], 16)
                sp.dma_start(mqa.w2[:, :, :], A["w2"]).then_inc(stage_in[1], 16)
                sp.wait_ge(stage_in[1], 16)
                sp.wait_ge(kept, 1)
                sp.dma_start(GD[:, :], gT[:, :]).then_inc(stored, 16)
                sp.wait_ge(stored, 16)

            @blk.scalar
            def _(act):
                for dst, src in weights:
                    act.dma_start(dst, src).then_inc(w_in, 16)
                act.wait_ge(aggr, NT)
                act.wait_ge(consts, 1)
                nc.scalar.activation(std[:, :], mv[:, :, 1], ACT.Sqrt, bias=epsb[:, :]).then_inc(std_done, 1)
                for q in range(NCH):
                    act.wait_ge(mi_full, q + 1)
                    nc.scalar.activation(xT[:, q * CH:(q + 1) * CH], ps[:, q % 2, :], ACT.Copy
                                         ).then_inc(xt_ready, 1)
                act.wait_ge(stage_in[0], 16)
                nc.scalar.activation(mqa.w1hi[:, :], raw[:, :], ACT.Copy).then_inc(split, 1)
                act.wait_ge(w_in, 16 * len(weights))
                nc.scalar.activation(ident16[:, :], ident[:, :], ACT.Copy)
                nc.scalar.activation(causal16[:, :], cst[:, :], ACT.Copy)
                for h in range(NH):
                    nc.scalar.activation(wk0[:, h, :], wk8[:, :], ACT.Copy)
                nc.scalar.activation(bkm[:, :], lane[:, :], ACT.Copy, scale=cols[:, 1:2])
                act.wait_ge(lg_dif, 1)
                nc.scalar.activation(ex[:, :, :], dif[:, :, :], ACT.Exp).then_inc(lg_exp, 1)
                for n in range(8):
                    act.wait_ge(turned, n + 1)
                    last = nc.scalar.activation(gT[:, n * 512:(n + 1) * 512], ps[0:16, n, :], ACT.Copy)
                last.then_inc(kept, 1)

            @blk.gpsimd
            def _(pool):
                nc.gpsimd.memset(epsb[:, :], EPS)
                nc.gpsimd.memset(ones[:, :], 1.0).then_inc(consts, 1)
                nc.gpsimd.memset(vx1[:, :, :, :], 0.0).then_inc(prep, 1)
                nc.gpsimd.memset(mqa.vx[:, :, :, :], 0.0).then_inc(prep, 1)
                pool.wait_ge(prep, 2)
                nc.gpsimd.memset(vx1[:, :, :, DH:DH + 1], 1.0)
                nc.gpsimd.memset(mqa.vx[:, :, :, DH:DH + 1], 1.0)
                nc.gpsimd.memset(racc[:, :, :], 0.0)
                nc.gpsimd.memset(mqa.lg[:, :, :], MASKED)
                nc.gpsimd.memset(mqa.rep[:, :, :], MASKED)
                nc.gpsimd.memset(gates[:, :, 15:16], 1.0)
                nc.gpsimd.memset(rep[:, :, :], MASKED)
                nc.gpsimd.memset(lg[:, :, NE0:NE0 + 5], MASKED).then_inc(consts, 1)

            @blk.vector
            def _(dve):
                for t in range(NT):
                    if t % XP == 0:
                        dve.wait_ge(x_in[t // XP], 16)
                    nc.vector.bn_stats(bs[:, t, :], xall[:, t, :]).then_inc(stats, 1)
                for t in range(NT):
                    dve.wait_ge(stats, t + 1)
                    nc.vector.bn_aggr(mv[:, t, :], bs[:, t, :]).then_inc(aggr, 1)
                dve.wait_ge(std_done, 1)
                nc.vector.reciprocal(rstd[:, :], std[:, :]).then_inc(rstd_done, 1)
                dve.wait_ge(rstd_done, 1)
                for t in range(NT):
                    q = t // CT
                    if q >= 2 and t % CT == 0:
                        dve.wait_ge(mi_full, q - 1)
                    nc.vector.tensor_scalar(xn[:, q % 2, t % CT, :], xall[:, t, :], mv[:, t, 0:1],
                                            rstd[:, t:t + 1], ALU.subtract, ALU.mult).then_inc(xn_ready, 1)
                dve.wait_ge(split, 1)
                nc.vector.tensor_tensor(mqa.w1lo[:, :], raw[:, :], mqa.w1hi[:, :].bitcast(F32), ALU.subtract)
                dve.wait_ge(scored, 1)
                dve.wait_ge(consts, 2)
                nc.vector.tensor_copy(lg[:, :, 0:NE0],
                                      ps[:, 3, :].rearrange("p (t e) -> p t e", e=16)[:, :, 0:NE0]
                                      ).then_inc(lg_ready, 1)
                dve.wait_ge(lg_ready, 1)
                for t in range(NT):
                    nc.vector.max(l8[:, t, :], lg[:, t, :]).then_inc(lg_max, 1)
                dve.wait_ge(lg_max, NT)
                nc.vector.tensor_tensor(dif[:, :, :], lg[:, :, 0:NE0],
                                        l8[:, :, 0:1].broadcast_to([P, NT, NE0]), ALU.subtract
                                        ).then_inc(lg_dif, 1)
                nc.vector.tensor_copy(rep[:, :, 0:3], l8[:, :, 0:3]).then_inc(lg_ready, 1)
                dve.wait_ge(lg_ready, 2)
                for t in range(NT):
                    nc.vector.match_replace(lt[:, t, :], rep[:, t, :], lg[:, t, :], TAKEN).then_inc(lg_taken, 1)
                dve.wait_ge(lg_exp, 1)
                nc.vector.reduce_sum(ws[:, :], ex[:, :, :], AX_X).then_inc(route, 1)
                dve.wait_ge(route, 1)
                nc.vector.reciprocal(rw[:, :], ws[:, :]).then_inc(route, 1)
                dve.wait_ge(route, 2)
                dve.wait_ge(lg_taken, NT)
                nc.vector.scalar_tensor_tensor(out=dif[:, :, :], in0=lt[:, :, 0:NE0], scalar=IS_TAKEN,
                                               in1=ex[:, :, :], op0=ALU.is_lt, op1=ALU.mult
                                               ).then_inc(route, 1)
                dve.wait_ge(route, 3)
                nc.vector.tensor_tensor(gates[:, :, 0:NE0], dif[:, :, :],
                                        rw[:, :].unsqueeze(2).broadcast_to([P, NT, NE0]), ALU.mult
                                        ).then_inc(route, 1)

            @blk.tensor
            def _(pe):
                pe.wait_ge(w_in, 16 * len(weights))
                for q in range(NCH):
                    pe.wait_ge(xn_ready, CT * (q + 1))
                    if q >= 2:
                        pe.wait_ge(xt_ready, q - 1)
                    for t in range(CT):
                        last = nc.tensor.transpose(ps[:, q % 2, t * P:(t + 1) * P], xn[:, q % 2, t, :],
                                                   ident[:, :])
                    last.then_inc(mi_full, 1)
                pe.wait_ge(xt_ready, NCH)
                pe.wait_ge(consts, 1)
                for t in range(NT):
                    o = ps[:, 3, t * 16:t * 16 + NE0]
                    nc.tensor.matmul(o, xT[:, t * P:(t + 1) * P], gw0[:, :], start=True, stop=False)
                    last = nc.tensor.matmul(o, ones[0:1, :], gb0[0:1, :], start=False, stop=True)
                last.then_inc(scored, 1)
                pe.wait_ge(route, 4)
                pe.wait_ge(consts, 2)
                for t in range(NT):
                    last = nc.tensor.transpose(ps[0:16, t // 4, (t % 4) * P:(t % 4 + 1) * P],
                                               gates[:, t, :], ident[:, :])
                    if t % 4 == 3:
                        last.then_inc(turned, 1)
        clear_semaphores()
        prologue.close()

        mqa.xw = sa("xw0", [P, CH])
        mqa.qT = sa("qT0", [P, 2, SEQ])
        mqa.km = sa("km0", [P, 2, HG, SEQ])
        mqa.e = sa("e0", [P, 2, 2, W0])
        mqa.mx = sa("mx0", [P, 2, 4])
        mqa.nm = sa("nm0", [P, 2, 4])
        mqa.ot = sa("ot0", [P, 2, HG, SEQ])
        mqa.att = sa("att0", [P, CT, D])
        mqa.hb = sa("hb", [P, 6, CH])
        mqa.gate = sa("gate", [P, 4, CH])
        mqa.gt = sa("gt", [16, CH])
        mqa.fs = mqa.xw
        mqa.g0 = sa("g0", [P, CT, D])
        mqa.x1 = sa("x1", [P, CT, D])
        mqa.xn = mqa.g0
        mqa.xtn = mqa.att[:, :, :].rearrange("p t d -> p (t d)")
        mqa.bs = sa("bs1", [P, CT, 6])
        mqa.mv = sa("mv1", [P, CT, 2])
        mqa.std = sa("std1", [P, CT])
        mqa.rstd = sa("rstd1", [P, CT])
        mqa.l8 = sa("l81", [P, CT, 8])
        mqa.lt = sa("lt1", [P, CT, NE1 + 6])
        mqa.dif = sa("dif1", [P, CT, NE1])
        mqa.ex = sa("ex1", [P, CT, NE1])
        mqa.ws = sa("ws1", [P, CT])
        mqa.rw = sa("rwt1", [P, CT])
        mqa.mw = sa("mw1", [P, CT, 16])
        mqa.mkT = mqa.gt[0:NE1, :]

        block(0, "A", False, 0)
        clear_semaphores()
        with nc.Fori(1, NCH) as i:
            block(i, "A", True, i * SEQ - SEQ)
            clear_semaphores()
        phase_a.close()

        moe = Bufs()
        moe.ghi = sb("ghi", [P, TILES1 * P], F32R)
        moe.glo = sb("glo", [P, TILES1 * P], F32R)
        moe.uhi = sb("uhi", [P, TILES1 * P], F32R)
        moe.ulo = sb("ulo", [P, TILES1 * P], F32R)
        moe.down = sb("down", [P, TILES1, D])
        moe.rsum = sb("rsum", [P, 16])
        moe.tot = sb("tot", [P, 16])
        moe.cnt = sb("cnt", [P, NE1])
        moe.rcnt = sb("rcnt", [P, NE1])
        moe.mean = sb("mean", [P, NE1])
        with ExitStack() as mid:
            moe.stage = sb("stage", [P, 2, 1024], F32, mid)
            block(0, "M", True, (NCH - 1) * SEQ)
            clear_semaphores()
        moe.mask = sb("mask", [P, 2, CH])
        moe.xmhi = sb("xmhi", [P, 2, CH], F32R)
        moe.xmlo = sb("xmlo", [P, 2, CH], F32R)
        moe.sg = sb("sg", [P, 2, CH])
        moe.h = sb("h1", [P, 2, CH])
        moe.fs = sb("fs1", [P, CH])
        with nc.Fori(0, NCH) as i:
            block(i, "B", True, i * SEQ + NCH * SEQ)
            clear_semaphores()

        out_v = out.rearrange("(t p) d -> p t d", p=P)
        g_all = xT[:, :].rearrange("p (t d) -> p t d", d=D)
        with nc.Block(no_gpsimd_drain=True) as blk:
            @blk.vector
            def _(dve):
                for n in range(4):
                    t = slice(n * XP, (n + 1) * XP)
                    nc.vector.tensor_tensor(sall[:, t, :], sall[:, t, :], g_all[:, t, :], ALU.mult
                                            ).then_inc(silu_done, 1)
                    dve.wait_ge(silu_done, n + 1)
                    nc.vector.tensor_tensor(xall[:, t, :], xall[:, t, :], sall[:, t, :], ALU.add
                                            ).then_inc(resid, 1)

            @blk.sync
            def _(sp):
                for n in range(4):
                    t = slice(n * XP, (n + 1) * XP)
                    sp.wait_ge(resid, n + 1)
                    sp.dma_start(out_v[:, t, :], xall[:, t, :]).then_inc(stored, 16)
                sp.wait_ge(stored, 64)


def kernel(**inputs):
    import concourse.bacc as _bacc
    from concourse.bass_utils import run_bass_kernel_spmd as _run

    a = {k: np.asarray(v) for k, v in inputs.items()}
    c = np.ascontiguousarray
    key = np.arange(P)
    host = {
        "x": a["L0_attn_x"].reshape(NTOK, D),
        "ident": np.eye(P, dtype=np.float32),
        "causal": np.where(key[None, :] > key[:, None], np.float32(MASKED), np.float32(0)),
        "lane": (key[:, None] // DH % HG == np.arange(HG)[None, :]).astype(np.float32),
        "gw0": a["L0_ffn_gW"], "gb0": a["L0_ffn_gb"].reshape(1, NE0),
        "wq0": a["L0_attn_Wq"].T, "wk0": a["L0_attn_Wk"].T, "wv0": a["L0_attn_Wv"].T,
        "wq1": a["L1_attn_Wq"].T, "wk1": a["L1_attn_Wk"].T, "wv1": a["L1_attn_Wv"].T,
        "wo1": a["L1_attn_Wo"].T,
        "rows1": np.concatenate([a["L1_attn_bv"], a["L1_attn_bo"]]).reshape(1, 2 * D),
        "cols1": np.stack([a["L1_attn_bq"], a["L1_attn_bk"]], axis=1),
        "rw1": a["L1_ffn_router_w"].T,
        "b1": np.concatenate([a["L0_ffn_sb1"].reshape(-1), a["L0_ffn_rb1"].reshape(-1)]
                             ).reshape(TILES0, P).T,
        "b2": np.concatenate([a["L0_ffn_rb2"], a["L0_ffn_sb2"]], axis=0),
        "w1": np.concatenate([a["L0_ffn_sW1"].transpose(1, 0, 2).reshape(D, -1),
                              a["L0_ffn_rW1"].transpose(1, 0, 2).reshape(D, -1)], axis=1),
        "w2": np.concatenate([a["L0_ffn_sW2"].reshape(-1, D), a["L0_ffn_rW2"].reshape(-1, D)], axis=0
                             ).reshape(TILES0, P, D).transpose(1, 0, 2),
        "w_gate": a["L1_ffn_gate_w"].reshape(TILES1 * P, D).T,
        "w_up": a["L1_ffn_up_w"].reshape(TILES1 * P, D).T,
        "w_down": a["L1_ffn_down_w"].transpose(0, 2, 1).reshape(TILES1, P, D).transpose(1, 0, 2),
    }
    host = {k: c(v) for k, v in host.items()}
    nc = _bacc.Bacc("TRN2", target_bir_lowering=False, num_devices=1)
    aps, arrays = {}, {}
    for name, v in host.items():
        arrays[f"in_{name}_dram"] = v
        aps[name] = nc.dram_tensor(f"in_{name}_dram", v.shape, mybir.dt.from_np(v.dtype),
                                   kind="ExternalInput").ap()
    out = nc.dram_tensor("out_0_dram", (NTOK, D), F32, kind="ExternalOutput").ap()
    build(nc, aps, out)
    r = _run(nc, [arrays], core_ids=[0])
    return r.results[0]["out_0_dram"].reshape(NSEQ, SEQ, D)
```

```python
from contextlib import ExitStack

import numpy as np

import concourse.bass as bass
from concourse import mybir

F32 = mybir.dt.float32
F32R = mybir.dt.float32r
BF16 = mybir.dt.bfloat16
ALU = mybir.AluOpType
ACT = mybir.ActivationFunctionType
AX_X = mybir.AxisListType.X

P = 128
D = 128
NSEQ, SEQ = 16, 256
NTOK = NSEQ * SEQ
NT = NTOK // P
CH = 512
CT = CH // P
NCH = NTOK // CH
NH, DH = 16, 8
NG, HG = 4, 4
SCALE = float(DH) ** -0.5
TOPK = 32
F_SH, F_R, NE0 = 512, 256, 15
T_SH = F_SH // P
TILES0 = (F_SH + NE0 * F_R) // P
NE1, F1 = 8, 512
TILES1 = NE1 * F1 // P
PER_E1 = F1 // P
EPS = 1e-5
MASKED = -1.0e30
TAKEN = -2.0e30
IS_TAKEN = -1.5e30
NEVER = -3.0e38
ROUNDS = 8
W1C = 3 * P
W0 = 2 * SEQ


def build(nc, A, out):
    GD = nc.dram_tensor("gates_t", (16, NTOK), F32, kind="Internal").ap()
    MD = nc.dram_tensor("masks_t", (NE1, NTOK), F32, kind="Internal").ap()
    with ExitStack() as ctx:
        def sb(name, shape, dt=F32, c=ctx):
            return c.enter_context(nc.sbuf_tensor(name, shape, dt))

        ps = ctx.enter_context(nc.psum_tensor("ps", [P, 8, 512], F32))
        B_H0, B_H1, B_ACC, B_MI, B_S, B_PT, B_O = 0, 1, 2, 3, 4, 6, 7
        S1 = ps[:, B_S:B_S + 2, :]
        S0 = [ps[:, 0:2, :], ps[:, 2:4, :]]
        PT = ps[:, B_PT, :]
        OB = [ps[:, B_O, 0:SEQ], ps[:, B_O, SEQ:2 * SEQ]]
        MI = ps[:, B_MI, :]
        ACC = ps[:, B_ACC, :]

        xall = sb("xall", [P, NT, D])
        sall = sb("sall", [P, NT, D])
        xT = sb("xT", [P, NTOK])
        ident = sb("ident", [P, P])
        ident16 = sb("ident16", [P, P], BF16)
        causal16 = sb("causal16", [P, P], BF16)
        lane = sb("lane", [P, HG])
        ones = sb("ones", [P, P])
        wq0 = sb("wq0", [P, D])
        wk0 = sb("wk0", [P, NH, DH])
        wv0 = sb("wv0", [P, DH])
        wq1 = sb("wq1", [P, D])
        wk1 = sb("wk1", [P, D])
        wv1 = sb("wv1", [P, D])
        wo1 = sb("wo1", [P, D])
        rows = sb("rows", [1, 2 * D])
        cols = sb("cols", [P, 2])
        bkm = sb("bkm", [P, HG])
        rw1 = sb("rw1", [P, NE1])
        epsb = sb("epsb", [P, 1])
        racc = sb("racc", [P, CT, 16])
        xw1 = sb("xw1", [P, SEQ])
        qT1 = sb("qT1", [P, SEQ])
        km1 = sb("km1", [P, HG, SEQ])
        vx1 = sb("vx1", [P, 2, NH, 32])
        e1 = sb("e1", [P, 2, 2, W1C])
        xr = sb("xr", [P, 2, 2, W1C])
        top8 = sb("top8", [P, 2, 4, 4, 8])
        nm1 = sb("nm1", [P, 2, 4])
        pts = sb("pts", [P, 2, 2, W0])
        ot1 = sb("ot1", [P, HG, SEQ])
        att1 = sb("att1", [P, 2, D])
        attT = sb("attT", [P, SEQ])
        rc1 = sb("rc1", [P, NH])
        xhi = sb("xhi", [P, CH], F32R)
        xlo = sb("xlo", [P, CH], F32R)

        sems = {}

        def sem(name):
            sems[name] = ctx.enter_context(nc.semaphore(name))
            return sems[name]

        x_in = [sem(f"x_in{n}") for n in range(4)]
        w_in = sem("w_in")
        stage_in = [sem(f"stage_in{n}") for n in range(2)]
        gate_in = [sem(f"gate_in{n}") for n in range(4)]
        stored = sem("stored")
        xw1_ready = sem("xw1_ready")
        xw0_ready = sem("xw0_ready")
        qk1_ready = sem("qk1_ready")
        qk0_ready = sem("qk0_ready")
        v1_ready = sem("v1_ready")
        scored1 = sem("scored1")
        scored0 = sem("scored0")
        neg_max1 = sem("neg_max1")
        neg_max0 = sem("neg_max0")
        row_max = sem("row_max")
        exp1_done = sem("exp1_done")
        exp0_done = sem("exp0_done")
        top_found = sem("top_found")
        top_taken = sem("top_taken")
        is_taken = sem("is_taken")
        p_ready = sem("p_ready")
        turned = sem("turned")
        pts_ready = sem("pts_ready")
        pv_done = sem("pv_done")
        o_taken = sem("o_taken")
        mi_full = sem("mi_full")
        mi_free = sem("mi_free")
        rc_ready = sem("rc_ready")
        rc_used = sem("rc_used")
        att1_ready = sem("att1_ready")
        att0_ready = sem("att0_ready")
        split = sem("split")
        up_done = sem("up_done")
        act_done = sem("act_done")
        gated = sem("gated")
        down_done = sem("down_done")
        masked = sem("masked")
        acc_taken = sem("acc_taken")
        silu_done = sem("silu_done")
        resid = sem("resid")
        stats = sem("stats")
        aggr = sem("aggr")
        std_done = sem("std_done")
        rstd_done = sem("rstd_done")
        xn_ready = sem("xn_ready")
        xt_ready = sem("xt_ready")
        kept = sem("kept")
        lg_ready = sem("lg_ready")
        lg_max = sem("lg_max")
        lg_dif = sem("lg_dif")
        lg_exp = sem("lg_exp")
        lg_taken = sem("lg_taken")
        route = sem("route")
        mask_t = sem("mask_t")
        prep = sem("prep")
        rsum_ready = sem("rsum_ready")
        mean_ready = sem("mean_ready")
        consts = sem("consts")

        numbers = sorted(s.num for s in sems.values())
        assert numbers == list(range(numbers[0], numbers[0] + len(numbers)))

        def clear_semaphores():
            nc.multi_engine_barrier(list(nc.engines.keys()),
                                    sems_to_clear=range(numbers[0], numbers[-1] + 1))

        clear_semaphores()

        def pair_heads(n):
            j, gp = n // 2, n % 2
            return j, (2 * gp, 2 * gp + 1)

        def tiles(n, layer):
            if layer == 1:
                return [(g, c, w) for g in range(2) for c, w in ((0, P), (P, 2 * P))]
            return [(g, c, SEQ) for g in range(2) for c in (0, SEQ)]

        L0_PAIRS = 2 * ROUNDS

        def block(i, phase, cur=False, prev=None, nxt=None):
            is_a, is_b, is_m = phase == "A", phase == "B", phase == "M"
            prev_is, nxt_is = prev is not None, nxt is not None
            tok0 = i * CH
            chunk = xT[:, bass.ds(tok0, CH)]
            x_tiles = xall[:, bass.ds(i * CT, CT), :]
            if is_a:
                n_steps = [9, 9, 8, 8, 6, 5, 5, 0]
                is_f = [r < 4 for r in range(ROUNDS)]
            else:
                n_steps = [4] * ROUNDS
                is_f = [False] * ROUNDS
            n_rounds = 0 if phase == "E" else ROUNDS

            def steps_of(r):
                base = 0 if (is_a and r == 4) else sum(n_steps[(4 if is_a and r > 4 else 0):r])
                return list(enumerate(range(base, base + n_steps[r])))

            order = [(1, -1)] if prev_is else []
            for r in range(n_rounds):
                if is_a and not is_f[r]:
                    for k, u in steps_of(r):
                        order += [(0, u - 1)] if u else []
                        order += [(1, r - 1)] if k == 1 and cur else []
                    if r == ROUNDS - 1:
                        order += [(0, L0_PAIRS - 1)] + ([(1, r - 1)] if cur else [])
                elif cur and r:
                    order += [(1, r - 1)]

            def odd_before(pair):
                return sum(1 for q in order[:order.index(pair)] if q[1] % 2 == 1)

            placed = {}
            if is_a:
                if cur:
                    placed[0, 4] = "v1"
                for n, name in enumerate(("qk0_0", "v0_0", "qk0_1", "v0_1")):
                    placed[(0, 5 + n) if n < 4 else (1, n - 4)] = name
                if prev_is:
                    for n, name in enumerate(("o1_0", "o1_1", "att1", "y1")):
                        placed[1, 4 + n] = name
            elif cur or prev_is:
                if cur:
                    placed[0, 3] = "v1"
                if prev_is:
                    for n, name in enumerate(("o1_0", "o1_1", "att1", "y1")):
                        placed[1, n] = name
            uses = [placed[k] for k in sorted(placed)]
            if is_a:
                uses += ["ffn", "o0_0", "o0_1", "o0_2", "o0_3"]
                uses += ["qkn"] if cur and nxt_is else []
                uses += ["ln", "logits", "masks"]
                uses += ["qkn"] if not cur and nxt_is else []
            else:
                if is_m:
                    uses += ["total"]
                uses += ["qkn"] if nxt_is else []
                if is_b:
                    uses += ["ffn"]

            def bank_mine(pe, name):
                if uses.index(name):
                    pe.wait_ge(mi_free, uses.index(name))

            def bank_full(eng, name):
                eng.wait_ge(mi_full, uses.index(name) + 1)

            with nc.Block(no_gpsimd_drain=True) as blk:

                @blk.sync
                def _(sp):
                    if is_a:
                        for e in range(NE0):
                            if e >= 4:
                                sp.wait_ge(gated, 2 * (e - 4) + 2)
                            sp.dma_start(mqa.gate[:, e % 4, :],
                                         GD[e:e + 1, bass.ds(tok0, CH)].broadcast_to([P, CH])
                                         ).then_inc(gate_in[e % 4], 16)
                            if e == 3:
                                sp.dma_start(mqa.gt[:, :], GD[:, bass.ds(tok0, CH)]).then_inc(w_in, 16)
                        sp.wait_ge(mask_t, 1)
                        sp.dma_start(MD[:, bass.ds(tok0, CH)], mqa.mkT).then_inc(stored, 16)
                        sp.wait_ge(stored, 16)
                    if is_b:
                        for e in range(NE1):
                            if e >= 2:
                                sp.wait_ge(masked, 2 * (e - 2) + 2)
                            sp.dma_start(moe.mask[:, e % 2, :],
                                         MD[e:e + 1, bass.ds(tok0, CH)].broadcast_to([P, CH])
                                         ).then_inc(gate_in[e % 2], 16)
                    if is_m:
                        sp.dma_start(moe.down[:, :, :], A["w_down"]).then_inc(w_in, 16)
                        for n in range(8):
                            if n >= 2:
                                sp.wait_ge(split, n - 1)
                            src = A["w_gate" if n < 4 else "w_up"][:, (n % 4) * 1024:(n % 4 + 1) * 1024]
                            sp.dma_start(moe.stage[:, n % 2, :], src).then_inc(stage_in[n % 2], 16)

                @blk.tensor
                def _(pe):
                    def up(t):
                        if t >= 2:
                            pe.wait_ge(act_done, t - 1)
                        if t == 0:
                            pe.wait_ge(split, 2)
                        f = slice(t * P, (t + 1) * P)
                        o = ps[:, B_H0 + t % 2, :]
                        nc.tensor.matmul(o, mqa.w1hi[:, f], xhi[:, :], start=True, stop=False)
                        nc.tensor.matmul(o, mqa.w1lo[:, f], xhi[:, :], start=False, stop=False)
                        nc.tensor.matmul(o, mqa.w1hi[:, f], xlo[:, :], start=False, stop=True
                                         ).then_inc(up_done, 1)

                    def down(t):
                        if t < T_SH:
                            pe.wait_ge(act_done, t + 1)
                        else:
                            pe.wait_ge(gated, t - T_SH + 1)
                        nc.tensor.matmul(ACC, mqa.w2[:, t, :], mqa.hb[:, t % 6, :], start=(t == 0),
                                         stop=False).then_inc(down_done, 1)

                    def gate1(t):
                        f = slice(t * P, (t + 1) * P)
                        if t:
                            pe.wait_ge(act_done, t)
                        else:
                            pe.wait_ge(split, 2)
                        o = ps[:, B_H0, :]
                        nc.tensor.matmul(o, moe.ghi[:, f], xhi[:, :], start=True, stop=False)
                        nc.tensor.matmul(o, moe.glo[:, f], xhi[:, :], start=False, stop=False)
                        nc.tensor.matmul(o, moe.ghi[:, f], xlo[:, :], start=False, stop=True
                                         ).then_inc(up_done, 1)

                    def up1(t):
                        f = slice(t * P, (t + 1) * P)
                        e = t // PER_E1
                        if t:
                            pe.wait_ge(gated, t)
                        if t % PER_E1 == 0:
                            pe.wait_ge(masked, 2 * e + 2)
                        o = ps[:, B_H1, :]
                        mhi, mlo = moe.xmhi[:, e % 2, :], moe.xmlo[:, e % 2, :]
                        nc.tensor.matmul(o, moe.uhi[:, f], mhi, start=True, stop=False)
                        nc.tensor.matmul(o, moe.ulo[:, f], mhi, start=False, stop=False)
                        nc.tensor.matmul(o, moe.uhi[:, f], mlo, start=False, stop=True
                                         ).then_inc(up_done, 1)

                    def down1(t):
                        pe.wait_ge(gated, t + 1)
                        nc.tensor.matmul(ACC, moe.down[:, t, :], moe.h[:, t % 2, :], start=(t == 0),
                                         stop=(t == TILES1 - 1)).then_inc(down_done, 1)

                    def scores1(n):
                        if cur:
                            pe.wait_ge(exp1_done, n)
                        j, groups = pair_heads(n % ROUNDS)
                        for b in range(2):
                            o = S1[:, b, 0:W1C].rearrange("p (a k) -> p a k", k=P)[:, 0:3:2, :]
                            nc.tensor.matmul(o, ident16[:, :],
                                             causal16[:, :].unsqueeze(1).broadcast_to([P, 2, P]),
                                             start=True, stop=True)
                        for c0, w, q0 in ((0, P, 0), (P, 2 * P, P)):
                            for b, g in enumerate(groups):
                                last = nc.tensor.matmul(S1[:, b, c0:c0 + w],
                                                        qT1[32 * g:32 * g + 32, q0:q0 + P],
                                                        km1[32 * g:32 * g + 32, j, 0:w],
                                                        start=False, stop=True, skip_group_check=True)
                        last.then_inc(scored1, 1)

                    def scores0(u):
                        if u >= 2:
                            pe.wait_ge(exp0_done, u - 1)
                        j, groups = pair_heads(u % ROUNDS)
                        s = u // ROUNDS
                        for q in range(2):
                            for b, g in enumerate(groups):
                                last = nc.tensor.matmul(S0[u % 2][:, b, q * SEQ:(q + 1) * SEQ],
                                                        mqa.qT[32 * g:32 * g + 32, s, q * P:(q + 1) * P],
                                                        mqa.km[32 * g:32 * g + 32, s, j, :],
                                                        start=True, stop=True)
                        last.then_inc(scored0, 1)

                    def turn(pair, b):
                        layer, n = pair
                        k = order.index(pair)
                        if 2 * k + b:
                            pe.wait_ge(pts_ready, 2 * k + b)
                        if layer == 1:
                            if n >= 0:
                                pe.wait_ge(p_ready, n + 1)
                            src, blocks = e1[:, n % 2, b, :], (0, P, 2 * P)
                        else:
                            pe.wait_ge(exp0_done, n + 1)
                            src, blocks = mqa.e[:, n % 2, b, :], (0, SEQ, P, SEQ + P)
                        for m, c in enumerate(blocks):
                            last = nc.tensor.transpose(PT[:, m * P:(m + 1) * P], src[:, c:c + P], ident[:, :])
                        last.then_inc(turned, 1)

                    def values(pair):
                        layer, n = pair
                        k = order.index(pair)
                        j, groups = pair_heads(n % ROUNDS)
                        pe.wait_ge(pts_ready, 2 * k + 2)
                        if odd_before(pair):
                            pe.wait_ge(o_taken, odd_before(pair))
                        if pair == (1, 0):
                            pe.wait_ge(v1_ready, 1)
                        for kt in range(2):
                            for b, g in enumerate(groups):
                                o = OB[layer][32 * g:32 * g + 32, :]
                                p = pts[:, k % 2, b, :]
                                if layer == 1:
                                    h = HG * g + j
                                    if kt == 0:
                                        last = nc.tensor.matmul(o, vx1[:, 0, h, :], p[:, 0:SEQ],
                                                                start=True, stop=True)
                                    else:
                                        last = nc.tensor.matmul(o[:, P:SEQ], vx1[:, 1, h, :], p[:, SEQ:W1C],
                                                                start=False, stop=True, skip_group_check=True)
                                else:
                                    last = nc.tensor.matmul(o, mqa.vx[:, n // ROUNDS, kt, :],
                                                            p[:, kt * SEQ:(kt + 1) * SEQ],
                                                            start=(kt == 0), stop=(kt == 1))
                        last.then_inc(pv_done, 1)

                    def tiles_turned(src):
                        for t in range(CT):
                            last = nc.tensor.transpose(MI[:, t * P:(t + 1) * P], src(t), ident[:, :])
                        last.then_inc(mi_full, 1)

                    def shared(name):
                        bank_mine(pe, name)
                        if name == "qkn":
                            pe.wait_ge(xw1_ready, 1)
                            nc.tensor.matmul(MI[:, 0:SEQ], wq1[:, :], xw1[:, :], start=True, stop=True)
                            nc.tensor.matmul(MI[:, SEQ:2 * SEQ], wk1[:, :], xw1[:, :], start=True,
                                             stop=True).then_inc(mi_full, 1)
                        elif name == "v1":
                            for q in range(2):
                                o = MI[:, q * P:(q + 1) * P]
                                nc.tensor.matmul(o, xw1[:, q * P:(q + 1) * P], wv1[:, :], start=True,
                                                 stop=False)
                                last = nc.tensor.matmul(o, ones[0:1, :], rows[0:1, 0:D], start=False, stop=True)
                            last.then_inc(mi_full, 1)
                        elif name[:3] == "qk0":
                            s = int(name[-1])
                            if s == 0:
                                pe.wait_ge(xw0_ready, 1)
                            xs = mqa.xw[:, s * SEQ:(s + 1) * SEQ]
                            nc.tensor.matmul(MI[:, 0:SEQ], wq0[:, :], xs, start=True, stop=True)
                            nc.tensor.matmul(MI[:, SEQ:2 * SEQ], wk0[:, :, :].rearrange("p h d -> p (h d)"),
                                             xs, start=True, stop=True).then_inc(mi_full, 1)
                        elif name[:2] == "v0":
                            s = int(name[-1])
                            for q in range(2):
                                last = nc.tensor.matmul(MI[:, q * DH:(q + 1) * DH],
                                                        mqa.xw[:, s * SEQ + q * P:s * SEQ + (q + 1) * P],
                                                        wv0[:, :], start=True, stop=True)
                            last.then_inc(mi_full, 1)
                        elif name[:2] in ("o0", "o1"):
                            q = int(name[-1])
                            if name == "o1_0":
                                pe.wait_ge(o_taken, 1)
                            if name == "o0_0":
                                pe.wait_ge(o_taken, odd_before((0, L0_PAIRS - 1)) + 1)
                                pe.wait_ge(exp0_done, L0_PAIRS)
                            ot = ot1 if name[1] == "1" else mqa.ot[:, q // 2]
                            q = q % 2
                            tiles_turned(lambda j: ot[:, j, q * P:(q + 1) * P])
                        elif name == "att1":
                            pe.wait_ge(att1_ready, 2)
                            for q in range(2):
                                last = nc.tensor.transpose(MI[:, q * P:(q + 1) * P], att1[:, q, :],
                                                           ident[:, :])
                            last.then_inc(mi_full, 1)
                        elif name == "y1":
                            for q in range(2):
                                o = MI[:, q * P:(q + 1) * P]
                                nc.tensor.matmul(o, attT[:, q * P:(q + 1) * P], wo1[:, :], start=True,
                                                 stop=False)
                                last = nc.tensor.matmul(o, ones[0:1, :], rows[0:1, D:2 * D], start=False,
                                                        stop=True)
                            last.then_inc(mi_full, 1)
                        elif name == "ffn":
                            pe.wait_ge(acc_taken, 1)
                            fs = mqa.fs if is_a else moe.fs
                            tiles_turned(lambda t: fs[:, t * P:(t + 1) * P])
                        elif name == "ln":
                            pe.wait_ge(xn_ready, CT)
                            tiles_turned(lambda t: mqa.xn[:, t, :])
                        elif name == "logits":
                            for t in range(CT):
                                last = nc.tensor.matmul(MI[:, t * NE1:(t + 1) * NE1],
                                                        mqa.xtn[:, t * P:(t + 1) * P], rw1[:, :],
                                                        start=True, stop=True)
                            last.then_inc(mi_full, 1)
                        elif name == "masks":
                            pe.wait_ge(route, 1)
                            for t in range(CT):
                                last = nc.tensor.transpose(MI[0:NE1, t * P:(t + 1) * P],
                                                           mqa.mw[:, t, 0:NE1], ident[:, :])
                            last.then_inc(mi_full, 1)
                        elif name == "total":
                            pe.wait_ge(rsum_ready, 1)
                            nc.tensor.matmul(MI[:, 0:16], ones[:, :], moe.rsum[:, :], start=True, stop=True
                                             ).then_inc(mi_full, 1)

                    def begin_next():
                        pe.wait_ge(qk1_ready, 1)
                        scores1(ROUNDS)

                    for r in range(n_rounds):
                        last_turned = ((1, r - 1) if cur and r else None) or (
                            (1, -1) if prev_is and r == 0 else None)
                        if is_f[r]:
                            for k, t in steps_of(r):
                                up(t)
                                if t >= 4:
                                    down(t - 4)
                                if last_turned and k in (1, 2):
                                    turn(last_turned, k - 1)
                                if last_turned and k == 3:
                                    values(last_turned)
                                if cur and k == 5:
                                    scores1(r + 1)
                                if (r, k) in placed:
                                    shared(placed[r, k])
                        elif is_a:
                            if r == 4:
                                for t in range(TILES0 - 4, TILES0):
                                    down(t)
                                pe.wait_ge(w_in, 16)
                                nc.tensor.matmul(ACC, mqa.b2[:, :], mqa.gt[:, :], start=False, stop=True
                                                 ).then_inc(down_done, 1)
                                pe.wait_ge(act_done, TILES0)
                                pe.wait_ge(qk0_ready, 1)
                                scores0(0)
                                shared("ffn")
                                pending = None
                            for k, u in steps_of(r):
                                if u:
                                    turn((0, u - 1), 0)
                                if u == 0:
                                    pe.wait_ge(mi_free, uses.index("ffn") + 1)
                                if u + 1 < L0_PAIRS:
                                    scores0(u + 1)
                                if u:
                                    turn((0, u - 1), 1)
                                    if pending:
                                        values(pending)
                                    pending = (0, u - 1)
                                if cur and k == 1:
                                    turn((1, r - 1), 0)
                                    scores1(r + 1)
                                    turn((1, r - 1), 1)
                                    values(pending)
                                    pending = (1, r - 1)
                            if r == ROUNDS - 1:
                                final = (0, L0_PAIRS - 1)
                                turn(final, 0)
                                values(pending)
                                turn(final, 1)
                                values(final)
                                if cur:
                                    turn((1, r - 1), 0)
                                for q in range(4):
                                    shared(f"o0_{q}")
                                    if cur and q == 1:
                                        turn((1, r - 1), 1)
                                if cur:
                                    values((1, r - 1))
                                if cur and nxt_is:
                                    shared("qkn")
                                    begin_next()
                                for name in ("ln", "logits", "masks"):
                                    shared(name)
                                if not cur and nxt_is:
                                    shared("qkn")
                                    begin_next()
                        else:
                            for k, t in steps_of(r):
                                if is_b:
                                    gate1(t)
                                if last_turned and k < 2:
                                    turn(last_turned, k)
                                if is_b:
                                    up1(t)
                                    if t:
                                        down1(t - 1)
                                if last_turned and k == 2:
                                    values(last_turned)
                                if cur and k == 2 and r < ROUNDS - 1:
                                    scores1(r + 1)
                                if (r, k) in placed:
                                    shared(placed[r, k])
                                if is_m and (r, k) == (3, 0):
                                    shared("total")
                                if nxt_is and (r, k) == (ROUNDS - 1, 0):
                                    shared("qkn")
                                if nxt_is and (r, k) == (ROUNDS - 1, 2):
                                    begin_next()
                    if is_b:
                        down1(TILES1 - 1)
                        shared("ffn")
                    if phase == "E":
                        turn((1, -1), 0)
                        turn((1, -1), 1)
                        values((1, -1))
                        for name in uses:
                            shared(name)

                @blk.scalar
                def _(act):
                    def gelu(t):
                        act.wait_ge(up_done, t + 1)
                        if t >= 6:
                            act.wait_ge(down_done, t - 5)
                        nc.scalar.activation(mqa.hb[:, t % 6, :], ps[:, B_H0 + t % 2, :], ACT.Gelu,
                                             bias=mqa.b1[:, t:t + 1]).then_inc(act_done, 1)

                    def silu(t):
                        act.wait_ge(up_done, 2 * t + 1)
                        if t >= 2:
                            act.wait_ge(gated, t - 1)
                        nc.scalar.activation(moe.sg[:, t % 2, :], ps[:, B_H0, :], ACT.Silu
                                             ).then_inc(act_done, 1)

                    def exp1(n):
                        act.wait_ge(neg_max1, n + 1)
                        act.wait_ge(top_taken, 16 * n + 4)
                        if n >= 2:
                            act.wait_ge(turned, 2 * order.index((1, n - 2)) + 2)
                        elif n == 1 and prev_is:
                            act.wait_ge(turned, 2)
                        for m, (b, c, w) in enumerate(tiles(n, 1)):
                            last = nc.scalar.activation(e1[:, n % 2, b, c:c + w], S1[:, b, c:c + w], ACT.Exp,
                                                        bias=nm1[:, n % 2, m:m + 1], scale=SCALE)
                        last.then_inc(exp1_done, 1)

                    def exp0(u):
                        act.wait_ge(neg_max0, u + 1)
                        if u >= 2:
                            act.wait_ge(turned, 2 * order.index((0, u - 2)) + 2)
                        for m, (b, c, w) in enumerate(tiles(u, 0)):
                            last = nc.scalar.activation(mqa.e[:, u % 2, b, c:c + w],
                                                        S0[u % 2][:, b, c:c + w], ACT.Exp,
                                                        bias=mqa.nm[:, u % 2, m:m + 1], scale=SCALE)
                        last.then_inc(exp0_done, 1)

                    def empty(pair, b):
                        k = order.index(pair)
                        w = W1C if pair[0] == 1 else W0
                        act.wait_ge(turned, 2 * k + b + 1)
                        if k >= 2:
                            act.wait_ge(pv_done, k - 1)
                        nc.scalar.activation(pts[:, k % 2, b, 0:w], PT[:, 0:w], ACT.Copy
                                             ).then_inc(pts_ready, 1)

                    def output(pair):
                        layer, n = pair
                        if n % 2 == 0:
                            return
                        act.wait_ge(pv_done, order.index(pair) + 1)
                        j = (n % ROUNDS) // 2
                        if layer == 1 and n == 1 and prev_is:
                            act.wait_ge(mi_full, uses.index("o1_1") + 1)
                        dst = ot1[:, j, :] if layer == 1 else mqa.ot[:, n // ROUNDS, j, :]
                        nc.scalar.activation(dst, OB[layer], ACT.Copy).then_inc(o_taken, 1)

                    def heads(name, bias_q, bias_k, qT, km, ready):
                        bank_full(act, name)
                        nc.scalar.activation(qT, MI[:, 0:SEQ], ACT.Identity, bias=bias_q)
                        for j in range(HG):
                            last = nc.scalar.activation(km[:, j, :], MI[:, SEQ:2 * SEQ], ACT.Identity,
                                                        bias=bias_k[j], scale=lane[:, j:j + 1])
                        last.then_inc(mi_free, 1)
                        act.wait_ge(mi_free, uses.index(name) + 1)
                        nc.scalar.sem_inc(ready, 1)

                    def tokens_next():
                        if is_a and not cur:
                            act.wait_ge(kept, 1)
                        nc.scalar.activation(xw1[:, :], xT[:, bass.ds(nxt, SEQ)], ACT.Copy
                                             ).then_inc(xw1_ready, 1)

                    def shared(name):
                        if name == "qkn":
                            if cur:
                                act.wait_ge(scored1, ROUNDS - 1)
                            heads(name, cols[:, 0:1], [bkm[:, j:j + 1] for j in range(HG)], qT1[:, :], km1,
                                  qk1_ready)
                        elif name == "v1":
                            bank_full(act, name)
                            if prev_is:
                                act.wait_ge(pv_done, 1)
                            nc.scalar.activation(vx1[:, :, :, 0:DH],
                                                 MI[:, 0:SEQ].rearrange("p (q h d) -> p q h d", q=2, d=DH),
                                                 ACT.Copy).then_inc(mi_free, 1)
                            act.wait_ge(mi_free, uses.index(name) + 1)
                            nc.scalar.sem_inc(v1_ready, 1)
                        elif name[:3] == "qk0":
                            s = int(name[-1])
                            heads(name, 0.0, [0.0] * HG, mqa.qT[:, s, :], mqa.km[:, s], qk0_ready)
                        elif name[:2] == "v0":
                            bank_full(act, name)
                            nc.scalar.activation(mqa.vx[:, int(name[-1]), :, 0:DH],
                                                 MI[:, 0:2 * DH].rearrange("p (q d) -> p q d", d=DH),
                                                 ACT.Copy).then_inc(mi_free, 1)
                        elif name == "att1":
                            bank_full(act, name)
                            nc.scalar.activation(attT[:, :], MI[:, 0:SEQ], ACT.Copy).then_inc(mi_free, 1)
                        elif name == "y1":
                            bank_full(act, name)
                            nc.scalar.activation(s_tiles(prev), MI[:, 0:SEQ].rearrange("p (q d) -> p q d", d=D),
                                                 ACT.Copy).then_inc(mi_free, 1)
                        elif name == "ffn":
                            bank_full(act, name)
                            dst = mqa.g0[:, :, :].rearrange("p t d -> p (t d)") if is_a else chunk
                            nc.scalar.activation(dst, MI, ACT.Silu).then_inc(mi_free, 1)

                    for r in range(n_rounds):
                        last_turned = ((1, r - 1) if cur and r else None) or (
                            (1, -1) if prev_is and r == 0 else None)
                        if is_f[r]:
                            if cur:
                                exp1(r)
                            for k, t in steps_of(r):
                                gelu(t)
                                if last_turned and k in (1, 2):
                                    empty(last_turned, k - 1)
                                if last_turned and k == 4:
                                    output(last_turned)
                                if (r, k) in placed:
                                    shared(placed[r, k])
                        elif is_a:
                            if r == 4:
                                shared("ffn")
                                exp0(0)
                                pending = None
                            for k, u in steps_of(r):
                                if u:
                                    empty((0, u - 1), 0)
                                    empty((0, u - 1), 1)
                                    if pending:
                                        output(pending)
                                    pending = (0, u - 1)
                                if u + 1 < L0_PAIRS:
                                    exp0(u + 1)
                                if cur and k == 0:
                                    exp1(r)
                                if cur and k == 1:
                                    empty((1, r - 1), 0)
                                    empty((1, r - 1), 1)
                                    output(pending)
                                    pending = (1, r - 1)
                            if r == ROUNDS - 1:
                                final = (0, L0_PAIRS - 1)
                                empty(final, 0)
                                output(pending)
                                empty(final, 1)
                                output(final)
                                if cur:
                                    exp1(r)
                                    empty((1, r - 1), 0)
                                    empty((1, r - 1), 1)
                                    if nxt_is:
                                        tokens_next()
                                        shared("qkn")
                                act.wait_ge(aggr, CT)
                                nc.scalar.activation(mqa.std[:, :], mqa.mv[:, :, 1], ACT.Sqrt,
                                                     bias=epsb[:, :]).then_inc(std_done, 1)
                                bank_full(act, "ln")
                                nc.scalar.activation(mqa.xtn, MI, ACT.Copy).then_inc(mi_free, 1)
                                act.wait_ge(mi_free, uses.index("ln") + 1)
                                nc.scalar.activation(chunk, mqa.xtn, ACT.Copy).then_inc(kept, 1)
                                act.wait_ge(lg_dif, 1)
                                nc.scalar.activation(mqa.ex[:, :, :], mqa.dif[:, :, :], ACT.Exp
                                                     ).then_inc(lg_exp, 1)
                                bank_full(act, "masks")
                                nc.scalar.activation(mqa.mkT, MI[0:NE1, :], ACT.Copy).then_inc(mi_free, 1)
                                act.wait_ge(mi_free, uses.index("masks") + 1)
                                nc.scalar.sem_inc(mask_t, 1)
                                if not cur and nxt_is:
                                    tokens_next()
                                    shared("qkn")
                        else:
                            if cur:
                                exp1(r)
                            if nxt_is and r == ROUNDS - 1:
                                tokens_next()
                            for k, t in steps_of(r):
                                if is_b:
                                    silu(t)
                                if last_turned and k < 2:
                                    empty(last_turned, k)
                                if last_turned and k == 3:
                                    output(last_turned)
                                if (r, k) in placed:
                                    shared(placed[r, k])
                                if nxt_is and (r, k) == (ROUNDS - 1, 0):
                                    shared("qkn")
                            if is_m:
                                act.wait_ge(stage_in[r % 2], 16 * (r // 2 + 1))
                                dst = moe.ghi if r < 4 else moe.uhi
                                nc.scalar.activation(dst[:, (r % 4) * 1024:(r % 4 + 1) * 1024],
                                                     moe.stage[:, r % 2, :], ACT.Copy).then_inc(kept, 1)
                    if is_m:
                        act.wait_ge(w_in, 16)
                        act.wait_ge(mean_ready, 4)
                        for e in range(NE1):
                            w = moe.down[:, e * PER_E1:(e + 1) * PER_E1, :]
                            nc.scalar.activation(w, w, ACT.Copy, scale=moe.mean[:, e:e + 1])
                    if is_b:
                        shared("ffn")
                    if phase == "E":
                        empty((1, -1), 0)
                        empty((1, -1), 1)
                        output((1, -1))
                        for name in uses:
                            shared(name)

                @blk.vector
                def _(dve):
                    def gated_tile(t):
                        dve.wait_ge(act_done, t + 1)
                        dve.wait_ge(up_done, 2 * t + 2)
                        if t >= 2:
                            dve.wait_ge(down_done, t - 1)
                        nc.vector.tensor_tensor(moe.h[:, t % 2, :], moe.sg[:, t % 2, :], ps[:, B_H1, :],
                                                ALU.mult).then_inc(gated, 1)

                    def max0(u):
                        dve.wait_ge(scored0, u + 1)
                        nc.vector.reduce_max(mqa.mx[:, u % 2, :],
                                             S0[u % 2].rearrange("p b (q k) -> p (b q) k", k=SEQ), AX_X
                                             ).then_inc(row_max, 1)
                        dve.wait_ge(row_max, u + 1)
                        nc.vector.tensor_scalar(mqa.nm[:, u % 2, :], mqa.mx[:, u % 2, :], -SCALE, None,
                                                ALU.mult).then_inc(neg_max0, 1)

                    def search(n, piece):
                        if not cur:
                            return
                        k = piece // 2
                        found = 16 * n + 4 * k
                        if piece == 0 and n:
                            dve.wait_ge(scored1, n)
                            if n >= 2:
                                dve.wait_ge(p_ready, n - 1)
                        for m, (b, c, w) in enumerate(tiles(n, 1)):
                            src = S1[:, b, c:c + w] if k == 0 else xr[:, n % 2, b, c:c + w]
                            if piece % 2 == 0:
                                if k:
                                    dve.wait_ge(top_taken, found - 4 + m + 1)
                                nc.vector.max(top8[:, n % 2, k, m, :], src).then_inc(top_found, 1)
                            else:
                                dve.wait_ge(top_found, found + m + 1)
                                nc.vector.match_replace(xr[:, n % 2, b, c:c + w], top8[:, n % 2, k, m, :],
                                                        src, TAKEN).then_inc(top_taken, 1)
                        if piece == 0:
                            dve.wait_ge(top_found, found + 4)
                            nc.vector.tensor_scalar(nm1[:, n % 2, :], top8[:, n % 2, 0, :, 0], -SCALE, None,
                                                    ALU.mult).then_inc(neg_max1, 1)
                        if piece == 7 and (is_a or n == ROUNDS - 1):
                            dve.wait_ge(top_taken, 16 * n + 16)
                            dve.wait_ge(exp1_done, n + 1)
                            last = nc.vector.scalar_tensor_tensor(out=e1[:, n % 2], in0=xr[:, n % 2],
                                                                  scalar=IS_TAKEN, in1=e1[:, n % 2],
                                                                  op0=ALU.is_lt, op1=ALU.mult)
                            if n < ROUNDS - 1:
                                last.then_inc(p_ready, 1)

                    def heads_out(name, dst, done, att_ready):
                        o = MI.rearrange("p (j g e) -> p j g e", j=HG, g=NG)
                        n = int(name[-1])
                        bank_full(dve, name)
                        if done:
                            dve.wait_ge(rc_used, done)
                        rc = rc1[:, :].rearrange("p (j g) -> p j g", j=HG)
                        nc.vector.reciprocal(rc, o[:, :, :, DH]).then_inc(rc_ready, 1)
                        dve.wait_ge(rc_ready, done + 1)
                        nc.vector.tensor_tensor(dst.rearrange("p (g j d) -> p j g d", g=NG, j=HG),
                                                o[:, :, :, 0:DH],
                                                rc.unsqueeze(3).broadcast_to([P, HG, NG, DH]),
                                                ALU.mult).then_inc(att_ready, 1)
                        dve.wait_ge(att_ready, n + 1)
                        nc.vector.sem_inc(rc_used, 1)
                        nc.vector.sem_inc(mi_free, 1)

                    n_prev = 2 if prev_is else 0

                    def shared(name):
                        if name[:2] == "o1":
                            q = int(name[-1])
                            heads_out(name, att1[:, q, :], q, att1_ready)

                    def tail_of_layer0(piece):
                        if piece in (1, 2):
                            for q in (2 * piece - 2, 2 * piece - 1):
                                heads_out(f"o0_{q}", mqa.att[:, q, :], n_prev + q, att0_ready)
                        if piece == 3:
                            dve.wait_ge(att0_ready, 4)
                            nc.vector.tensor_tensor(mqa.g0[:, :, :], mqa.g0[:, :, :], mqa.att[:, :, :],
                                                    ALU.mult).then_inc(silu_done, 1)
                            dve.wait_ge(silu_done, 1)
                            nc.vector.tensor_tensor(mqa.x1[:, :, :], x_tiles, mqa.g0[:, :, :],
                                                    ALU.add).then_inc(resid, 1)
                            dve.wait_ge(resid, 1)
                            for t in range(CT):
                                nc.vector.bn_stats(mqa.bs[:, t, :], mqa.x1[:, t, :]).then_inc(stats, 1)
                            for t in range(CT):
                                dve.wait_ge(stats, t + 1)
                                nc.vector.bn_aggr(mqa.mv[:, t, :], mqa.bs[:, t, :]).then_inc(aggr, 1)
                        if piece == 5:
                            dve.wait_ge(std_done, 1)
                            nc.vector.reciprocal(mqa.rstd[:, :], mqa.std[:, :]).then_inc(rstd_done, 1)
                            dve.wait_ge(rstd_done, 1)
                            for t in range(CT):
                                nc.vector.tensor_scalar(mqa.xn[:, t, :], mqa.x1[:, t, :],
                                                        mqa.mv[:, t, 0:1], mqa.rstd[:, t:t + 1],
                                                        ALU.subtract, ALU.mult).then_inc(xn_ready, 1)
                        if piece == 7:
                            bank_full(dve, "logits")
                            nc.vector.tensor_copy(mqa.lg[:, :, 0:NE1],
                                                  MI[:, 0:CT * NE1].rearrange("p (t e) -> p t e", e=NE1)
                                                  ).then_inc(lg_ready, 1)
                            dve.wait_ge(lg_ready, 1)
                            nc.vector.sem_inc(mi_free, 1)
                            for t in range(CT):
                                nc.vector.max(mqa.l8[:, t, :], mqa.lg[:, t, :]).then_inc(lg_max, 1)
                            dve.wait_ge(lg_max, CT)
                            nc.vector.tensor_tensor(mqa.dif[:, :, :], mqa.lg[:, :, 0:NE1],
                                                    mqa.l8[:, :, 0:1].broadcast_to([P, CT, NE1]),
                                                    ALU.subtract).then_inc(lg_dif, 1)
                            nc.vector.tensor_copy(mqa.rep[:, :, 0:2], mqa.l8[:, :, 0:2]).then_inc(lg_ready, 1)
                            dve.wait_ge(lg_ready, 2)
                            for t in range(CT):
                                nc.vector.match_replace(mqa.lt[:, t, :], mqa.rep[:, t, :], mqa.lg[:, t, :],
                                                        TAKEN).then_inc(lg_taken, 1)
                            dve.wait_ge(lg_taken, CT)
                            nc.vector.tensor_scalar(mqa.mw[:, :, 0:NE1], mqa.lt[:, :, 0:NE1], IS_TAKEN, None,
                                                    ALU.is_lt).then_inc(route, 1)
                            dve.wait_ge(route, 1)
                            dve.wait_ge(lg_exp, 1)
                            nc.vector.tensor_tensor(mqa.dif[:, :, :], mqa.mw[:, :, 0:NE1], mqa.ex[:, :, :],
                                                    ALU.mult).then_inc(route, 1)
                            dve.wait_ge(route, 2)
                            nc.vector.reduce_sum(mqa.ws[:, :], mqa.dif[:, :, :], AX_X).then_inc(route, 1)
                            dve.wait_ge(route, 3)
                            nc.vector.reciprocal(mqa.rw[:, :], mqa.ws[:, :]).then_inc(route, 1)
                            dve.wait_ge(route, 4)
                            nc.vector.tensor_tensor(mqa.mw[:, :, NE1:2 * NE1], mqa.dif[:, :, :],
                                                    mqa.rw[:, :].unsqueeze(2).broadcast_to([P, CT, NE1]),
                                                    ALU.mult).then_inc(route, 1)
                            dve.wait_ge(route, 5)
                            nc.vector.tensor_tensor(racc[:, :, :], racc[:, :, :], mqa.mw[:, :, :],
                                                    ALU.add).then_inc(route, 1)

                    if is_a:
                        nc.vector.tensor_copy(mqa.xw[:, :], chunk).then_inc(xw0_ready, 1)
                    if is_a or is_b:
                        nc.vector.tensor_copy(xhi[:, :], chunk).then_inc(split, 1)
                        dve.wait_ge(split, 1)
                        nc.vector.tensor_tensor(xlo[:, :], chunk, xhi[:, :].bitcast(F32), ALU.subtract
                                                ).then_inc(split, 1)
                    if is_m:
                        nc.vector.reduce_sum(moe.rsum[:, :], racc[:, :, :].rearrange("p t e -> p e t"), AX_X
                                             ).then_inc(rsum_ready, 1)
                    for r in range(n_rounds):
                        if is_a and r == 4:
                            dve.wait_ge(down_done, TILES0 + 1)
                            nc.vector.tensor_tensor(mqa.fs[:, :], ACC, mqa.xw[:, :], ALU.add
                                                    ).then_inc(acc_taken, 1)
                            max0(0)
                        steps = steps_of(r)
                        done = 0
                        if is_a and r == ROUNDS - 1:
                            for piece in range(8):
                                search(r, piece)
                                tail_of_layer0(piece)
                        for k, t in steps:
                            if is_a and not is_f[r] and t + 1 < L0_PAIRS:
                                max0(t + 1)
                            upto = -(-8 * (k + 1) // len(steps))
                            for piece in range(done, upto):
                                search(r, piece)
                            done = upto
                            if is_b:
                                gated_tile(t)
                            if (r, k) in placed:
                                shared(placed[r, k])
                        if is_m and r == 3:
                            bank_full(dve, "total")
                            nc.vector.tensor_copy(moe.tot[:, :], MI[:, 0:16]).then_inc(mean_ready, 1)
                            dve.wait_ge(mean_ready, 1)
                            nc.vector.sem_inc(mi_free, 1)
                            nc.vector.tensor_scalar(moe.cnt[:, :], moe.tot[:, 0:NE1], 1.0, None, ALU.max
                                                    ).then_inc(mean_ready, 1)
                            dve.wait_ge(mean_ready, 2)
                            nc.vector.reciprocal(moe.rcnt[:, :], moe.cnt[:, :]).then_inc(mean_ready, 1)
                            dve.wait_ge(mean_ready, 3)
                            nc.vector.tensor_tensor(moe.mean[:, :], moe.tot[:, NE1:2 * NE1], moe.rcnt[:, :],
                                                    ALU.mult).then_inc(mean_ready, 1)
                    if is_b:
                        dve.wait_ge(down_done, TILES1)
                        nc.vector.tensor_copy(moe.fs[:, :], ACC).then_inc(acc_taken, 1)
                    if phase == "E":
                        for name in uses:
                            shared(name)

                @blk.gpsimd
                def _(pool):
                    def gate(t):
                        e = (t - T_SH) // 2
                        pool.wait_ge(act_done, t + 1)
                        pool.wait_ge(gate_in[e % 4], 16 * (e // 4 + 1))
                        h = mqa.hb[:, t % 6, :]
                        nc.gpsimd.tensor_tensor(h, h, mqa.gate[:, e % 4, :], ALU.mult).then_inc(gated, 1)

                    def mask(e):
                        if e == 0:
                            pool.wait_ge(split, 2)
                        pool.wait_ge(gate_in[e % 2], 16 * (e // 2 + 1))
                        if e >= 2:
                            pool.wait_ge(up_done, 2 * PER_E1 * (e - 1))
                        for src, dst in ((xhi, moe.xmhi), (xlo, moe.xmlo)):
                            nc.gpsimd.tensor_tensor(dst[:, e % 2, :], src[:, :].bitcast(F32),
                                                    moe.mask[:, e % 2, :], ALU.mult).then_inc(masked, 1)

                    def select(n):
                        pool.wait_ge(top_taken, 16 * n + 16)
                        pool.wait_ge(exp1_done, n + 1)
                        nc.gpsimd.tensor_scalar(xr[:, n % 2], xr[:, n % 2], IS_TAKEN, None, ALU.is_lt
                                                ).then_inc(is_taken, 1)
                        pool.wait_ge(is_taken, n + 1)
                        nc.gpsimd.tensor_tensor(e1[:, n % 2], e1[:, n % 2], xr[:, n % 2], ALU.mult
                                                ).then_inc(p_ready, 1)

                    if is_b:
                        mask(0)
                    for r in range(n_rounds):
                        if is_a and is_f[r]:
                            for _, t in steps_of(r):
                                if t >= T_SH:
                                    gate(t)
                        if is_a and r == ROUNDS - 1:
                            pool.wait_ge(resid, 1)
                            nc.gpsimd.tensor_copy(x_tiles, mqa.x1[:, :, :])
                        if is_b and r + 1 < NE1:
                            mask(r + 1)
                        if is_m:
                            pool.wait_ge(kept, r + 1)
                            hi, lo = (moe.ghi, moe.glo) if r < 4 else (moe.uhi, moe.ulo)
                            c = slice((r % 4) * 1024, (r % 4 + 1) * 1024)
                            nc.gpsimd.tensor_tensor(lo[:, c], moe.stage[:, r % 2, :],
                                                    hi[:, c].bitcast(F32), ALU.subtract).then_inc(split, 1)
                        if not is_a and cur and r < ROUNDS - 1:
                            select(r)

        def s_tiles(seq0):
            return sall[:, :, :].rearrange("p t d -> p (t d)")[:, bass.ds(seq0, SEQ)
                                                               ].rearrange("p (q d) -> p q d", d=D)

        class Bufs:
            pass

        phase_a = ExitStack()
        mqa = Bufs()

        def sa(name, shape, dt=F32):
            return sb(name, shape, dt, phase_a)

        mqa.w1hi = sa("w1hi", [P, TILES0 * P], F32R)
        mqa.w1lo = sa("w1lo", [P, TILES0 * P], F32R)
        mqa.w2 = sa("w2", [P, TILES0, D])
        mqa.b1 = sa("b1", [P, TILES0])
        mqa.b2 = sa("b2", [16, D])
        mqa.vx = sa("vx0", [P, 2, 2, 32])
        mqa.lg = sa("lg1", [P, CT, NE1 + 6])
        mqa.rep = sa("rep1", [P, CT, 8])

        prologue = ExitStack()

        def sp_(name, shape, dt=F32):
            return sb(name, shape, dt, prologue)

        raw = sp_("raw", [P, TILES0 * P])
        cst = sp_("cst", [P, P])
        wk8 = sp_("wk8", [P, DH])
        gw0 = sp_("gw0", [P, NE0])
        gb0 = sp_("gb0", [1, NE0])
        bs = sp_("bs", [P, NT, 6])
        mv = sp_("mv", [P, NT, 2])
        std = sp_("std", [P, NT])
        rstd = sp_("rstd", [P, NT])
        xn = sp_("xn", [P, 2, CT, D])
        lg = sp_("lg", [P, NT, NE0 + 5])
        lt = sp_("lt", [P, NT, NE0 + 5])
        l8 = sp_("l8", [P, NT, 8])
        rep = sp_("rep", [P, NT, 8])
        dif = sp_("dif", [P, NT, NE0])
        ex = sp_("ex", [P, NT, NE0])
        ws = sp_("ws", [P, NT])
        rw = sp_("rw", [P, NT])
        gates = sp_("gates", [P, NT, 16])
        gT = sp_("gT", [16, NTOK])
        XP = NT // 4
        weights = [(ident[:, :], A["ident"]), (cst[:, :], A["causal"]), (lane[:, :], A["lane"]),
                   (gw0[:, :], A["gw0"]), (gb0[:, :], A["gb0"]),
                   (wq0[:, :], A["wq0"]), (wk8[:, :], A["wk0"]), (wv0[:, :], A["wv0"]),
                   (wq1[:, :], A["wq1"]), (wk1[:, :], A["wk1"]), (wv1[:, :], A["wv1"]),
                   (wo1[:, :], A["wo1"]), (rows[:, :], A["rows1"]), (cols[:, :], A["cols1"]),
                   (rw1[:, :], A["rw1"]), (mqa.b1[:, :], A["b1"]), (mqa.b2[:, :], A["b2"])]
        x_dram = A["x"].rearrange("(t p) d -> p t d", p=P)

        with nc.Block(no_gpsimd_drain=True) as blk:
            @blk.sync
            def _(sp):
                for n in range(4):
                    sp.dma_start(xall[:, n * XP:(n + 1) * XP, :], x_dram[:, n * XP:(n + 1) * XP, :]
                                 ).then_inc(x_in[n], 16)
                sp.dma_start(raw[:, :], A["w1"]).then_inc(stage_in[0], 16)
                sp.dma_start(mqa.w2[:, :, :], A["w2"]).then_inc(stage_in[1], 16)
                sp.wait_ge(stage_in[1], 16)
                sp.wait_ge(kept, 1)
                sp.dma_start(GD[:, :], gT[:, :]).then_inc(stored, 16)
                sp.wait_ge(stored, 16)

            @blk.scalar
            def _(act):
                for dst, src in weights:
                    act.dma_start(dst, src).then_inc(w_in, 16)
                act.wait_ge(aggr, NT)
                act.wait_ge(consts, 1)
                nc.scalar.activation(std[:, :], mv[:, :, 1], ACT.Sqrt, bias=epsb[:, :]).then_inc(std_done, 1)
                for q in range(NCH):
                    act.wait_ge(mi_full, q + 1)
                    nc.scalar.activation(xT[:, q * CH:(q + 1) * CH], ps[:, q % 2, :], ACT.Copy
                                         ).then_inc(xt_ready, 1)
                act.wait_ge(stage_in[0], 16)
                nc.scalar.activation(mqa.w1hi[:, :], raw[:, :], ACT.Copy).then_inc(split, 1)
                act.wait_ge(w_in, 16 * len(weights))
                nc.scalar.activation(ident16[:, :], ident[:, :], ACT.Copy)
                nc.scalar.activation(causal16[:, :], cst[:, :], ACT.Copy)
                for h in range(NH):
                    nc.scalar.activation(wk0[:, h, :], wk8[:, :], ACT.Copy)
                nc.scalar.activation(bkm[:, :], lane[:, :], ACT.Copy, scale=cols[:, 1:2])
                act.wait_ge(lg_dif, 1)
                nc.scalar.activation(ex[:, :, :], dif[:, :, :], ACT.Exp).then_inc(lg_exp, 1)
                for n in range(8):
                    act.wait_ge(turned, n + 1)
                    last = nc.scalar.activation(gT[:, n * 512:(n + 1) * 512], ps[0:16, n, :], ACT.Copy)
                last.then_inc(kept, 1)

            @blk.gpsimd
            def _(pool):
                nc.gpsimd.memset(epsb[:, :], EPS)
                nc.gpsimd.memset(ones[:, :], 1.0).then_inc(consts, 1)
                nc.gpsimd.memset(vx1[:, :, :, :], 0.0).then_inc(prep, 1)
                nc.gpsimd.memset(mqa.vx[:, :, :, :], 0.0).then_inc(prep, 1)
                pool.wait_ge(prep, 2)
                nc.gpsimd.memset(vx1[:, :, :, DH:DH + 1], 1.0)
                nc.gpsimd.memset(mqa.vx[:, :, :, DH:DH + 1], 1.0)
                nc.gpsimd.memset(racc[:, :, :], 0.0)
                nc.gpsimd.memset(mqa.lg[:, :, :], MASKED)
                nc.gpsimd.memset(mqa.rep[:, :, :], MASKED)
                nc.gpsimd.memset(gates[:, :, 15:16], 1.0)
                nc.gpsimd.memset(rep[:, :, :], MASKED)
                nc.gpsimd.memset(lg[:, :, NE0:NE0 + 5], MASKED).then_inc(consts, 1)

            @blk.vector
            def _(dve):
                for t in range(NT):
                    if t % XP == 0:
                        dve.wait_ge(x_in[t // XP], 16)
                    nc.vector.bn_stats(bs[:, t, :], xall[:, t, :]).then_inc(stats, 1)
                for t in range(NT):
                    dve.wait_ge(stats, t + 1)
                    nc.vector.bn_aggr(mv[:, t, :], bs[:, t, :]).then_inc(aggr, 1)
                dve.wait_ge(std_done, 1)
                nc.vector.reciprocal(rstd[:, :], std[:, :]).then_inc(rstd_done, 1)
                dve.wait_ge(rstd_done, 1)
                for t in range(NT):
                    q = t // CT
                    if q >= 2 and t % CT == 0:
                        dve.wait_ge(mi_full, q - 1)
                    nc.vector.tensor_scalar(xn[:, q % 2, t % CT, :], xall[:, t, :], mv[:, t, 0:1],
                                            rstd[:, t:t + 1], ALU.subtract, ALU.mult).then_inc(xn_ready, 1)
                dve.wait_ge(split, 1)
                nc.vector.tensor_tensor(mqa.w1lo[:, :], raw[:, :], mqa.w1hi[:, :].bitcast(F32), ALU.subtract)
                dve.wait_ge(scored1, 1)
                dve.wait_ge(consts, 2)
                nc.vector.tensor_copy(lg[:, :, 0:NE0],
                                      ps[:, 3, :].rearrange("p (t e) -> p t e", e=16)[:, :, 0:NE0]
                                      ).then_inc(lg_ready, 1)
                dve.wait_ge(lg_ready, 1)
                for t in range(NT):
                    nc.vector.max(l8[:, t, :], lg[:, t, :]).then_inc(lg_max, 1)
                dve.wait_ge(lg_max, NT)
                nc.vector.tensor_tensor(dif[:, :, :], lg[:, :, 0:NE0],
                                        l8[:, :, 0:1].broadcast_to([P, NT, NE0]), ALU.subtract
                                        ).then_inc(lg_dif, 1)
                nc.vector.tensor_copy(rep[:, :, 0:3], l8[:, :, 0:3]).then_inc(lg_ready, 1)
                dve.wait_ge(lg_ready, 2)
                for t in range(NT):
                    nc.vector.match_replace(lt[:, t, :], rep[:, t, :], lg[:, t, :], TAKEN).then_inc(lg_taken, 1)
                dve.wait_ge(lg_exp, 1)
                nc.vector.reduce_sum(ws[:, :], ex[:, :, :], AX_X).then_inc(route, 1)
                dve.wait_ge(route, 1)
                nc.vector.reciprocal(rw[:, :], ws[:, :]).then_inc(route, 1)
                dve.wait_ge(route, 2)
                dve.wait_ge(lg_taken, NT)
                nc.vector.scalar_tensor_tensor(out=dif[:, :, :], in0=lt[:, :, 0:NE0], scalar=IS_TAKEN,
                                               in1=ex[:, :, :], op0=ALU.is_lt, op1=ALU.mult
                                               ).then_inc(route, 1)
                dve.wait_ge(route, 3)
                nc.vector.tensor_tensor(gates[:, :, 0:NE0], dif[:, :, :],
                                        rw[:, :].unsqueeze(2).broadcast_to([P, NT, NE0]), ALU.mult
                                        ).then_inc(route, 1)

            @blk.tensor
            def _(pe):
                pe.wait_ge(w_in, 16 * len(weights))
                for q in range(NCH):
                    pe.wait_ge(xn_ready, CT * (q + 1))
                    if q >= 2:
                        pe.wait_ge(xt_ready, q - 1)
                    for t in range(CT):
                        last = nc.tensor.transpose(ps[:, q % 2, t * P:(t + 1) * P], xn[:, q % 2, t, :],
                                                   ident[:, :])
                    last.then_inc(mi_full, 1)
                pe.wait_ge(xt_ready, NCH)
                pe.wait_ge(consts, 1)
                for t in range(NT):
                    o = ps[:, 3, t * 16:t * 16 + NE0]
                    nc.tensor.matmul(o, xT[:, t * P:(t + 1) * P], gw0[:, :], start=True, stop=False)
                    last = nc.tensor.matmul(o, ones[0:1, :], gb0[0:1, :], start=False, stop=True)
                last.then_inc(scored1, 1)
                pe.wait_ge(route, 4)
                pe.wait_ge(consts, 2)
                for t in range(NT):
                    last = nc.tensor.transpose(ps[0:16, t // 4, (t % 4) * P:(t % 4 + 1) * P],
                                               gates[:, t, :], ident[:, :])
                    if t % 4 == 3:
                        last.then_inc(turned, 1)
        clear_semaphores()
        prologue.close()

        mqa.xw = sa("xw0", [P, CH])
        mqa.qT = sa("qT0", [P, 2, SEQ])
        mqa.km = sa("km0", [P, 2, HG, SEQ])
        mqa.e = sa("e0", [P, 2, 2, W0])
        mqa.mx = sa("mx0", [P, 2, 4])
        mqa.nm = sa("nm0", [P, 2, 4])
        mqa.ot = sa("ot0", [P, 2, HG, SEQ])
        mqa.att = sa("att0", [P, CT, D])
        mqa.hb = sa("hb", [P, 6, CH])
        mqa.gate = sa("gate", [P, 4, CH])
        mqa.gt = sa("gt", [16, CH])
        mqa.fs = mqa.xw
        mqa.g0 = sa("g0", [P, CT, D])
        mqa.x1 = sa("x1", [P, CT, D])
        mqa.xn = mqa.g0
        mqa.xtn = mqa.att[:, :, :].rearrange("p t d -> p (t d)")
        mqa.bs = sa("bs1", [P, CT, 6])
        mqa.mv = sa("mv1", [P, CT, 2])
        mqa.std = sa("std1", [P, CT])
        mqa.rstd = sa("rstd1", [P, CT])
        mqa.l8 = sa("l81", [P, CT, 8])
        mqa.lt = sa("lt1", [P, CT, NE1 + 6])
        mqa.dif = sa("dif1", [P, CT, NE1])
        mqa.ex = sa("ex1", [P, CT, NE1])
        mqa.ws = sa("ws1", [P, CT])
        mqa.rw = sa("rwt1", [P, CT])
        mqa.mw = sa("mw1", [P, CT, 16])
        mqa.mkT = mqa.gt[0:NE1, :]

        block(0, "A", nxt=0)
        clear_semaphores()
        block(1, "A", cur=True, nxt=SEQ)
        clear_semaphores()
        with nc.Fori(2, NCH) as i:
            block(i, "A", cur=True, prev=i * SEQ - 2 * SEQ, nxt=i * SEQ)
            clear_semaphores()
        phase_a.close()

        moe = Bufs()
        moe.ghi = sb("ghi", [P, TILES1 * P], F32R)
        moe.glo = sb("glo", [P, TILES1 * P], F32R)
        moe.uhi = sb("uhi", [P, TILES1 * P], F32R)
        moe.ulo = sb("ulo", [P, TILES1 * P], F32R)
        moe.down = sb("down", [P, TILES1, D])
        moe.rsum = sb("rsum", [P, 16])
        moe.tot = sb("tot", [P, 16])
        moe.cnt = sb("cnt", [P, NE1])
        moe.rcnt = sb("rcnt", [P, NE1])
        moe.mean = sb("mean", [P, NE1])
        with ExitStack() as mid:
            moe.stage = sb("stage", [P, 2, 1024], F32, mid)
            block(0, "M", cur=True, prev=(NCH - 2) * SEQ, nxt=NCH * SEQ)
            clear_semaphores()
        moe.mask = sb("mask", [P, 2, CH])
        moe.xmhi = sb("xmhi", [P, 2, CH], F32R)
        moe.xmlo = sb("xmlo", [P, 2, CH], F32R)
        moe.sg = sb("sg", [P, 2, CH])
        moe.h = sb("h1", [P, 2, CH])
        moe.fs = sb("fs1", [P, CH])
        with nc.Fori(0, NCH - 1) as i:
            block(i, "B", cur=True, prev=i * SEQ + (NCH - 1) * SEQ, nxt=i * SEQ + (NCH + 1) * SEQ)
            clear_semaphores()
        block(NCH - 1, "B", cur=True, prev=(NSEQ - 2) * SEQ)
        clear_semaphores()
        block(0, "E", prev=(NSEQ - 1) * SEQ)
        clear_semaphores()

        out_v = out.rearrange("(t p) d -> p t d", p=P)
        g_all = xT[:, :].rearrange("p (t d) -> p t d", d=D)
        with nc.Block(no_gpsimd_drain=True) as blk:
            @blk.vector
            def _(dve):
                for n in range(4):
                    t = slice(n * XP, (n + 1) * XP)
                    nc.vector.tensor_tensor(sall[:, t, :], sall[:, t, :], g_all[:, t, :], ALU.mult
                                            ).then_inc(silu_done, 1)
                    dve.wait_ge(silu_done, n + 1)
                    nc.vector.tensor_tensor(xall[:, t, :], xall[:, t, :], sall[:, t, :], ALU.add
                                            ).then_inc(resid, 1)

            @blk.sync
            def _(sp):
                for n in range(4):
                    t = slice(n * XP, (n + 1) * XP)
                    sp.wait_ge(resid, n + 1)
                    sp.dma_start(out_v[:, t, :], xall[:, t, :]).then_inc(stored, 16)
                sp.wait_ge(stored, 64)


def kernel(**inputs):
    import concourse.bacc as _bacc
    from concourse.bass_utils import run_bass_kernel_spmd as _run

    a = {k: np.asarray(v) for k, v in inputs.items()}
    c = np.ascontiguousarray
    key = np.arange(P)
    host = {
        "x": a["L0_attn_x"].reshape(NTOK, D),
        "ident": np.eye(P, dtype=np.float32),
        "causal": np.where(key[None, :] > key[:, None], np.float32(MASKED), np.float32(0)),
        "lane": (key[:, None] // DH % HG == np.arange(HG)[None, :]).astype(np.float32),
        "gw0": a["L0_ffn_gW"], "gb0": a["L0_ffn_gb"].reshape(1, NE0),
        "wq0": a["L0_attn_Wq"].T, "wk0": a["L0_attn_Wk"].T, "wv0": a["L0_attn_Wv"].T,
        "wq1": a["L1_attn_Wq"].T, "wk1": a["L1_attn_Wk"].T, "wv1": a["L1_attn_Wv"].T,
        "wo1": a["L1_attn_Wo"].T,
        "rows1": np.concatenate([a["L1_attn_bv"], a["L1_attn_bo"]]).reshape(1, 2 * D),
        "cols1": np.stack([a["L1_attn_bq"], a["L1_attn_bk"]], axis=1),
        "rw1": a["L1_ffn_router_w"].T,
        "b1": np.concatenate([a["L0_ffn_sb1"].reshape(-1), a["L0_ffn_rb1"].reshape(-1)]
                             ).reshape(TILES0, P).T,
        "b2": np.concatenate([a["L0_ffn_rb2"], a["L0_ffn_sb2"]], axis=0),
        "w1": np.concatenate([a["L0_ffn_sW1"].transpose(1, 0, 2).reshape(D, -1),
                              a["L0_ffn_rW1"].transpose(1, 0, 2).reshape(D, -1)], axis=1),
        "w2": np.concatenate([a["L0_ffn_sW2"].reshape(-1, D), a["L0_ffn_rW2"].reshape(-1, D)], axis=0
                             ).reshape(TILES0, P, D).transpose(1, 0, 2),
        "w_gate": a["L1_ffn_gate_w"].reshape(TILES1 * P, D).T,
        "w_up": a["L1_ffn_up_w"].reshape(TILES1 * P, D).T,
        "w_down": a["L1_ffn_down_w"].transpose(0, 2, 1).reshape(TILES1, P, D).transpose(1, 0, 2),
    }
    host = {k: c(v) for k, v in host.items()}
    nc = _bacc.Bacc("TRN2", target_bir_lowering=False, num_devices=1)
    aps, arrays = {}, {}
    for name, v in host.items():
        arrays[f"in_{name}_dram"] = v
        aps[name] = nc.dram_tensor(f"in_{name}_dram", v.shape, mybir.dt.from_np(v.dtype),
                                   kind="ExternalInput").ap()
    out = nc.dram_tensor("out_0_dram", (NTOK, D), F32, kind="ExternalOutput").ap()
    build(nc, aps, out)
    r = _run(nc, [arrays], core_ids=[0])
    return r.results[0]["out_0_dram"].reshape(NSEQ, SEQ, D)
```

```python
from contextlib import ExitStack

import numpy as np

import concourse.bass as bass
from concourse import mybir

F32 = mybir.dt.float32
F32R = mybir.dt.float32r
BF16 = mybir.dt.bfloat16
ALU = mybir.AluOpType
ACT = mybir.ActivationFunctionType
AX_X = mybir.AxisListType.X

P = 128
D = 128
NSEQ, SEQ = 16, 256
NTOK = NSEQ * SEQ
NT = NTOK // P
CH = 512
CT = CH // P
NCH = NTOK // CH
NH, DH = 16, 8
NG, HG = 4, 4
SCALE = float(DH) ** -0.5
TOPK = 32
F_SH, F_R, NE0 = 512, 256, 15
T_SH = F_SH // P
TILES0 = (F_SH + NE0 * F_R) // P
NE1, F1 = 8, 512
TILES1 = NE1 * F1 // P
PER_E1 = F1 // P
EPS = 1e-5
MASKED = -1.0e30
TAKEN = -2.0e30
IS_TAKEN = -1.5e30
ROUNDS = 8
W1C = 3 * P
W0 = 2 * SEQ
R_HI, R_LO_Q, R_LO_K, R_MAX = 0, DH, 2 * DH, 3 * DH
STEPS_A = [7, 8, 7, 6, 6, 6, 6, 4]
F_ROUNDS = 5
EARLY = 2
LEAD = 4


def build(nc, A, out):
    GD = nc.dram_tensor("gates_t", (16, NTOK), F32, kind="Internal").ap()
    MD = nc.dram_tensor("masks_t", (NE1, NTOK), F32, kind="Internal").ap()
    with ExitStack() as ctx:
        def sb(name, shape, dt=F32, c=ctx):
            return c.enter_context(nc.sbuf_tensor(name, shape, dt))

        ps = ctx.enter_context(nc.psum_tensor("ps", [P, 8, 512], F32))
        B_H0, B_H1, B_ACC, B_MI, B_S, B_PT, B_O = 0, 1, 2, 3, 4, 6, 7
        S1 = ps[:, B_S:B_S + 2, :]
        PT = ps[:, B_PT, :]
        OB = [ps[:, B_O, 0:SEQ], ps[:, B_O, SEQ:2 * SEQ]]
        MI = ps[:, B_MI, :]
        ACC = ps[:, B_ACC, :]

        xall = sb("xall", [P, NT, D])
        sall = sb("sall", [P, NT, D])
        xT = sb("xT", [P, NTOK])
        ident = sb("ident", [P, P])
        ident16 = sb("ident16", [P, P], BF16)
        causal16 = sb("causal16", [P, P], BF16)
        group = sb("group", [P, NG])
        parts = sb("parts", [P, 4])
        ones = sb("ones", [P, P])
        wq0 = sb("wq0", [P, HG, P])
        wq1 = sb("wq1", [P, HG, P])
        wk1 = sb("wk1", [P, HG, P])
        wv1 = sb("wv1", [P, D])
        wo1 = sb("wo1", [P, D])
        rows = sb("rows", [1, 2 * D])
        cols = sb("cols", [P, 2, HG])
        cols_lo = sb("cols_lo", [P, 2, HG])
        rw1 = sb("rw1", [P, NE1])
        epsb = sb("epsb", [P, 1])
        racc = sb("racc", [P, CT, 16])
        xw1 = sb("xw1", [P, SEQ])
        full = sb("full", [P, CH])
        high = sb("high", [P, CH], F32R)
        q1 = sb("q1", [P, HG, SEQ], F32R)
        k1 = sb("k1", [P, HG, SEQ], F32R)
        vx1 = sb("vx1", [P, 2, NH, 32])
        e1 = sb("e1", [P, 2, 2, W1C])
        xr = sb("xr", [P, 2, 2, W1C])
        top8 = sb("top8", [P, 2, 4, 4, 8])
        nm1 = sb("nm1", [P, 2, 4])
        pts = sb("pts", [P, 2, 2, W1C])
        ot1 = sb("ot1", [P, HG, SEQ])
        att1 = sb("att1", [P, 2, D])
        attT = sb("attT", [P, SEQ])
        rc1 = sb("rc1", [P, NH])
        xhi = sb("xhi", [P, CH], F32R)
        xlo = sb("xlo", [P, CH], F32R)

        sems = {}

        def sem(name):
            sems[name] = ctx.enter_context(nc.semaphore(name))
            return sems[name]

        x_in = [sem(f"x_in{n}") for n in range(4)]
        first_in = sem("first_in")
        w_in = sem("w_in")
        stage_in = [sem(f"stage_in{n}") for n in range(2)]
        gate_in = [sem(f"gate_in{n}") for n in range(4)]
        stored = sem("stored")
        xw1_ready = sem("xw1_ready")
        xw0_ready = sem("xw0_ready")
        proj_ready = sem("proj_ready")
        split1 = sem("split1")
        split0 = sem("split0")
        v1_ready = sem("v1_ready")
        v0_ready = sem("v0_ready")
        scored1 = sem("scored1")
        scored0 = sem("scored0")
        scored0_t = sem("scored0_t")
        neg_max1 = sem("neg_max1")
        row_max = sem("row_max")
        max_off = sem("max_off")
        k_ready = sem("k_ready")
        exp1_done = sem("exp1_done")
        exp0_done = sem("exp0_done")
        top_found = sem("top_found")
        top_taken = sem("top_taken")
        is_taken = sem("is_taken")
        p_ready = sem("p_ready")
        p_ready_late = sem("p_ready_late")
        turned = sem("turned")
        pts_ready = sem("pts_ready")
        pv_done = sem("pv_done")
        o_taken = sem("o_taken")
        mi_full = sem("mi_full")
        mi_free = sem("mi_free")
        rc_ready = sem("rc_ready")
        rc_used = sem("rc_used")
        att1_ready = sem("att1_ready")
        att0_ready = sem("att0_ready")
        split = sem("split")
        up_done = sem("up_done")
        act_done = sem("act_done")
        gated = sem("gated")
        down_done = sem("down_done")
        masked = sem("masked")
        acc_taken = sem("acc_taken")
        silu_done = sem("silu_done")
        resid = sem("resid")
        stats = sem("stats")
        aggr = sem("aggr")
        std_done = sem("std_done")
        rstd_done = sem("rstd_done")
        xn_ready = sem("xn_ready")
        xt_ready = sem("xt_ready")
        kept = sem("kept")
        lg_ready = sem("lg_ready")
        lg_max = sem("lg_max")
        lg_dif = sem("lg_dif")
        lg_exp = sem("lg_exp")
        lg_taken = sem("lg_taken")
        route = sem("route")
        mask_t = sem("mask_t")
        prep = sem("prep")
        high_ready = sem("high_ready")
        rsum_ready = sem("rsum_ready")
        mean_ready = sem("mean_ready")
        consts = sem("consts")

        numbers = sorted(s.num for s in sems.values())
        assert numbers == list(range(numbers[0], numbers[0] + len(numbers)))

        def clear_semaphores():
            nc.multi_engine_barrier(list(nc.engines.keys()),
                                    sems_to_clear=range(numbers[0], numbers[-1] + 1))

        clear_semaphores()

        def pair_heads(n):
            j, gp = n // 2, n % 2
            return j, (2 * gp, 2 * gp + 1)

        tiles1 = [(g, c, w) for g in range(2) for c, w in ((0, P), (P, 2 * P))]

        L0_PAIRS = 2 * ROUNDS

        def block(i, phase, cur=False, prev=None, nxt=None, tail=None, ffn_of=None,
                  begun=False, ahead=False):
            is_a, is_b, is_m = phase == "A", phase == "B", phase == "M"
            prev_is, nxt_is = prev is not None, nxt is not None
            tok0 = i * CH
            chunk = xT[:, bass.ds(tok0, CH)]
            has_tail = tail is not None
            own_tail = has_tail and is_a and not cur
            if is_a:
                n_steps = STEPS_A
                is_f = [r < F_ROUNDS for r in range(ROUNDS)]
            else:
                n_steps = [4] * ROUNDS
                is_f = [False] * ROUNDS
            n_rounds = 0 if phase == "E" else ROUNDS

            def steps_of(r):
                base = sum(n_steps[(F_ROUNDS if is_a and r >= F_ROUNDS else 0):r])
                return list(enumerate(range(base, base + n_steps[r])))

            order = [(1, -1)] if prev_is else []
            for r in range(n_rounds):
                if is_a and not is_f[r]:
                    for k, u in steps_of(r):
                        order += [(0, u - 1)] if u else []
                        order += [(1, r - 1)] if k == 4 and cur else []
                    if r == ROUNDS - 1:
                        order += [(1, r - 1)] if n_steps[r] <= 4 and cur else []
                        order += [(0, L0_PAIRS - 1)]
                elif cur and r:
                    order += [(1, r - 1)]
            turn_order = [q for q in order if q[0] == 1]

            def odd_before(pair):
                return sum(1 for q in order[:order.index(pair)] if q[1] % 2 == 1)

            slots = []
            if is_a:
                for u in range(-LEAD, L0_PAIRS):
                    if u + LEAD < L0_PAIRS:
                        slots += [("M", 2 * (u + LEAD)), ("M", 2 * (u + LEAD) + 1)]
                    if u >= 0:
                        slots += [("X", 2 * u), ("X", 2 * u + 1)]

            placed = {}

            def place(r, names, steps=range(ROUNDS)):
                for k, name in zip(steps, names):
                    placed[r, k] = name

            of_prev = ("o1_0", "o1_1", "att1", "y1")
            of_cur = ("qk1_1", "qk1_2", "qk1_3", "v1")
            in_tail = ("o0_0", "o0_1", "o0_2", "o0_3", "ln", "logits", "masks")
            if is_a:
                at = {"q0_0": 15, "q0_1": 21, "q0_2": 23, "q0_3": 27, "k0": 29, "v0": 31}
                if cur:
                    at |= {"qk1_1": 3, "v1": 5, "qk1_2": 13, "qk1_3": 25}
                if prev_is:
                    at |= {"o1_0": 9, "o1_1": 10, "att1": 11, "y1": 12}
                if has_tail and cur:
                    at |= {"o0_0": 1, "o0_1": 2, "o0_2": 7, "o0_3": 8, "ln": 18, "logits": 19, "masks": 20}
                step_of_tile = {t: (r, k) for r in range(F_ROUNDS) for k, t in steps_of(r)}
                placed = {step_of_tile[t]: name for name, t in at.items()}
                if nxt_is and cur:
                    placed[[(ROUNDS - 1, k) for k, u in steps_of(ROUNDS - 1) if u == L0_PAIRS - 2][0]] = "qkn"
            else:
                if ffn_of is not None:
                    place(0, ("ffn",))
                if cur:
                    place(0, of_cur[:2], (1, 3))
                    place(1, of_cur[3:], (1,))
                    place(3, of_cur[2:3])
                if prev_is:
                    place(1, of_prev[:2], (2, 3))
                    place(2, of_prev[2:])
                if has_tail:
                    place(2, in_tail[0:2], (2, 3))
                    place(3, in_tail[2:4], (1, 2))
                    place(4, in_tail[4:6], (2, 3))
                    place(5, in_tail[6:7], (1,))
            uses = [placed[k] for k in sorted(placed) if placed[k] != "qkn"]
            if is_a:
                uses += ["ffn"] + [f"m_{v}" for v in range(L0_PAIRS // 2)]
                if own_tail:
                    uses += list(in_tail)
                uses += ["qkn"] if nxt_is else []
            else:
                if is_m:
                    uses += ["total"]
                uses += ["qkn"] if nxt_is else []
            std_at, exp_at = ((2, 2), (3, 2)) if is_a else ((4, 2), (5, 2))
            outputs = [name for name in uses if name[:2] in ("o0", "o1")]
            projections = [name for name in uses if name[:2] in ("qk", "q0", "k0")]
            of_layer1 = [name for name in projections if name[:2] == "qk"]
            of_layer0 = [name for name in projections if name[:2] != "qk"]

            def parts_free(act, name):
                n = projections.index(name)
                if n:
                    before = projections[n - 1]
                    if before in of_layer1:
                        act.wait_ge(split1, 2 * of_layer1.index(before) + 2)
                    else:
                        act.wait_ge(split0, of_layer0.index(before) + 1)

            def masks_done(e):
                return 2 * (e + 1 - begun)

            def masks_in(e):
                return 16 * (e // 2 + 1 - (begun and e % 2 == 0))

            by_pool = range(F_ROUNDS if is_a else 0, ROUNDS - 1)

            def numerators_ready(eng, n):
                if n in by_pool:
                    eng.wait_ge(p_ready_late, n - by_pool[0] + 1)
                else:
                    eng.wait_ge(p_ready, n + 1)

            def finish(eng, engine, t):
                eng.wait_ge(mi_free, uses.index("ffn") + 1)
                g = xT[:, :].rearrange("p (t d) -> p t d", d=D)[:, t, :]
                engine.tensor_tensor(g, g, sall[:, t, :], ALU.mult).then_inc(silu_done, 1)
                eng.wait_ge(silu_done, 1)
                engine.tensor_tensor(xall[:, t, :], xall[:, t, :], g, ALU.add).then_inc(resid, 1)

            def store(sp, first, count):
                sp.wait_ge(resid, 1)
                sp.dma_start(out[bass.ds(first * P, count * P), :].rearrange("(t p) d -> p t d", p=P),
                             xall[:, bass.ds(first, count), :]).then_inc(stored, 16)

            def bank_mine(pe, name):
                if uses.index(name):
                    pe.wait_ge(mi_free, uses.index(name))

            def bank_full(eng, name):
                eng.wait_ge(mi_full, uses.index(name) + 1)

            with nc.Block(no_gpsimd_drain=True) as blk:

                @blk.sync
                def _(sp):
                    if is_a:
                        for e in range(NE0):
                            if e >= 4:
                                sp.wait_ge(gated, 2 * (e - 4) + 2)
                            sp.dma_start(mqa.gate[:, e % 4, :],
                                         GD[e:e + 1, bass.ds(tok0, CH)].broadcast_to([P, CH])
                                         ).then_inc(gate_in[e % 4], 16)
                            if e == 3:
                                sp.dma_start(mqa.gt, GD[:, bass.ds(tok0, CH)]).then_inc(w_in, 16)
                    if is_b:
                        for e in range(begun, NE1 + ahead):
                            if e == 2 and ffn_of is not None:
                                store(sp, ffn_of * CT, CT)
                            if e >= 2 + begun:
                                sp.wait_ge(masked, masks_done(e - 2))
                            row, first = (0, tok0 + CH) if e == NE1 else (e, tok0)
                            sp.dma_start(moe.mask[e % 2],
                                         MD[row:row + 1, bass.ds(first, CH)].broadcast_to([P, CH])
                                         ).then_inc(gate_in[e % 2], 16)
                    if is_b and ffn_of is not None:
                        sp.wait_ge(stored, 16)
                    if is_m:
                        sp.dma_start(moe.down[:, :, :], A["w_down"]).then_inc(w_in, 16)
                        for n in range(8):
                            if n >= 2:
                                sp.wait_ge(split, n - 1)
                            src = A["w_gate" if n < 4 else "w_up"][:, (n % 4) * 1024:(n % 4 + 1) * 1024]
                            sp.dma_start(moe.stage[:, n % 2, :], src).then_inc(stage_in[n % 2], 16)
                    if phase == "E":
                        store(sp, (NCH - 1) * CT, CT)
                        sp.wait_ge(stored, 16)
                    if has_tail:
                        sp.wait_ge(mask_t, 1)
                        sp.dma_start(MD[:, bass.ds(tail * CH, CH)], mqa.mkT).then_inc(stored, 16)
                        sp.wait_ge(stored, 16)

                @blk.tensor
                def _(pe):
                    def up(t):
                        if t >= 2:
                            pe.wait_ge(act_done, t - 1)
                        if t == 0 and not begun:
                            pe.wait_ge(split, 2)
                        f = slice(t * P, (t + 1) * P)
                        o = ps[:, B_H0 + t % 2, :]
                        nc.tensor.matmul(o, mqa.w1hi[:, f], xhi[:, :], start=True, stop=False)
                        nc.tensor.matmul(o, mqa.w1lo[:, f], xhi[:, :], start=False, stop=False)
                        nc.tensor.matmul(o, mqa.w1hi[:, f], xlo[:, :], start=False, stop=True
                                         ).then_inc(up_done, 1)

                    def down(t):
                        if t < T_SH:
                            pe.wait_ge(act_done, t + 1)
                        else:
                            pe.wait_ge(gated, t - T_SH + 1)
                        nc.tensor.matmul(ACC, mqa.w2[:, t, :], mqa.hb[:, t % 6, :], start=(t == 0),
                                         stop=False).then_inc(down_done, 1)

                    def gate1(t):
                        f = slice(t * P, (t + 1) * P)
                        if t:
                            pe.wait_ge(act_done, t)
                        elif not begun:
                            pe.wait_ge(split, 2)
                        o = ps[:, B_H0, :]
                        nc.tensor.matmul(o, moe.ghi[:, f], xhi[:, :], start=True, stop=False)
                        nc.tensor.matmul(o, moe.glo[:, f], xhi[:, :], start=False, stop=False)
                        nc.tensor.matmul(o, moe.ghi[:, f], xlo[:, :], start=False, stop=True
                                         ).then_inc(up_done, 1)

                    def up1(t):
                        f = slice(t * P, (t + 1) * P)
                        e = t // PER_E1
                        if t:
                            pe.wait_ge(gated, t)
                        if t % PER_E1 == 0 and e >= begun:
                            pe.wait_ge(masked, masks_done(e))
                        o = ps[:, B_H1, :]
                        mhi, mlo = moe.xmhi[:, e % 2, :], moe.xmlo[:, e % 2, :]
                        nc.tensor.matmul(o, moe.uhi[:, f], mhi, start=True, stop=False)
                        nc.tensor.matmul(o, moe.ulo[:, f], mhi, start=False, stop=False)
                        nc.tensor.matmul(o, moe.uhi[:, f], mlo, start=False, stop=True
                                         ).then_inc(up_done, 1)

                    def down1(t):
                        pe.wait_ge(gated, t + 1)
                        nc.tensor.matmul(ACC, moe.down[:, t, :], moe.h[:, t % 2, :], start=(t == 0),
                                         stop=(t == TILES1 - 1)).then_inc(down_done, 1)

                    def scores1(n):
                        if cur:
                            pe.wait_ge(exp1_done, n)
                        if n % 2 == 0:
                            pe.wait_ge(split1, 2 * of_layer1.index(
                                "qkn" if n == ROUNDS else f"qk1_{n // 2}") + 2)
                        j, groups = pair_heads(n % ROUNDS)
                        for b in range(2):
                            o = S1[:, b, 0:W1C].rearrange("p (a k) -> p a k", k=P)[:, 0:3:2, :]
                            nc.tensor.matmul(o, ident16[:, :],
                                             causal16[:, :].unsqueeze(1).broadcast_to([P, 2, P]),
                                             start=True, stop=True)
                        for c0, w, q0 in ((0, P, 0), (P, 2 * P, P)):
                            for b, g in enumerate(groups):
                                last = nc.tensor.matmul(S1[:, b, c0:c0 + w],
                                                        q1[32 * g:32 * g + 32, j, q0:q0 + P],
                                                        k1[32 * g:32 * g + 32, j, 0:w],
                                                        start=False, stop=True, skip_group_check=True)
                        last.then_inc(scored1, 1)

                    def score_bank(kind, h):
                        k = slots.index((kind, h))
                        if k < 3:
                            if k % 2 == 0:
                                pe.wait_ge(k_ready, 2 + k)
                            if k == 2:
                                pe.wait_ge(acc_taken, 1)
                            else:
                                pe.wait_ge(act_done, TILES0 - 1 + k)
                        else:
                            kind, h = slots[k - 3]
                            pe.wait_ge(row_max if kind == "M" else exp0_done, h + 1)
                        return ps[:, k % 3, :]

                    def head0(h):
                        n = h // 2
                        return pair_heads(n % ROUNDS)[1][h % 2], n // ROUNDS, (n % ROUNDS) // 2

                    def scores0(u):
                        for h in (2 * u, 2 * u + 1):
                            o = score_bank("M", h)
                            g, s, j = head0(h)
                            for q in range(2):
                                t = s * SEQ + q * P
                                last = nc.tensor.matmul(o[:, q * SEQ:(q + 1) * SEQ], mqa.q[:, j, t:t + P],
                                                        mqa.kg[g][:, s * SEQ:(s + 1) * SEQ],
                                                        start=True, stop=True)
                            last.then_inc(scored0, 1)

                    def scores0_turned(u):
                        if u % 2 == 0:
                            pe.wait_ge(max_off, u // 2 + 1)
                        for h in (2 * u, 2 * u + 1):
                            o = score_bank("X", h)
                            g, s, j = head0(h)
                            for kt in range(2):
                                t = s * SEQ + kt * P
                                last = nc.tensor.matmul(o[:, kt * SEQ:(kt + 1) * SEQ], mqa.kg[g][:, t:t + P],
                                                        mqa.q[:, j, s * SEQ:(s + 1) * SEQ],
                                                        start=True, stop=True)
                            last.then_inc(scored0_t, 1)

                    def turn(pair, b):
                        n = pair[1]
                        k = turn_order.index(pair)
                        if 2 * k + b:
                            pe.wait_ge(pts_ready, 2 * k + b)
                        if n >= 0:
                            numerators_ready(pe, n)
                        for m, c in enumerate((0, P, 2 * P)):
                            last = nc.tensor.transpose(PT[:, m * P:(m + 1) * P],
                                                       e1[:, n % 2, b, c:c + P], ident[:, :])
                        last.then_inc(turned, 1)

                    def values(pair):
                        layer, n = pair
                        j, groups = pair_heads(n % ROUNDS)
                        if odd_before(pair):
                            pe.wait_ge(o_taken, odd_before(pair))
                        if layer == 1:
                            k = turn_order.index(pair)
                            pe.wait_ge(pts_ready, 2 * k + 2)
                            if n == 0:
                                pe.wait_ge(v1_ready, 1)
                        else:
                            if n == 0:
                                pe.wait_ge(v0_ready, 1)
                            pe.wait_ge(exp0_done, 2 * n + 2)
                        for kt in range(2):
                            for b, g in enumerate(groups):
                                o = OB[layer][32 * g:32 * g + 32, :]
                                if layer == 1:
                                    h = HG * g + j
                                    p = pts[:, k % 2, b, :]
                                    if kt == 0:
                                        last = nc.tensor.matmul(o, vx1[:, 0, h, :], p[:, 0:SEQ],
                                                                start=True, stop=True)
                                    else:
                                        last = nc.tensor.matmul(o[:, P:SEQ], vx1[:, 1, h, :], p[:, SEQ:W1C],
                                                                start=False, stop=True, skip_group_check=True)
                                else:
                                    last = nc.tensor.matmul(o, mqa.vx[:, n // ROUNDS, kt, :],
                                                            mqa.e[:, n % 2, b, kt * SEQ:(kt + 1) * SEQ],
                                                            start=(kt == 0), stop=(kt == 1))
                        last.then_inc(pv_done, 1)

                    def tiles_turned(src):
                        for t in range(CT):
                            last = nc.tensor.transpose(MI[:, t * P:(t + 1) * P], src(t), ident[:, :])
                        last.then_inc(mi_full, 1)

                    def shared(name):
                        bank_mine(pe, name)
                        if name[:2] == "qk":
                            if name == "qkn":
                                pe.wait_ge(xw1_ready, 1)
                            j = 0 if name == "qkn" else int(name[-1])
                            nc.tensor.matmul(MI[:, 0:SEQ], wq1[:, j, :], xw1[:, :], start=True, stop=True)
                            nc.tensor.matmul(MI[:, SEQ:2 * SEQ], wk1[:, j, :], xw1[:, :], start=True,
                                             stop=True).then_inc(mi_full, 1)
                        elif name == "v1":
                            for q in range(2):
                                o = MI[:, q * P:(q + 1) * P]
                                nc.tensor.matmul(o, xw1[:, q * P:(q + 1) * P], wv1[:, :], start=True,
                                                 stop=False)
                                last = nc.tensor.matmul(o, ones[0:1, :], rows[0:1, 0:D], start=False, stop=True)
                            last.then_inc(mi_full, 1)
                        elif name[:2] in ("q0", "k0"):
                            if not begun:
                                pe.wait_ge(xw0_ready, 1)
                            w = wk0[:, :] if name == "k0" else wq0[:, int(name[-1]), :]
                            nc.tensor.matmul(MI, w, mqa.xw[:, :], start=True, stop=True).then_inc(mi_full, 1)
                        elif name == "v0":
                            for t in range(CT):
                                last = nc.tensor.matmul(MI[:, t * DH:(t + 1) * DH],
                                                        mqa.xw[:, t * P:(t + 1) * P], wv0[:, :],
                                                        start=True, stop=True)
                            last.then_inc(mi_full, 1)
                        elif name[:2] == "m_":
                            v = int(name[-1])
                            pe.wait_ge(row_max, 4 * v + 4)
                            for q in range(2):
                                last = nc.tensor.transpose(MI[:, q * P:(q + 1) * P], mqa.mx[:, v % 2, q, :],
                                                           ident[:, :])
                            last.then_inc(mi_full, 1)
                        elif name[:2] in ("o0", "o1"):
                            q = int(name[-1])
                            if name == "o1_0":
                                pe.wait_ge(o_taken, 1)
                            if name == "o0_0" and own_tail:
                                pe.wait_ge(o_taken, odd_before((0, L0_PAIRS - 1)) + 1)
                            ot = ot1 if name[1] == "1" else mqa.ot[:, q // 2]
                            q = q % 2
                            tiles_turned(lambda j: ot[:, j, q * P:(q + 1) * P])
                        elif name == "att1":
                            pe.wait_ge(att1_ready, 2)
                            for q in range(2):
                                last = nc.tensor.transpose(MI[:, q * P:(q + 1) * P], att1[:, q, :],
                                                           ident[:, :])
                            last.then_inc(mi_full, 1)
                        elif name == "y1":
                            for q in range(2):
                                o = MI[:, q * P:(q + 1) * P]
                                nc.tensor.matmul(o, attT[:, q * P:(q + 1) * P], wo1[:, :], start=True,
                                                 stop=False)
                                last = nc.tensor.matmul(o, ones[0:1, :], rows[0:1, D:2 * D], start=False,
                                                        stop=True)
                            last.then_inc(mi_full, 1)
                        elif name == "ffn":
                            if is_a:
                                pe.wait_ge(acc_taken, 1)
                            fs = mqa.fs if is_a else moe.fs
                            tiles_turned(lambda t: fs[:, t * P:(t + 1) * P])
                        elif name == "ln":
                            pe.wait_ge(xn_ready, CT)
                            tiles_turned(lambda t: mqa.xn[:, t, :])
                        elif name == "logits":
                            for t in range(CT):
                                last = nc.tensor.matmul(MI[:, t * NE1:(t + 1) * NE1],
                                                        mqa.xtn[:, t * P:(t + 1) * P], rw1[:, :],
                                                        start=True, stop=True)
                            last.then_inc(mi_full, 1)
                        elif name == "masks":
                            pe.wait_ge(route, 1)
                            for t in range(CT):
                                last = nc.tensor.transpose(MI[0:NE1, t * P:(t + 1) * P],
                                                           mqa.mw[:, t, 0:NE1], ident[:, :])
                            last.then_inc(mi_full, 1)
                        elif name == "total":
                            pe.wait_ge(rsum_ready, 1)
                            nc.tensor.matmul(MI[:, 0:16], ones[:, :], moe.rsum[:, :], start=True, stop=True
                                             ).then_inc(mi_full, 1)

                    def begin_next():
                        scores1(ROUNDS)

                    downs, unmultiplied = 0, None
                    for r in range(n_rounds):
                        last_turned = ((1, r - 1) if cur and r else None) or (
                            (1, -1) if prev_is and r == 0 else None)
                        if is_f[r]:
                            for k, t in steps_of(r):
                                up(t)
                                if last_turned and k in (0, 2):
                                    turn(last_turned, k // 2)
                                while downs < (t - 1 if cur and k == 4 else t - 4):
                                    down(downs)
                                    downs += 1
                                if last_turned and k == 4:
                                    values(last_turned)
                                if cur and k == min(5, n_steps[r] - 1):
                                    scores1(r + 1)
                                if (r, k) in placed:
                                    shared(placed[r, k])
                        elif is_a:
                            if r == F_ROUNDS:
                                for t in range(downs, TILES0):
                                    down(t)
                                pe.wait_ge(w_in, 16)
                                nc.tensor.matmul(ACC, mqa.b2[:, :], mqa.gt, start=False, stop=True
                                                 ).then_inc(down_done, 1)
                                scores0(0)
                                shared("ffn")
                                scores0(1)
                                scores0(2)
                                shared("m_0")
                                scores0(3)
                            for k, u in steps_of(r):
                                if u + LEAD < L0_PAIRS:
                                    scores0(u + LEAD)
                                if u % 2 == 0 and u + 2 < L0_PAIRS:
                                    shared(f"m_{u // 2 + 1}")
                                scores0_turned(u)
                                if cur and k in (2, 3):
                                    turn((1, r - 1), k - 2)
                                if u:
                                    values((0, u - 1))
                                if cur and k == 2 and r < ROUNDS - 1:
                                    scores1(r + 1)
                                if cur and k == 4:
                                    values((1, r - 1))
                                if (r, k) in placed:
                                    shared(placed[r, k])
                            if r == ROUNDS - 1:
                                if cur and n_steps[r] <= 4:
                                    values((1, r - 1))
                                values((0, L0_PAIRS - 1))
                                if own_tail:
                                    for name in in_tail:
                                        shared(name)
                                    shared("qkn")
                                begin_next()
                        else:
                            for k, t in steps_of(r):
                                if is_b:
                                    gate1(t)
                                if is_b:
                                    up1(t)
                                    if t:
                                        down1(t - 1)
                                if unmultiplied and k == 0:
                                    values(unmultiplied)
                                    unmultiplied = None
                                if last_turned and k in (2, 3):
                                    turn(last_turned, k - 2)
                                    unmultiplied = last_turned if k == 3 else None
                                if cur and k == 3 and r < ROUNDS - 1:
                                    scores1(r + 1)
                                if (r, k) in placed:
                                    shared(placed[r, k])
                                if is_m and (r, k) == (6, 0):
                                    shared("total")
                                if nxt_is and (r, k) == (ROUNDS - 1, 0):
                                    shared("qkn")
                                if nxt_is and (r, k) == (ROUNDS - 1, 3):
                                    begin_next()
                            if r == ROUNDS - 1 and unmultiplied:
                                values(unmultiplied)
                    if is_b:
                        down1(TILES1 - 1)
                    if phase == "E":
                        turn((1, -1), 0)
                        turn((1, -1), 1)
                        values((1, -1))
                        for name in uses:
                            shared(name)

                @blk.scalar
                def _(act):
                    def gelu(t):
                        act.wait_ge(up_done, t + 1)
                        if t >= 6:
                            act.wait_ge(down_done, t - 5)
                        nc.scalar.activation(mqa.hb[:, t % 6, :], ps[:, B_H0 + t % 2, :], ACT.Gelu,
                                             bias=mqa.b1[:, t:t + 1]).then_inc(act_done, 1)

                    def silu(t):
                        act.wait_ge(up_done, 2 * t + 1)
                        if t >= 2:
                            act.wait_ge(gated, t - 1)
                        nc.scalar.activation(moe.sg[:, t % 2, :], ps[:, B_H0, :], ACT.Silu
                                             ).then_inc(act_done, 1)

                    def exp1(n):
                        act.wait_ge(neg_max1, n + 1)
                        act.wait_ge(top_taken, 16 * n + 4)
                        if n >= 2:
                            act.wait_ge(turned, 2 * turn_order.index((1, n - 2)) + 2)
                        elif n == 1 and prev_is:
                            act.wait_ge(turned, 2)
                        for m, (b, c, w) in enumerate(tiles1):
                            last = nc.scalar.activation(e1[:, n % 2, b, c:c + w], S1[:, b, c:c + w], ACT.Exp,
                                                        bias=nm1[:, n % 2, m:m + 1], scale=SCALE)
                        last.then_inc(exp1_done, 1)

                    def exp0(u):
                        if u >= 2:
                            act.wait_ge(pv_done, order.index((0, u - 2)) + 1)
                        for h in (2 * u, 2 * u + 1):
                            act.wait_ge(scored0_t, h + 1)
                            nc.scalar.activation(mqa.e[:, u % 2, h % 2, :], ps[:, slots.index(("X", h)) % 3, :],
                                                 ACT.Exp, scale=SCALE).then_inc(exp0_done, 1)

                    def empty(pair, b):
                        k = turn_order.index(pair)
                        act.wait_ge(turned, 2 * k + b + 1)
                        if k >= 2:
                            act.wait_ge(pv_done, order.index(turn_order[k - 2]) + 1)
                        nc.scalar.activation(pts[:, k % 2, b, :], PT[:, 0:W1C], ACT.Copy
                                             ).then_inc(pts_ready, 1)

                    def output(pair):
                        layer, n = pair
                        if n % 2 == 0:
                            return
                        act.wait_ge(pv_done, order.index(pair) + 1)
                        j = (n % ROUNDS) // 2
                        if layer == 1 and n == 1 and prev_is:
                            act.wait_ge(mi_full, uses.index("o1_1") + 1)
                        dst = ot1[:, j, :] if layer == 1 else mqa.ot[:, n // ROUNDS, j, :]
                        nc.scalar.activation(dst, OB[layer], ACT.Copy).then_inc(o_taken, 1)

                    def project(name, j=None):
                        bank_full(act, name)
                        parts_free(act, name)
                        if j is not None:
                            for m in range(2):
                                c = slice(m * SEQ, (m + 1) * SEQ)
                                nc.scalar.activation(high[:, c], MI[:, c], ACT.Identity,
                                                     bias=cols_lo[:, m, j:j + 1], scale=parts[:, m:m + 1])
                                last = nc.scalar.activation(full[:, c], MI[:, c], ACT.Identity,
                                                            bias=cols[:, m, j:j + 1])
                        else:
                            m = 1 if name == "k0" else 0
                            nc.scalar.activation(high[:, :], MI, ACT.Copy, scale=parts[:, m:m + 1])
                            last = nc.scalar.activation(full[:, :], MI, ACT.Identity,
                                                        bias=parts[:, 2:3] if m else 0.0)
                        last.then_inc(mi_free, 1)
                        act.wait_ge(mi_free, uses.index(name) + 1)
                        nc.scalar.sem_inc(proj_ready, 1)

                    def tokens_next():
                        if is_a and has_tail:
                            act.wait_ge(kept, 1)
                        nc.scalar.activation(xw1[:, :], xT[:, bass.ds(nxt, SEQ)], ACT.Copy
                                             ).then_inc(xw1_ready, 1)

                    def shared(name):
                        if name == "qkn":
                            if cur:
                                act.wait_ge(scored1, ROUNDS - 1)
                            project(name, 0)
                        elif name[:3] == "qk1":
                            project(name, int(name[-1]))
                        elif name[:2] in ("q0", "k0"):
                            project(name)
                        elif name == "v1":
                            bank_full(act, name)
                            if prev_is:
                                act.wait_ge(pv_done, 1)
                            nc.scalar.activation(vx1[:, :, :, 0:DH],
                                                 MI[:, 0:SEQ].rearrange("p (q h d) -> p q h d", q=2, d=DH),
                                                 ACT.Copy).then_inc(mi_free, 1)
                            act.wait_ge(mi_free, uses.index(name) + 1)
                            nc.scalar.sem_inc(v1_ready, 1)
                        elif name == "v0":
                            bank_full(act, name)
                            nc.scalar.activation(mqa.vx[:, :, :, 0:DH],
                                                 MI[:, 0:CT * DH].rearrange("p (s q d) -> p s q d", s=2, d=DH),
                                                 ACT.Copy).then_inc(mi_free, 1)
                            act.wait_ge(mi_free, uses.index(name) + 1)
                            nc.scalar.sem_inc(v0_ready, 1)
                        elif name == "att1":
                            bank_full(act, name)
                            nc.scalar.activation(attT[:, :], MI[:, 0:SEQ], ACT.Copy).then_inc(mi_free, 1)
                        elif name == "y1":
                            bank_full(act, name)
                            nc.scalar.activation(s_tiles(prev), MI[:, 0:SEQ].rearrange("p (q d) -> p q d", d=D),
                                                 ACT.Copy).then_inc(mi_free, 1)
                        elif name == "ffn":
                            bank_full(act, name)
                            dst = mqa.g0[:, :, :].rearrange("p t d -> p (t d)") if is_a else (
                                xT[:, bass.ds(ffn_of * CH, CH)])
                            nc.scalar.activation(dst, MI, ACT.Silu).then_inc(mi_free, 1)
                        elif name == "ln":
                            bank_full(act, name)
                            nc.scalar.activation(mqa.xtn, MI, ACT.Copy).then_inc(mi_free, 1)
                            act.wait_ge(mi_free, uses.index(name) + 1)
                            nc.scalar.activation(xT[:, bass.ds(tail * CH, CH)], mqa.xtn, ACT.Copy
                                                 ).then_inc(kept, 1)
                        elif name == "masks":
                            bank_full(act, name)
                            nc.scalar.activation(mqa.mkT, MI[0:NE1, :], ACT.Copy).then_inc(mi_free, 1)
                            act.wait_ge(mi_free, uses.index(name) + 1)
                            nc.scalar.sem_inc(mask_t, 1)

                    def tail_std():
                        act.wait_ge(aggr, CT)
                        nc.scalar.activation(mqa.std[:, :], mqa.mv[:, :, 1], ACT.Sqrt, bias=epsb[:, :]
                                             ).then_inc(std_done, 1)

                    def tail_exp():
                        act.wait_ge(lg_dif, 1)
                        nc.scalar.activation(mqa.ex[:, :, :], mqa.dif[:, :, :], ACT.Exp).then_inc(lg_exp, 1)

                    for r in range(n_rounds):
                        last_turned = ((1, r - 1) if cur and r else None) or (
                            (1, -1) if prev_is and r == 0 else None)
                        if is_f[r]:
                            for k, t in steps_of(r):
                                gelu(t)
                                if last_turned and k in (1, 2):
                                    empty(last_turned, k - 1)
                                if has_tail and cur and (r, k) == std_at:
                                    tail_std()
                                if cur and k == 2:
                                    exp1(r)
                                if has_tail and cur and (r, k) == exp_at:
                                    tail_exp()
                                if last_turned and k == min(5, n_steps[r] - 1):
                                    output(last_turned)
                                if (r, k) in placed:
                                    shared(placed[r, k])
                        elif is_a:
                            if r == F_ROUNDS:
                                act.wait_ge(split0, len(of_layer0))
                                for g in range(NG):
                                    e = max(e for e in range(NE0) if e % 4 == g)
                                    act.wait_ge(gated, 2 * e + 2)
                                    nc.scalar.activation(mqa.kg[g], mqa.k[:, :].bitcast(F32), ACT.Copy,
                                                         scale=group[:, g:g + 1]).then_inc(k_ready, 1)
                                shared("ffn")
                            for k, u in steps_of(r):
                                exp0(u)
                                if cur and k in (2, 3):
                                    empty((1, r - 1), k - 2)
                                if u:
                                    output((0, u - 1))
                                if cur and k == 4:
                                    output((1, r - 1))
                                if cur and k == 0:
                                    exp1(r)
                                if (r, k) in placed:
                                    tokens_next()
                                    shared(placed[r, k])
                            if r == ROUNDS - 1:
                                if cur and n_steps[r] <= 4:
                                    output((1, r - 1))
                                output((0, L0_PAIRS - 1))
                                if own_tail:
                                    tail_std()
                                    shared("ln")
                                    tail_exp()
                                    shared("masks")
                                    tokens_next()
                                    shared("qkn")
                        else:
                            if nxt_is and r == ROUNDS - 1:
                                tokens_next()
                            for k, t in steps_of(r):
                                if is_b:
                                    silu(t)
                                if has_tail and (r, k) == std_at:
                                    tail_std()
                                if cur and k == 2:
                                    exp1(r)
                                if has_tail and (r, k) == exp_at:
                                    tail_exp()
                                if last_turned and k in (2, 3):
                                    empty(last_turned, k - 2)
                                if cur and k == 0 and r > 1:
                                    output((1, r - 2))
                                if prev_is and (r, k) == (1, 0):
                                    output((1, -1))
                                if (r, k) in placed:
                                    shared(placed[r, k])
                                if nxt_is and (r, k) == (ROUNDS - 1, 0):
                                    shared("qkn")
                                if is_m and r == ROUNDS - 1:
                                    if k == 0:
                                        act.wait_ge(w_in, 16)
                                        act.wait_ge(mean_ready, 4)
                                    for e in (2 * k, 2 * k + 1):
                                        w = moe.down[:, e * PER_E1:(e + 1) * PER_E1, :]
                                        nc.scalar.activation(w, w, ACT.Copy, scale=moe.mean[:, e:e + 1])
                            if is_m:
                                act.wait_ge(stage_in[r % 2], 16 * (r // 2 + 1))
                                dst = moe.ghi if r < 4 else moe.uhi
                                nc.scalar.activation(dst[:, (r % 4) * 1024:(r % 4 + 1) * 1024],
                                                     moe.stage[:, r % 2, :], ACT.Copy).then_inc(high_ready, 1)
                    if phase == "E":
                        empty((1, -1), 0)
                        empty((1, -1), 1)
                        output((1, -1))
                        for name in uses:
                            shared(name)

                @blk.vector
                def _(dve):
                    def gated_tile(t):
                        dve.wait_ge(act_done, t + 1)
                        dve.wait_ge(up_done, 2 * t + 2)
                        if t >= 2:
                            dve.wait_ge(down_done, t - 1)
                        nc.vector.tensor_tensor(moe.h[:, t % 2, :], moe.sg[:, t % 2, :], ps[:, B_H1, :],
                                                ALU.mult).then_inc(gated, 1)

                    def max0(u):
                        for h in (2 * u, 2 * u + 1):
                            dve.wait_ge(scored0, h + 1)
                            g = 2 * (u % 2) + h % 2
                            nc.vector.reduce_max(mqa.mx[:, u // 2 % 2, :, 32 * g + R_MAX],
                                                 ps[:, slots.index(("M", h)) % 3, :].rearrange(
                                                     "p (q k) -> p q k", k=SEQ), AX_X).then_inc(row_max, 1)

                    def take_off(v):
                        bank_full(dve, f"m_{v}")
                        s, j = v // HG, v % HG
                        q = mqa.q[:, j, s * SEQ:(s + 1) * SEQ]
                        nc.vector.scalar_tensor_tensor(out=q, in0=MI[:, 0:SEQ], scalar=parts[:, 3:4],
                                                       in1=q.bitcast(F32), op0=ALU.mult, op1=ALU.add
                                                       ).then_inc(max_off, 1)
                        dve.wait_ge(max_off, v + 1)
                        nc.vector.sem_inc(mi_free, 1)

                    def search(n, piece):
                        if not cur:
                            return
                        k = piece // 2
                        found = 16 * n + 4 * k
                        if piece == 0 and n:
                            dve.wait_ge(scored1, n)
                            if n >= 2:
                                numerators_ready(dve, n - 2)
                        for m, (b, c, w) in enumerate(tiles1):
                            src = S1[:, b, c:c + w] if k == 0 else xr[:, n % 2, b, c:c + w]
                            if piece % 2 == 0:
                                if k:
                                    dve.wait_ge(top_taken, found - 4 + m + 1)
                                nc.vector.max(top8[:, n % 2, k, m, :], src).then_inc(top_found, 1)
                            else:
                                dve.wait_ge(top_found, found + m + 1)
                                nc.vector.match_replace(xr[:, n % 2, b, c:c + w], top8[:, n % 2, k, m, :],
                                                        src, TAKEN).then_inc(top_taken, 1)
                        if piece == 0:
                            dve.wait_ge(top_found, found + 4)
                            nc.vector.tensor_scalar(nm1[:, n % 2, :], top8[:, n % 2, 0, :, 0], -SCALE, None,
                                                    ALU.mult).then_inc(neg_max1, 1)
                        if piece == 7 and n not in by_pool:
                            dve.wait_ge(top_taken, 16 * n + 16)
                            dve.wait_ge(exp1_done, n + 1)
                            last = nc.vector.scalar_tensor_tensor(out=e1[:, n % 2], in0=xr[:, n % 2],
                                                                  scalar=IS_TAKEN, in1=e1[:, n % 2],
                                                                  op0=ALU.is_lt, op1=ALU.mult)
                            if n < ROUNDS - 1:
                                last.then_inc(p_ready, 1)

                    def heads_out(name, dst, att_ready):
                        o = MI.rearrange("p (j g e) -> p j g e", j=HG, g=NG)
                        n = int(name[-1])
                        done = outputs.index(name)
                        bank_full(dve, name)
                        if done:
                            dve.wait_ge(rc_used, done)
                        rc = rc1[:, :].rearrange("p (j g) -> p j g", j=HG)
                        nc.vector.reciprocal(rc, o[:, :, :, DH]).then_inc(rc_ready, 1)
                        dve.wait_ge(rc_ready, done + 1)
                        nc.vector.tensor_tensor(dst.rearrange("p (g j d) -> p j g d", g=NG, j=HG),
                                                o[:, :, :, 0:DH],
                                                rc.unsqueeze(3).broadcast_to([P, HG, NG, DH]),
                                                ALU.mult).then_inc(att_ready, 1)
                        dve.wait_ge(att_ready, n + 1)
                        nc.vector.sem_inc(rc_used, 1)
                        nc.vector.sem_inc(mi_free, 1)

                    def shared(name):
                        q = int(name[-1]) if name in outputs else None
                        if name[:2] == "o1":
                            heads_out(name, att1[:, q, :], att1_ready)
                        if name[:2] == "o0":
                            heads_out(name, mqa.att[:, q, :], att0_ready)
                        if name == "o0_3":
                            tail_residual()
                        if name == "logits":
                            tail_choice()
                        if name in of_layer0:
                            n = of_layer0.index(name)
                            dve.wait_ge(proj_ready, projections.index(name) + 1)
                            dst = mqa.k[:, :] if name == "k0" else mqa.q[:, n, :]
                            nc.vector.tensor_tensor(dst, full[:, :], high[:, :].bitcast(F32), ALU.subtract
                                                    ).then_inc(split0, 1)

                    def tail_residual():
                        x_tiles = xall[:, bass.ds(tail * CT, CT), :]
                        dve.wait_ge(att0_ready, CT)
                        nc.vector.tensor_tensor(mqa.g0[:, :, :], mqa.g0[:, :, :], mqa.att[:, :, :],
                                                ALU.mult).then_inc(silu_done, 1)
                        dve.wait_ge(silu_done, 1)
                        nc.vector.tensor_tensor(x_tiles, x_tiles, mqa.g0[:, :, :], ALU.add).then_inc(resid, 1)
                        dve.wait_ge(resid, 1)
                        for t in range(CT):
                            nc.vector.bn_stats(mqa.bs[:, t, :], x_tiles[:, t, :]).then_inc(stats, 1)
                        for t in range(CT):
                            dve.wait_ge(stats, t + 1)
                            nc.vector.bn_aggr(mqa.mv[:, t, :], mqa.bs[:, t, :]).then_inc(aggr, 1)

                    def tail_norm():
                        x_tiles = xall[:, bass.ds(tail * CT, CT), :]
                        dve.wait_ge(std_done, 1)
                        nc.vector.reciprocal(mqa.rstd[:, :], mqa.std[:, :]).then_inc(rstd_done, 1)
                        dve.wait_ge(rstd_done, 1)
                        for t in range(CT):
                            nc.vector.tensor_scalar(mqa.xn[:, t, :], x_tiles[:, t, :],
                                                    mqa.mv[:, t, 0:1], mqa.rstd[:, t:t + 1],
                                                    ALU.subtract, ALU.mult).then_inc(xn_ready, 1)

                    def tail_choice():
                        bank_full(dve, "logits")
                        nc.vector.tensor_copy(mqa.lg[:, :, 0:NE1],
                                              MI[:, 0:CT * NE1].rearrange("p (t e) -> p t e", e=NE1)
                                              ).then_inc(lg_ready, 1)
                        dve.wait_ge(lg_ready, 1)
                        nc.vector.sem_inc(mi_free, 1)
                        for t in range(CT):
                            nc.vector.max(mqa.l8[:, t, :], mqa.lg[:, t, :]).then_inc(lg_max, 1)
                        dve.wait_ge(lg_max, CT)
                        nc.vector.tensor_tensor(mqa.dif[:, :, :], mqa.lg[:, :, 0:NE1],
                                                mqa.l8[:, :, 0:1].broadcast_to([P, CT, NE1]),
                                                ALU.subtract).then_inc(lg_dif, 1)
                        nc.vector.tensor_copy(mqa.rep[:, :, 0:2], mqa.l8[:, :, 0:2]).then_inc(lg_ready, 1)
                        dve.wait_ge(lg_ready, 2)
                        for t in range(CT):
                            nc.vector.match_replace(mqa.lt[:, t, :], mqa.rep[:, t, :], mqa.lg[:, t, :],
                                                    TAKEN).then_inc(lg_taken, 1)
                        dve.wait_ge(lg_taken, CT)
                        nc.vector.tensor_scalar(mqa.mw[:, :, 0:NE1], mqa.lt[:, :, 0:NE1], IS_TAKEN, None,
                                                ALU.is_lt).then_inc(route, 1)

                    def tail_weights():
                        dve.wait_ge(route, 1)
                        dve.wait_ge(lg_exp, 1)
                        nc.vector.tensor_tensor(mqa.dif[:, :, :], mqa.mw[:, :, 0:NE1], mqa.ex[:, :, :],
                                                ALU.mult).then_inc(route, 1)
                        dve.wait_ge(route, 2)
                        nc.vector.reduce_sum(mqa.ws[:, :], mqa.dif[:, :, :], AX_X).then_inc(route, 1)
                        dve.wait_ge(route, 3)
                        nc.vector.reciprocal(mqa.rw[:, :], mqa.ws[:, :]).then_inc(route, 1)
                        dve.wait_ge(route, 4)
                        nc.vector.tensor_tensor(mqa.mw[:, :, NE1:2 * NE1], mqa.dif[:, :, :],
                                                mqa.rw[:, :].unsqueeze(2).broadcast_to([P, CT, NE1]),
                                                ALU.mult).then_inc(route, 1)
                        dve.wait_ge(route, 5)
                        nc.vector.tensor_tensor(racc[:, :, :], racc[:, :, :], mqa.mw[:, :, :],
                                                ALU.add).then_inc(route, 1)

                    if is_a and not begun:
                        nc.vector.tensor_copy(mqa.xw[:, :], chunk).then_inc(xw0_ready, 1)
                    def split_tokens(tokens, done):
                        nc.vector.tensor_copy(xhi[:, :], tokens).then_inc(split, 1)
                        dve.wait_ge(split, done + 1)
                        nc.vector.tensor_tensor(xlo[:, :], tokens, xhi[:, :].bitcast(F32), ALU.subtract
                                                ).then_inc(split, 1)

                    if (is_a or is_b) and not begun:
                        split_tokens(chunk, 0)
                    for r in range(n_rounds):
                        done = 0
                        if is_a and r == F_ROUNDS:
                            for done in range(EARLY):
                                search(r, done)
                            done = EARLY
                            dve.wait_ge(down_done, TILES0 + 1)
                            nc.vector.tensor_tensor(mqa.fs[:, :], ACC, mqa.xw[:, :], ALU.add
                                                    ).then_inc(acc_taken, 1)
                            max0(0)
                            max0(1)
                            max0(2)
                            take_off(0)
                            max0(3)
                        steps = steps_of(r)
                        for k, t in steps:
                            if is_a and not is_f[r] and t + LEAD < L0_PAIRS:
                                max0(t + LEAD)
                            upto = max(done, -(-8 * (k + 1) // len(steps)))
                            for piece in range(done, upto):
                                search(r, piece)
                            done = upto
                            if is_a and not is_f[r] and t % 2 == 0 and t + 2 < L0_PAIRS:
                                take_off(t // 2 + 1)
                            if is_b:
                                gated_tile(t)
                            if (r, k) in placed:
                                shared(placed[r, k])
                            if has_tail and not own_tail and (r, k) == std_at:
                                tail_norm()
                            if has_tail and not own_tail and (r, k) == (exp_at[0], exp_at[1] + 1):
                                tail_weights()
                        if own_tail and r == ROUNDS - 1:
                            for q in range(CT):
                                shared(f"o0_{q}")
                            tail_norm()
                            tail_choice()
                            tail_weights()
                        if is_m and r == 5:
                            dve.wait_ge(route, 6)
                            nc.vector.reduce_sum(moe.rsum[:, :], racc[:, :, :].rearrange("p t e -> p e t"),
                                                 AX_X).then_inc(rsum_ready, 1)
                        if is_m and r == 6:
                            bank_full(dve, "total")
                            nc.vector.tensor_copy(moe.tot[:, :], MI[:, 0:16]).then_inc(mean_ready, 1)
                            dve.wait_ge(mean_ready, 1)
                            nc.vector.sem_inc(mi_free, 1)
                            nc.vector.tensor_scalar(moe.cnt[:, :], moe.tot[:, 0:NE1], 1.0, None, ALU.max
                                                    ).then_inc(mean_ready, 1)
                            dve.wait_ge(mean_ready, 2)
                            nc.vector.reciprocal(moe.rcnt[:, :], moe.cnt[:, :]).then_inc(mean_ready, 1)
                            dve.wait_ge(mean_ready, 3)
                            nc.vector.tensor_tensor(moe.mean[:, :], moe.tot[:, NE1:2 * NE1], moe.rcnt[:, :],
                                                    ALU.mult).then_inc(mean_ready, 1)
                    if ahead and is_a:
                        dve.wait_ge(mi_full, uses.index("ffn") + 1)
                        following = xT[:, bass.ds(tok0 + CH, CH)]
                        nc.vector.tensor_copy(mqa.xw[:, :], following)
                        split_tokens(following, 0 if begun else 2)
                    if ahead and is_b:
                        dve.wait_ge(masked, masks_done(NE1 - 1))
                        done = 0 if begun else 2
                        split_tokens(xT[:, bass.ds(tok0 + CH, CH)], done)
                        dve.wait_ge(split, done + 2)
                        dve.wait_ge(gate_in[0], masks_in(NE1))
                        for src, dst in ((xhi, moe.xmhi), (xlo, moe.xmlo)):
                            nc.vector.tensor_tensor(dst[:, 0, :], src[:, :].bitcast(F32), moe.mask[0], ALU.mult)
                    if is_b:
                        dve.wait_ge(down_done, TILES1)
                        if ffn_of is not None:
                            dve.wait_ge(mi_full, 1)
                        nc.vector.tensor_copy(moe.fs, ACC).then_inc(acc_taken, 1)
                    if phase == "E":
                        for name in uses:
                            shared(name)
                        dve.wait_ge(mi_free, len(uses))
                        finish(dve, nc.vector, slice((NCH - 1) * CT, NCH * CT))

                @blk.gpsimd
                def _(pool):
                    def gate(t):
                        e = (t - T_SH) // 2
                        pool.wait_ge(act_done, t + 1)
                        pool.wait_ge(gate_in[e % 4], 16 * (e // 4 + 1))
                        h = mqa.hb[:, t % 6, :]
                        nc.gpsimd.tensor_tensor(h, h, mqa.gate[:, e % 4, :], ALU.mult).then_inc(gated, 1)

                    def mask(e):
                        if e == 0:
                            pool.wait_ge(split, 2)
                        pool.wait_ge(gate_in[e % 2], masks_in(e))
                        if e >= 2:
                            pool.wait_ge(up_done, 2 * PER_E1 * (e - 1))
                        for src, dst in ((xhi, moe.xmhi), (xlo, moe.xmlo)):
                            nc.gpsimd.tensor_tensor(dst[:, e % 2, :], src[:, :].bitcast(F32),
                                                    moe.mask[e % 2], ALU.mult).then_inc(masked, 1)

                    def select(n):
                        pool.wait_ge(top_taken, 16 * n + 16)
                        pool.wait_ge(exp1_done, n + 1)
                        nc.gpsimd.tensor_scalar(xr[:, n % 2], xr[:, n % 2], IS_TAKEN, None, ALU.is_lt
                                                ).then_inc(is_taken, 1)
                        pool.wait_ge(is_taken, n - by_pool[0] + 1)
                        nc.gpsimd.tensor_tensor(e1[:, n % 2], e1[:, n % 2], xr[:, n % 2], ALU.mult
                                                ).then_inc(p_ready_late, 1)

                    def split_parts(name):
                        pool.wait_ge(proj_ready, projections.index(name) + 1)
                        j = 0 if name == "qkn" else int(name[-1])
                        for m, dst in enumerate((q1, k1)):
                            c = slice(m * SEQ, (m + 1) * SEQ)
                            nc.gpsimd.tensor_tensor(dst[:, j, :], full[:, c], high[:, c].bitcast(F32), ALU.subtract
                                                    ).then_inc(split1, 1)

                    if is_b and not begun:
                        mask(0)
                    if is_b and ffn_of is not None:
                        finish(pool, nc.gpsimd, bass.ds(ffn_of * CT, CT))
                    for r in range(n_rounds):
                        if is_a and is_f[r]:
                            for k, t in steps_of(r):
                                if (r, k) in placed and placed[r, k] in of_layer1:
                                    split_parts(placed[r, k])
                                if t >= T_SH:
                                    gate(t)
                        elif not is_a:
                            if is_b and r + 1 < NE1:
                                mask(r + 1)
                            for k, _ in steps_of(r):
                                if placed.get((r, k)) in of_layer1:
                                    split_parts(placed[r, k])
                        if nxt_is and r == ROUNDS - 1:
                            split_parts("qkn")
                        if is_m:
                            pool.wait_ge(high_ready, r + 1)
                            hi, lo = (moe.ghi, moe.glo) if r < 4 else (moe.uhi, moe.ulo)
                            c = slice((r % 4) * 1024, (r % 4 + 1) * 1024)
                            nc.gpsimd.tensor_tensor(lo[:, c], moe.stage[:, r % 2, :],
                                                    hi[:, c].bitcast(F32), ALU.subtract).then_inc(split, 1)
                        if cur and r in by_pool:
                            select(r)

        def s_tiles(seq0):
            return sall[:, :, :].rearrange("p t d -> p (t d)")[:, bass.ds(seq0, SEQ)
                                                               ].rearrange("p (q d) -> p q d", d=D)

        class Bufs:
            pass

        phase_a = ExitStack()
        mqa = Bufs()
        mqa.ot = sb("ot0", [P, 2, HG, SEQ])
        mqa.att = sb("att0", [P, CT, D])
        mqa.g0 = sb("g0", [P, CT, D])
        by_expert = sb("by_expert", [64, CH])
        mqa.gt = by_expert[0:16, :]
        mqa.mkT = by_expert[32:32 + NE1, :]
        mqa.xn = mqa.g0
        mqa.xtn = mqa.att[:, :, :].rearrange("p t d -> p (t d)")
        mqa.bs = sb("bs1", [P, CT, 6])
        mqa.mv = sb("mv1", [P, CT, 2])
        mqa.std = sb("std1", [P, CT])
        mqa.rstd = sb("rstd1", [P, CT])
        mqa.l8 = sb("l81", [P, CT, 8])
        mqa.lt = sb("lt1", [P, CT, NE1 + 6])
        mqa.dif = sb("dif1", [P, CT, NE1])
        mqa.ex = sb("ex1", [P, CT, NE1])
        mqa.ws = sb("ws1", [P, CT])
        mqa.rw = sb("rwt1", [P, CT])
        mqa.mw = sb("mw1", [P, CT, 16])
        mqa.lg = sb("lg1", [P, CT, NE1 + 6])
        mqa.rep = sb("rep1", [P, CT, 8])

        def sa(name, shape, dt=F32):
            return sb(name, shape, dt, phase_a)

        mqa.w1hi = sa("w1hi", [P, TILES0 * P], F32R)
        mqa.w1lo = sa("w1lo", [P, TILES0 * P], F32R)
        mqa.w2 = sa("w2", [P, TILES0, D])
        wk0 = sa("wk0", [P, P])
        wv0 = sa("wv0", [P, DH])
        mqa.b1 = sa("b1", [P, TILES0])
        mqa.b2 = sa("b2", [16, D])
        mqa.vx = sa("vx0", [P, 2, 2, 32])
        mqa.mx = sa("mx0", [P, 2, 2, P])

        prologue = ExitStack()

        def sp_(name, shape, dt=F32):
            return sb(name, shape, dt, prologue)

        raw = sp_("raw", [P, TILES0 * P])
        cst = sp_("cst", [P, P])
        gw0 = sp_("gw0", [P, NE0])
        gb0 = sp_("gb0", [P, NE0])
        bs = sp_("bs", [P, NT, 6])
        mv = sp_("mv", [P, NT, 2])
        std = sp_("std", [P, NT])
        rstd = sp_("rstd", [P, NT])
        xn = mqa.ot[:, 0, :, :].rearrange("p (n j) (t d) -> p n (j t) d", n=2, d=D)
        lg = sp_("lg", [P, NT, NE0 + 5])
        lt = sp_("lt", [P, NT, NE0 + 5])
        l8 = sp_("l8", [P, NT, 8])
        rep = sp_("rep", [P, NT, 8])
        dif = sp_("dif", [P, NT, NE0])
        ex = sp_("ex", [P, NT, NE0])
        ws = sp_("ws", [P, NT])
        rw = sp_("rw", [P, NT])
        gates = sp_("gates", [P, NT, 16])
        gT = raw[0:16, 0:NTOK]
        XP = NT // 4
        first_weights = [(ident[:, :], A["ident"]), (gw0[:, :], A["gw0"]),
                         (gb0[:, :], A["gb0"].broadcast_to([P, NE0]))]
        weights = [(cst[:, :], A["causal"]), (parts[:, :], A["parts"]), (group[:, :], A["group"]),
                   (wq0[:, :, :], A["wq0"]), (wk0[:, :], A["wk0"]), (wv0[:, :], A["wv0"]),
                   (wq1[:, :, :], A["wq1"]), (wk1[:, :, :], A["wk1"]), (wv1[:, :], A["wv1"]),
                   (wo1[:, :], A["wo1"]), (rows[:, :], A["rows1"]), (cols[:, :, :], A["cols1"]),
                   (rw1[:, :], A["rw1"]), (mqa.b1[:, :], A["b1"]), (mqa.b2[:, :], A["b2"])]
        x_dram = A["x"].rearrange("(t p) d -> p t d", p=P)

        with nc.Block(no_gpsimd_drain=True) as blk:
            @blk.sync
            def _(sp):
                for n in range(4):
                    sp.dma_start(xall[:, n * XP:(n + 1) * XP, :], x_dram[:, n * XP:(n + 1) * XP, :]
                                 ).then_inc(x_in[n], 16)
                sp.dma_start(raw[:, :], A["w1"]).then_inc(stage_in[0], 16)
                sp.dma_start(mqa.w2[:, :, :], A["w2"]).then_inc(stage_in[1], 16)
                sp.wait_ge(stage_in[1], 16)
                sp.wait_ge(kept, 1)
                sp.dma_start(GD[:, :], gT).then_inc(stored, 16)
                sp.wait_ge(stored, 16)

            @blk.scalar
            def _(act):
                for dst, src in first_weights:
                    act.dma_start(dst, src).then_inc(first_in, 16)
                for dst, src in weights:
                    act.dma_start(dst, src).then_inc(w_in, 16)
                act.wait_ge(aggr, NT)
                act.wait_ge(consts, 1)
                nc.scalar.activation(std[:, :], mv[:, :, 1], ACT.Sqrt, bias=epsb[:, :]).then_inc(std_done, 1)
                for q in range(NCH):
                    act.wait_ge(mi_full, q + 1)
                    nc.scalar.activation(xT[:, q * CH:(q + 1) * CH], ps[:, q % 2, :], ACT.Copy
                                         ).then_inc(xt_ready, 1)
                act.wait_ge(stage_in[0], 16)
                nc.scalar.activation(mqa.w1hi[:, :], raw[:, :], ACT.Copy).then_inc(split, 1)
                act.wait_ge(first_in, 16 * len(first_weights))
                act.wait_ge(w_in, 16 * len(weights))
                nc.scalar.activation(ident16[:, :], ident[:, :], ACT.Copy)
                nc.scalar.activation(causal16[:, :], cst[:, :], ACT.Copy)
                for m in range(2):
                    nc.scalar.activation(cols_lo[:, m, :], cols[:, m, :], ACT.Copy, scale=parts[:, m:m + 1])
                act.wait_ge(lg_dif, 1)
                nc.scalar.activation(ex[:, :, :], dif[:, :, :], ACT.Exp).then_inc(lg_exp, 1)
                act.wait_ge(split, 2)
                for n in range(8):
                    act.wait_ge(turned, n + 1)
                    last = nc.scalar.activation(gT[:, n * 512:(n + 1) * 512], ps[0:16, n, :], ACT.Copy)
                last.then_inc(kept, 1)

            @blk.gpsimd
            def _(pool):
                nc.gpsimd.memset(epsb[:, :], EPS)
                nc.gpsimd.memset(ones[:, :], 1.0).then_inc(consts, 1)
                nc.gpsimd.memset(vx1[:, :, :, :], 0.0).then_inc(prep, 1)
                nc.gpsimd.memset(mqa.vx[:, :, :, :], 0.0).then_inc(prep, 1)
                pool.wait_ge(prep, 2)
                nc.gpsimd.memset(vx1[:, :, :, DH:DH + 1], 1.0)
                nc.gpsimd.memset(mqa.vx[:, :, :, DH:DH + 1], 1.0)
                nc.gpsimd.memset(racc[:, :, :], 0.0)
                nc.gpsimd.memset(mqa.mx[:, :, :, :], 0.0)
                nc.gpsimd.memset(mqa.lg[:, :, :], MASKED)
                nc.gpsimd.memset(mqa.rep[:, :, :], MASKED)
                nc.gpsimd.memset(gates[:, :, 15:16], 1.0)
                nc.gpsimd.memset(rep[:, :, :], MASKED)
                nc.gpsimd.memset(lg[:, :, NE0:NE0 + 5], MASKED).then_inc(consts, 1)
                pool.wait_ge(split, 1)
                nc.gpsimd.tensor_tensor(mqa.w1lo[:, :], raw[:, :], mqa.w1hi[:, :].bitcast(F32), ALU.subtract
                                        ).then_inc(split, 1)

            @blk.vector
            def _(dve):
                for t in range(NT):
                    if t % XP == 0:
                        dve.wait_ge(x_in[t // XP], 16)
                    nc.vector.bn_stats(bs[:, t, :], xall[:, t, :]).then_inc(stats, 1)
                for t in range(NT):
                    dve.wait_ge(stats, t + 1)
                    nc.vector.bn_aggr(mv[:, t, :], bs[:, t, :]).then_inc(aggr, 1)
                dve.wait_ge(std_done, 1)
                nc.vector.reciprocal(rstd[:, :], std[:, :]).then_inc(rstd_done, 1)
                dve.wait_ge(rstd_done, 1)
                for t in range(NT):
                    q = t // CT
                    if q >= 2 and t % CT == 0:
                        dve.wait_ge(mi_full, q - 1)
                    nc.vector.tensor_scalar(xn[:, q % 2, t % CT, :], xall[:, t, :], mv[:, t, 0:1],
                                            rstd[:, t:t + 1], ALU.subtract, ALU.mult).then_inc(xn_ready, 1)
                dve.wait_ge(scored1, 1)
                dve.wait_ge(consts, 2)
                dve.wait_ge(first_in, 16 * len(first_weights))
                nc.vector.tensor_tensor(lg[:, :, 0:NE0],
                                        ps[:, 3, :].rearrange("p (t e) -> p t e", e=16)[:, :, 0:NE0],
                                        gb0[:, :].unsqueeze(1).broadcast_to([P, NT, NE0]), ALU.add
                                        ).then_inc(lg_ready, 1)
                dve.wait_ge(lg_ready, 1)
                for t in range(NT):
                    nc.vector.max(l8[:, t, :], lg[:, t, :]).then_inc(lg_max, 1)
                dve.wait_ge(lg_max, NT)
                nc.vector.tensor_tensor(dif[:, :, :], lg[:, :, 0:NE0],
                                        l8[:, :, 0:1].broadcast_to([P, NT, NE0]), ALU.subtract
                                        ).then_inc(lg_dif, 1)
                nc.vector.tensor_copy(rep[:, :, 0:3], l8[:, :, 0:3]).then_inc(lg_ready, 1)
                dve.wait_ge(lg_ready, 2)
                for t in range(NT):
                    nc.vector.match_replace(lt[:, t, :], rep[:, t, :], lg[:, t, :], TAKEN).then_inc(lg_taken, 1)
                dve.wait_ge(lg_exp, 1)
                nc.vector.reduce_sum(ws[:, :], ex[:, :, :], AX_X).then_inc(route, 1)
                dve.wait_ge(route, 1)
                nc.vector.reciprocal(rw[:, :], ws[:, :]).then_inc(route, 1)
                dve.wait_ge(route, 2)
                dve.wait_ge(lg_taken, NT)
                nc.vector.scalar_tensor_tensor(out=dif[:, :, :], in0=lt[:, :, 0:NE0], scalar=IS_TAKEN,
                                               in1=ex[:, :, :], op0=ALU.is_lt, op1=ALU.mult
                                               ).then_inc(route, 1)
                dve.wait_ge(route, 3)
                nc.vector.tensor_tensor(gates[:, :, 0:NE0], dif[:, :, :],
                                        rw[:, :].unsqueeze(2).broadcast_to([P, NT, NE0]), ALU.mult
                                        ).then_inc(route, 1)

            @blk.tensor
            def _(pe):
                pe.wait_ge(first_in, 16 * len(first_weights))
                for q in range(NCH + 2):
                    if q < NCH:
                        pe.wait_ge(xn_ready, CT * (q + 1))
                        if q >= 2:
                            pe.wait_ge(xt_ready, q - 1)
                        for t in range(CT):
                            last = nc.tensor.transpose(ps[:, q % 2, t * P:(t + 1) * P], xn[:, q % 2, t, :],
                                                       ident[:, :])
                        last.then_inc(mi_full, 1)
                    if q >= 2:
                        pe.wait_ge(xt_ready, q - 1)
                        for t in range((q - 2) * CT, (q - 1) * CT):
                            last = nc.tensor.matmul(ps[:, 3, t * 16:t * 16 + NE0], xT[:, t * P:(t + 1) * P],
                                                    gw0[:, :], start=True, stop=True)
                last.then_inc(scored1, 1)
                pe.wait_ge(route, 4)
                pe.wait_ge(consts, 2)
                for t in range(NT):
                    last = nc.tensor.transpose(ps[0:16, t // 4, (t % 4) * P:(t % 4 + 1) * P],
                                               gates[:, t, :], ident[:, :])
                    if t % 4 == 3:
                        last.then_inc(turned, 1)
        clear_semaphores()
        prologue.close()

        mqa.xw = sa("xw0", [P, CH])
        mqa.q = sa("q0", [P, HG, CH], F32R)
        mqa.k = sa("k0", [P, CH], F32R)
        mqa.hb = sa("hb", [P, 6, CH])
        mqa.e = mqa.hb[:, 0:4, :].rearrange("p (n b) k -> p n b k", b=2)
        mqa.gate = sa("gate", [P, 4, CH])
        mqa.kg = [mqa.gate[:, g, :].bitcast(F32R) for g in range(NG)]
        mqa.fs = mqa.xw

        block(0, "A", nxt=0, tail=0, ahead=True)
        clear_semaphores()
        block(1, "A", cur=True, nxt=SEQ, begun=True, ahead=True)
        clear_semaphores()
        with nc.Fori(2, NCH - 1) as i:
            block(i, "A", cur=True, prev=i * SEQ - 2 * SEQ, nxt=i * SEQ, tail=i - 1, begun=True, ahead=True)
            clear_semaphores()
        block(NCH - 1, "A", cur=True, prev=(NCH - 3) * SEQ, nxt=(NCH - 1) * SEQ, tail=NCH - 2, begun=True)
        clear_semaphores()
        phase_a.close()

        moe = Bufs()
        moe.ghi = sb("ghi", [P, TILES1 * P], F32R)
        moe.glo = sb("glo", [P, TILES1 * P], F32R)
        moe.uhi = sb("uhi", [P, TILES1 * P], F32R)
        moe.ulo = sb("ulo", [P, TILES1 * P], F32R)
        moe.down = sb("down", [P, TILES1, D])
        moe.rsum = sb("rsum", [P, 16])
        moe.tot = sb("tot", [P, 16])
        moe.cnt = sb("cnt", [P, NE1])
        moe.rcnt = sb("rcnt", [P, NE1])
        moe.mean = sb("mean", [P, NE1])
        with ExitStack() as mid:
            moe.stage = sb("stage", [P, 2, 1024], F32, mid)
            block(0, "M", cur=True, prev=(NCH - 2) * SEQ, nxt=NCH * SEQ, tail=NCH - 1)
            clear_semaphores()
        moe.mask = [mqa.att[:, :, :].rearrange("p t d -> p (t d)"), wq0[:, :, :].rearrange("p j k -> p (j k)")]
        moe.xmhi = sb("xmhi", [P, 2, CH], F32R)
        moe.xmlo = sb("xmlo", [P, 2, CH], F32R)
        moe.sg = mqa.ot[:, 0, :, :].rearrange("p (n j) k -> p n (j k)", n=2)
        moe.h = mqa.ot[:, 1, :, :].rearrange("p (n j) k -> p n (j k)", n=2)
        moe.fs = mqa.g0[:, :, :].rearrange("p t d -> p (t d)")
        block(0, "B", cur=True, prev=(NCH - 1) * SEQ, nxt=(NCH + 1) * SEQ, ahead=True)
        clear_semaphores()
        with nc.Fori(1, NCH - 1) as i:
            block(i, "B", cur=True, prev=i * SEQ + (NCH - 1) * SEQ, nxt=i * SEQ + (NCH + 1) * SEQ,
                  ffn_of=i - 1, begun=True, ahead=True)
            clear_semaphores()
        block(NCH - 1, "B", cur=True, prev=(NSEQ - 2) * SEQ, ffn_of=NCH - 2, begun=True)
        clear_semaphores()
        block(0, "E", prev=(NSEQ - 1) * SEQ, ffn_of=NCH - 1)
        clear_semaphores()


def kernel(**inputs):
    import concourse.bacc as _bacc
    from concourse.bass_utils import run_bass_kernel_spmd as _run

    a = {k: np.asarray(v) for k, v in inputs.items()}
    c = np.ascontiguousarray
    key = np.arange(P)
    row = key % 32
    part = key[:, None] * 0 + (row[:, None] // DH == np.array([[R_LO_Q // DH, R_LO_K // DH, R_MAX // DH]]))
    part = part.astype(np.float32)
    part[row != R_MAX, 2] = 0

    def head_rows(w, tiles):
        w = w.reshape(-1, DH, w.shape[-1])
        o = np.zeros((tiles, NG, 32, w.shape[-1]), w.dtype)
        for j in range(tiles):
            for g in range(NG):
                for m in range(3):
                    o[j, g, m * DH:(m + 1) * DH] = w[(HG * g + j) % len(w)]
        return o.reshape(tiles, P, -1).transpose(2, 0, 1)

    host = {
        "x": a["L0_attn_x"].reshape(NTOK, D),
        "ident": np.eye(P, dtype=np.float32),
        "causal": np.where(key[None, :] > key[:, None], np.float32(MASKED), np.float32(0)),
        "group": (key[:, None] // 32 == np.arange(NG)[None, :]).astype(np.float32),
        "parts": np.concatenate([part, 0 - part[:, 2:]], axis=1),
        "gw0": a["L0_ffn_gW"], "gb0": a["L0_ffn_gb"].reshape(1, NE0),
        "wq0": head_rows(a["L0_attn_Wq"], HG), "wk0": head_rows(a["L0_attn_Wk"], 1)[:, 0],
        "wq1": head_rows(a["L1_attn_Wq"], HG), "wk1": head_rows(a["L1_attn_Wk"], HG),
        "wv0": a["L0_attn_Wv"].T, "wv1": a["L1_attn_Wv"].T,
        "wo1": a["L1_attn_Wo"].T,
        "rows1": np.concatenate([a["L1_attn_bv"], a["L1_attn_bo"]]).reshape(1, 2 * D),
        "cols1": np.stack([head_rows(a[n][:, None], HG)[0].T for n in ("L1_attn_bq", "L1_attn_bk")], axis=1),
        "rw1": a["L1_ffn_router_w"].T,
        "b1": np.concatenate([a["L0_ffn_sb1"].reshape(-1), a["L0_ffn_rb1"].reshape(-1)]
                             ).reshape(TILES0, P).T,
        "b2": np.concatenate([a["L0_ffn_rb2"], a["L0_ffn_sb2"]], axis=0),
        "w1": np.concatenate([a["L0_ffn_sW1"].transpose(1, 0, 2).reshape(D, -1),
                              a["L0_ffn_rW1"].transpose(1, 0, 2).reshape(D, -1)], axis=1),
        "w2": np.concatenate([a["L0_ffn_sW2"].reshape(-1, D), a["L0_ffn_rW2"].reshape(-1, D)], axis=0
                             ).reshape(TILES0, P, D).transpose(1, 0, 2),
        "w_gate": a["L1_ffn_gate_w"].reshape(TILES1 * P, D).T,
        "w_up": a["L1_ffn_up_w"].reshape(TILES1 * P, D).T,
        "w_down": a["L1_ffn_down_w"].transpose(0, 2, 1).reshape(TILES1, P, D).transpose(1, 0, 2),
    }
    host = {k: c(v) for k, v in host.items()}
    nc = _bacc.Bacc("TRN2", target_bir_lowering=False, num_devices=1)
    aps, arrays = {}, {}
    for name, v in host.items():
        arrays[f"in_{name}_dram"] = v
        aps[name] = nc.dram_tensor(f"in_{name}_dram", v.shape, mybir.dt.from_np(v.dtype),
                                   kind="ExternalInput").ap()
    out = nc.dram_tensor("out_0_dram", (NTOK, D), F32, kind="ExternalOutput").ap()
    build(nc, aps, out)
    r = _run(nc, [arrays], core_ids=[0])
    return r.results[0]["out_0_dram"].reshape(NSEQ, SEQ, D)
```
